# Optimizing a Trainium2 kernel written in Bass

```python
import numpy as np
import jax
import jax.numpy as jnp

def _softmax(x, axis=-1):
    return jax.nn.softmax(x, axis=axis)

def _gelu(x):
    return jax.nn.gelu(x, approximate=True)

def _silu(x):
    return jax.nn.silu(x)

def _sigmoid(x):
    return jax.nn.sigmoid(x)

def _layernorm(x, axis=-1, eps=1e-05):
    m = jnp.mean(x, axis=axis, keepdims=True)
    v = jnp.var(x, axis=axis, keepdims=True)
    return (x - m) / jnp.sqrt(v + eps)

def _scatter_add(tgt, idx, src, axis=0):
    return tgt.at[idx].add(src)

def _segment_sum(src, seg, n):
    return jax.ops.segment_sum(src, seg, n)
kernel_name = 'mk_flamingo_gated_d2_seqx_r4_3807a4'

def setup_inputs(seed: int=0):
    np.random.seed(seed)
    _w = jnp.asarray

    def _rec_inputs():
        import jax
        import jax.numpy as jnp
        _rk = jax.random.key(seed)
        x = -0.0002928 + 1 * jax.random.normal(jax.random.fold_in(_rk, 1), (16, 256, 256), jnp.float32)
        _lenS = 256 - jax.random.randint(jax.random.fold_in(_rk, 7), (16,), 0, max(1, 256 // 4) + 1, jnp.int32)
        _lenS2 = 256 - jax.random.randint(jax.random.fold_in(_rk, 8), (16,), 0, max(1, 256 // 4) + 1, jnp.int32)
        _ctx_1024P = jax.random.normal(jax.random.fold_in(_rk, 11), (16, 16, 256), jnp.float32)
        _ctx_1024c = jax.random.dirichlet(jax.random.fold_in(_rk, 511), 0.3 * jnp.ones((16,), jnp.float32), (16, 256))
        _ctx_1024t = jnp.einsum('bsk,bkd->bsd', _ctx_1024c, _ctx_1024P)
        _ctx_1024t = _ctx_1024t * jax.lax.rsqrt(jnp.mean(jnp.square(_ctx_1024t)) + 1e-12) * 0.953939
        ctx_1024 = -1.39393e-06 + 0.999914 * (_ctx_1024t + 0.3 * jax.random.normal(jax.random.fold_in(_rk, 611), (16, 256, 256), jnp.float32))
        _g = jax.random.normal(jax.random.fold_in(_rk, 9001), (2, 2), jnp.float32)
        _g = jnp.sign(_g) * jnp.maximum(jnp.abs(_g), 1.0) + (_g == 0) * 1.0
        g_xattn = _g[0]
        g_ffn = _g[1]
        return (x, ctx_1024, g_xattn, g_ffn)
    x, ctx_1024, g_xattn, g_ffn = _rec_inputs()

    def _L0_xattn_setup():
        import jax, jax.numpy as jnp
        import numpy as np
        EMBED_DIM = 256
        NUM_HEADS = 16
        PROJ_DIM = EMBED_DIM // NUM_HEADS

        def _split_heads(x, B):
            return x.reshape(B, -1, NUM_HEADS, PROJ_DIM).transpose(0, 2, 1, 3)
        key = jax.random.key(seed)
        ks = jax.random.split(key, 11)
        B, S, D = (2, 512, EMBED_DIM)
        scale = 1.0 / np.sqrt(D)
        inp = {'q': jax.random.normal(ks[0], (B, S, D), jnp.float32), 'k': jax.random.normal(ks[1], (B, S, D), jnp.float32), 'v': jax.random.normal(ks[2], (B, S, D), jnp.float32), 'Wq': jax.random.normal(ks[3], (D, D), jnp.float32) * scale, 'bq': jnp.zeros((D,), jnp.float32), 'Wk': jax.random.normal(ks[4], (D, D), jnp.float32) * scale, 'bk': jnp.zeros((D,), jnp.float32), 'Wv': jax.random.normal(ks[5], (D, D), jnp.float32) * scale, 'bv': jnp.zeros((D,), jnp.float32), 'Wo': jax.random.normal(ks[6], (D, D), jnp.float32) * scale, 'bo': jnp.zeros((D,), jnp.float32), 'use_causal_mask': 1}
        return inp
    _L0_xattn_all = _L0_xattn_setup()
    _L0_xattn_in = {k: v for k, v in _L0_xattn_all.items() if k in ('Wq', 'bq', 'Wk', 'bk', 'Wv', 'bv', 'Wo', 'bo')}
    del _L0_xattn_all

    def _L0_ffn_setup():
        import jax, jax.numpy as jnp
        import numpy as np
        B, S, H, F, E, K = (4, 512, 256, 896, 8, 2)
        CAP_FACTOR = 1.25

        def _moe_forward(hidden_states, gate_w, w1, w2, w3):
            b, s, h = hidden_states.shape
            dtype = hidden_states.dtype
            x = hidden_states.reshape(-1, h)
            router_logits = x @ gate_w.T
            expert_weights = jax.nn.softmax(router_logits.astype(jnp.float32), axis=1)
            _, selected_experts = jax.lax.top_k(expert_weights, K)
            top_k_idx = selected_experts.reshape(b, s, K)
            probs = expert_weights.reshape(b, s, E)
            capacity = int(s * K / E * CAP_FACTOR)
            expert_mask = jax.nn.one_hot(top_k_idx, E, dtype=jnp.int32)
            mask_fused = expert_mask.reshape(b, s * K, E)
            count_fused = jnp.cumsum(mask_fused, axis=1)
            count = count_fused.reshape(b, s, K, E)
            trunc_mask = expert_mask * (count <= capacity).astype(jnp.int32)
            combined_mask = trunc_mask.sum(axis=2)
            masked_probs = probs * combined_mask
            pos_fused = mask_fused * count_fused
            pos = pos_fused.reshape(b, s, K, E)
            combined_pos = pos.sum(axis=2) * combined_mask
            pos_in_cap = jax.nn.one_hot(combined_pos, capacity + 1, dtype=jnp.int32)
            combine_mask = masked_probs[..., None] * pos_in_cap
            combine_mask = combine_mask[..., 1:].astype(dtype)
            dispatch_mask = (combine_mask != 0).astype(dtype)
            dispatch = jnp.einsum('bsm,bsec->ebcm', hidden_states, dispatch_mask)
            h1 = jnp.einsum('ebcm,emh->ebch', dispatch, w1)
            h3 = jnp.einsum('ebcm,emh->ebch', dispatch, w3)
            expert_out = jnp.einsum('ebch,ehm->ebcm', jax.nn.silu(h1) * h3, w2)
            final = jnp.einsum('ebcm,bsec->bsm', expert_out, combine_mask)
            return final
        key = jax.random.key(seed)
        k1, k2, k3, k4, k5 = jax.random.split(key, 5)
        s_h = 1.0 / np.sqrt(H)
        s_f = 1.0 / np.sqrt(F)
        return {'hidden_states': jax.random.normal(k1, (B, S, H), dtype=jnp.float32), 'gate_w': jax.random.normal(k2, (E, H), dtype=jnp.float32) * s_h, 'w1': jax.random.normal(k3, (E, H, F), dtype=jnp.float32) * s_h, 'w2': jax.random.normal(k4, (E, F, H), dtype=jnp.float32) * s_f, 'w3': jax.random.normal(k5, (E, H, F), dtype=jnp.float32) * s_h}
    _L0_ffn_all = _L0_ffn_setup()
    _L0_ffn_in = {k: v for k, v in _L0_ffn_all.items() if k in ('gate_w', 'w1', 'w2', 'w3')}
    del _L0_ffn_all

    def _L1_xattn_setup():
        import jax, jax.numpy as jnp
        import numpy as np
        EMBED_DIM = 256
        NUM_HEADS = 16
        HEAD_DIM = EMBED_DIM // NUM_HEADS
        WINDOW = 128
        B, S_Q, S_K = (2, 512, 512)

        def apply_rope(x):
            Dh = x.shape[-1]
            half = Dh // 2
            pos = jnp.arange(x.shape[2], dtype=jnp.float32)
            inv_freq = 1.0 / 10000.0 ** (jnp.arange(0, half, dtype=jnp.float32) / half)
            ang = pos[:, None] * inv_freq[None, :]
            cos = jnp.cos(ang)[None, None, :, :].astype(x.dtype)
            sin = jnp.sin(ang)[None, None, :, :].astype(x.dtype)
            x1, x2 = (x[..., :half], x[..., half:])
            return jnp.concatenate([x1 * cos - x2 * sin, x1 * sin + x2 * cos], axis=-1)
        key = jax.random.key(seed)
        ks = jax.random.split(key, 11)
        scale = 1.0 / np.sqrt(EMBED_DIM)
        inp = {'query': jax.random.normal(ks[0], (B, S_Q, EMBED_DIM), jnp.float32), 'key': jax.random.normal(ks[1], (B, S_K, EMBED_DIM), jnp.float32), 'value': jax.random.normal(ks[2], (B, S_K, EMBED_DIM), jnp.float32), 'Wq': jax.random.normal(ks[3], (EMBED_DIM, EMBED_DIM), jnp.float32) * scale, 'bq': jnp.zeros((EMBED_DIM,), jnp.float32), 'Wk': jax.random.normal(ks[4], (EMBED_DIM, EMBED_DIM), jnp.float32) * scale, 'bk': jnp.zeros((EMBED_DIM,), jnp.float32), 'Wv': jax.random.normal(ks[5], (EMBED_DIM, EMBED_DIM), jnp.float32) * scale, 'bv': jnp.zeros((EMBED_DIM,), jnp.float32), 'Wo': jax.random.normal(ks[6], (EMBED_DIM, EMBED_DIM), jnp.float32) * scale, 'bo': jnp.zeros((EMBED_DIM,), jnp.float32)}
        return inp
    _L1_xattn_all = _L1_xattn_setup()
    _L1_xattn_in = {k: v for k, v in _L1_xattn_all.items() if k in ('Wq', 'bq', 'Wk', 'bk', 'Wv', 'bv', 'Wo', 'bo')}
    del _L1_xattn_all

    def _L1_ffn_setup():
        import jax, jax.numpy as jnp
        import numpy as np
        B, S, H = (1, 512, 256)
        E, K = (16, 4)
        G, TG = (4, 2)
        I_MOE = 128
        N_SH = 2
        SCALE = 2.5

        def _mlp(x, gw, uw, dw):
            return jax.nn.silu(x @ gw.T) * (x @ uw.T) @ dw.T

        def _route(x2d, router_weight, e_bias):
            T = x2d.shape[0]
            scores = jax.nn.sigmoid(x2d @ router_weight.T)
            sc = scores + e_bias[None, :]
            group_scores = jnp.sum(jax.lax.top_k(sc.reshape(T, G, E // G), 2)[0], axis=-1)
            _, gidx = jax.lax.top_k(group_scores, TG)
            gmask = jnp.zeros((T, G), sc.dtype).at[jnp.arange(T)[:, None], gidx].set(1.0)
            smask = jnp.repeat(gmask, E // G, axis=1)
            masked = jnp.where(smask > 0, sc, 0.0)
            _, tidx = jax.lax.top_k(masked, K)
            tw = jnp.take_along_axis(scores, tidx, axis=1)
            tw = tw / (jnp.sum(tw, axis=-1, keepdims=True) + 1e-20)
            tw = tw * SCALE
            return (tidx, tw)

        def _moe_forward(hidden_states, router_weight, e_bias, gate_w, up_w, down_w, sh_gate_w, sh_up_w, sh_down_w):
            orig_shape = hidden_states.shape
            x = hidden_states.reshape(-1, H)
            T = x.shape[0]
            tidx, tw = _route(x, router_weight, e_bias)
            g = jnp.einsum('th,eih->tei', x, gate_w)
            u = jnp.einsum('th,eih->tei', x, up_w)
            h = jax.nn.silu(g) * u
            yo = jnp.einsum('tei,ehi->teh', h, down_w)
            combine = jnp.zeros((T, E), tw.dtype).at[jnp.arange(T)[:, None], tidx].add(tw)
            routed = jnp.einsum('te,teh->th', combine, yo)
            shared = _mlp(hidden_states.reshape(-1, H), sh_gate_w, sh_up_w, sh_down_w)
            return (routed + shared).reshape(orig_shape)
        key = jax.random.key(seed)
        ks = jax.random.split(key, 9)
        s = 0.02
        return {'hidden_states': jax.random.normal(ks[0], (B, S, H), jnp.float32), 'router_weight': jax.random.normal(ks[1], (E, H), jnp.float32) * s, 'e_bias': jnp.zeros((E,), jnp.float32), 'gate_w': jax.random.normal(ks[2], (E, I_MOE, H), jnp.float32) * s, 'up_w': jax.random.normal(ks[3], (E, I_MOE, H), jnp.float32) * s, 'down_w': jax.random.normal(ks[4], (E, H, I_MOE), jnp.float32) * s, 'sh_gate_w': jax.random.normal(ks[5], (N_SH * I_MOE, H), jnp.float32) * s, 'sh_up_w': jax.random.normal(ks[6], (N_SH * I_MOE, H), jnp.float32) * s, 'sh_down_w': jax.random.normal(ks[7], (H, N_SH * I_MOE), jnp.float32) * s}
    _L1_ffn_all = _L1_ffn_setup()
    _L1_ffn_in = {k: v for k, v in _L1_ffn_all.items() if k in ('router_weight', 'e_bias', 'gate_w', 'up_w', 'down_w', 'sh_gate_w', 'sh_up_w', 'sh_down_w')}
    del _L1_ffn_all
    return {'x': x, 'ctx_1024': ctx_1024, 'g_xattn': g_xattn, 'g_ffn': g_ffn, 'L0_xattn_Wq': _L0_xattn_in['Wq'], 'L0_xattn_bq': _L0_xattn_in['bq'], 'L0_xattn_Wk': _L0_xattn_in['Wk'], 'L0_xattn_bk': _L0_xattn_in['bk'], 'L0_xattn_Wv': _L0_xattn_in['Wv'], 'L0_xattn_bv': _L0_xattn_in['bv'], 'L0_xattn_Wo': _L0_xattn_in['Wo'], 'L0_xattn_bo': _L0_xattn_in['bo'], 'L0_ffn_gate_w': _L0_ffn_in['gate_w'], 'L0_ffn_w1': _L0_ffn_in['w1'], 'L0_ffn_w2': _L0_ffn_in['w2'], 'L0_ffn_w3': _L0_ffn_in['w3'], 'L1_xattn_Wq': _L1_xattn_in['Wq'], 'L1_xattn_bq': _L1_xattn_in['bq'], 'L1_xattn_Wk': _L1_xattn_in['Wk'], 'L1_xattn_bk': _L1_xattn_in['bk'], 'L1_xattn_Wv': _L1_xattn_in['Wv'], 'L1_xattn_bv': _L1_xattn_in['bv'], 'L1_xattn_Wo': _L1_xattn_in['Wo'], 'L1_xattn_bo': _L1_xattn_in['bo'], 'L1_ffn_router_weight': _L1_ffn_in['router_weight'], 'L1_ffn_e_bias': _L1_ffn_in['e_bias'], 'L1_ffn_gate_w': _L1_ffn_in['gate_w'], 'L1_ffn_up_w': _L1_ffn_in['up_w'], 'L1_ffn_down_w': _L1_ffn_in['down_w'], 'L1_ffn_sh_gate_w': _L1_ffn_in['sh_gate_w'], 'L1_ffn_sh_up_w': _L1_ffn_in['sh_up_w'], 'L1_ffn_sh_down_w': _L1_ffn_in['sh_down_w']}

def reference(x, ctx_1024, g_xattn, g_ffn, L0_xattn_Wq, L0_xattn_bq, L0_xattn_Wk, L0_xattn_bk, L0_xattn_Wv, L0_xattn_bv, L0_xattn_Wo, L0_xattn_bo, L0_ffn_gate_w, L0_ffn_w1, L0_ffn_w2, L0_ffn_w3, L1_xattn_Wq, L1_xattn_bq, L1_xattn_Wk, L1_xattn_bk, L1_xattn_Wv, L1_xattn_bv, L1_xattn_Wo, L1_xattn_bo, L1_ffn_router_weight, L1_ffn_e_bias, L1_ffn_gate_w, L1_ffn_up_w, L1_ffn_down_w, L1_ffn_sh_gate_w, L1_ffn_sh_up_w, L1_ffn_sh_down_w):
    import jax
    import jax.numpy as jnp

    def _L0_xattn_ref(q, k, v, Wq, bq, Wk, bk, Wv, bv, Wo, bo, use_causal_mask):
        import jax, jax.numpy as jnp
        import numpy as np
        EMBED_DIM = 256
        NUM_HEADS = 16
        PROJ_DIM = EMBED_DIM // NUM_HEADS

        def _split_heads(x, B):
            return x.reshape(B, -1, NUM_HEADS, PROJ_DIM).transpose(0, 2, 1, 3)
        B, S, D = q.shape
        qh = _split_heads(q @ Wq + bq, B)
        kh = _split_heads(k @ Wk + bk, B)
        vh = _split_heads(v @ Wv + bv, B)
        logits = jnp.einsum('bhqd,bhkd->bhqk', qh, kh) / jnp.sqrt(jnp.asarray(PROJ_DIM, jnp.float32))
        if use_causal_mask:
            tril = jnp.tril(jnp.ones((S, S), dtype=logits.dtype))
            logits = logits + jnp.log(tril * 1e-09 + 1e-09)
        attn = jax.nn.softmax(logits, axis=-1)
        out = jnp.einsum('bhqk,bhkd->bhqd', attn, vh)
        out = out.transpose(0, 2, 1, 3).reshape(B, S, D)
        return out @ Wo + bo

    def _L0_ffn_ref(hidden_states, gate_w, w1, w2, w3):
        import jax, jax.numpy as jnp
        import numpy as np
        B, S, H, F, E, K = (4, 512, 256, 896, 8, 2)
        CAP_FACTOR = 1.25

        def _moe_forward(hidden_states, gate_w, w1, w2, w3):
            b, s, h = hidden_states.shape
            dtype = hidden_states.dtype
            x = hidden_states.reshape(-1, h)
            router_logits = x @ gate_w.T
            expert_weights = jax.nn.softmax(router_logits.astype(jnp.float32), axis=1)
            _, selected_experts = jax.lax.top_k(expert_weights, K)
            top_k_idx = selected_experts.reshape(b, s, K)
            probs = expert_weights.reshape(b, s, E)
            capacity = int(s * K / E * CAP_FACTOR)
            expert_mask = jax.nn.one_hot(top_k_idx, E, dtype=jnp.int32)
            mask_fused = expert_mask.reshape(b, s * K, E)
            count_fused = jnp.cumsum(mask_fused, axis=1)
            count = count_fused.reshape(b, s, K, E)
            trunc_mask = expert_mask * (count <= capacity).astype(jnp.int32)
            combined_mask = trunc_mask.sum(axis=2)
            masked_probs = probs * combined_mask
            pos_fused = mask_fused * count_fused
            pos = pos_fused.reshape(b, s, K, E)
            combined_pos = pos.sum(axis=2) * combined_mask
            pos_in_cap = jax.nn.one_hot(combined_pos, capacity + 1, dtype=jnp.int32)
            combine_mask = masked_probs[..., None] * pos_in_cap
            combine_mask = combine_mask[..., 1:].astype(dtype)
            dispatch_mask = (combine_mask != 0).astype(dtype)
            dispatch = jnp.einsum('bsm,bsec->ebcm', hidden_states, dispatch_mask)
            h1 = jnp.einsum('ebcm,emh->ebch', dispatch, w1)
            h3 = jnp.einsum('ebcm,emh->ebch', dispatch, w3)
            expert_out = jnp.einsum('ebch,ehm->ebcm', jax.nn.silu(h1) * h3, w2)
            final = jnp.einsum('ebcm,bsec->bsm', expert_out, combine_mask)
            return final
        return _moe_forward(hidden_states, gate_w, w1, w2, w3)

    def _L1_xattn_ref(query, key, value, Wq, bq, Wk, bk, Wv, bv, Wo, bo):
        import jax, jax.numpy as jnp
        import numpy as np
        EMBED_DIM = 256
        NUM_HEADS = 16
        HEAD_DIM = EMBED_DIM // NUM_HEADS
        WINDOW = 128
        B, S_Q, S_K = (2, 512, 512)

        def apply_rope(x):
            Dh = x.shape[-1]
            half = Dh // 2
            pos = jnp.arange(x.shape[2], dtype=jnp.float32)
            inv_freq = 1.0 / 10000.0 ** (jnp.arange(0, half, dtype=jnp.float32) / half)
            ang = pos[:, None] * inv_freq[None, :]
            cos = jnp.cos(ang)[None, None, :, :].astype(x.dtype)
            sin = jnp.sin(ang)[None, None, :, :].astype(x.dtype)
            x1, x2 = (x[..., :half], x[..., half:])
            return jnp.concatenate([x1 * cos - x2 * sin, x1 * sin + x2 * cos], axis=-1)
        Bq, Sq, D = query.shape
        Sk = key.shape[1]
        H, Dh = (NUM_HEADS, HEAD_DIM)

        def proj(x, W, b):
            return (x @ W.T + b).reshape(x.shape[0], x.shape[1], H, Dh).transpose(0, 2, 1, 3)
        q = apply_rope(proj(query, Wq, bq))
        k = apply_rope(proj(key, Wk, bk))
        v = proj(value, Wv, bv)
        q = q * Dh ** (-0.5)
        scores = jnp.einsum('bhqd,bhkd->bhqk', q, k)
        q_idx = jnp.arange(Sq)[:, None]
        kv_idx = jnp.arange(Sk)[None, :]
        rel = kv_idx - q_idx
        mask = (rel > 0) | (rel < -WINDOW)
        mask4 = mask[None, None, :, :]
        neg = jnp.finfo(scores.dtype).min
        scores = jnp.where(mask4, neg, scores)
        probs = jax.nn.softmax(scores, axis=-1)
        all_masked = jnp.all(mask4, axis=-1, keepdims=True)
        probs = jnp.where(all_masked, jnp.zeros((), probs.dtype), probs)
        out = jnp.einsum('bhqk,bhkd->bhqd', probs, v)
        out = out.transpose(0, 2, 1, 3).reshape(Bq, Sq, D)
        return out @ Wo.T + bo

    def _L1_ffn_ref(hidden_states, router_weight, e_bias, gate_w, up_w, down_w, sh_gate_w, sh_up_w, sh_down_w):
        import jax, jax.numpy as jnp
        import numpy as np
        B, S, H = (1, 512, 256)
        E, K = (16, 4)
        G, TG = (4, 2)
        I_MOE = 128
        N_SH = 2
        SCALE = 2.5

        def _mlp(x, gw, uw, dw):
            return jax.nn.silu(x @ gw.T) * (x @ uw.T) @ dw.T

        def _route(x2d, router_weight, e_bias):
            T = x2d.shape[0]
            scores = jax.nn.sigmoid(x2d @ router_weight.T)
            sc = scores + e_bias[None, :]
            group_scores = jnp.sum(jax.lax.top_k(sc.reshape(T, G, E // G), 2)[0], axis=-1)
            _, gidx = jax.lax.top_k(group_scores, TG)
            gmask = jnp.zeros((T, G), sc.dtype).at[jnp.arange(T)[:, None], gidx].set(1.0)
            smask = jnp.repeat(gmask, E // G, axis=1)
            masked = jnp.where(smask > 0, sc, 0.0)
            _, tidx = jax.lax.top_k(masked, K)
            tw = jnp.take_along_axis(scores, tidx, axis=1)
            tw = tw / (jnp.sum(tw, axis=-1, keepdims=True) + 1e-20)
            tw = tw * SCALE
            return (tidx, tw)

        def _moe_forward(hidden_states, router_weight, e_bias, gate_w, up_w, down_w, sh_gate_w, sh_up_w, sh_down_w):
            orig_shape = hidden_states.shape
            x = hidden_states.reshape(-1, H)
            T = x.shape[0]
            tidx, tw = _route(x, router_weight, e_bias)
            g = jnp.einsum('th,eih->tei', x, gate_w)
            u = jnp.einsum('th,eih->tei', x, up_w)
            h = jax.nn.silu(g) * u
            yo = jnp.einsum('tei,ehi->teh', h, down_w)
            combine = jnp.zeros((T, E), tw.dtype).at[jnp.arange(T)[:, None], tidx].add(tw)
            routed = jnp.einsum('te,teh->th', combine, yo)
            shared = _mlp(hidden_states.reshape(-1, H), sh_gate_w, sh_up_w, sh_down_w)
            return (routed + shared).reshape(orig_shape)
        return _moe_forward(hidden_states, router_weight, e_bias, gate_w, up_w, down_w, sh_gate_w, sh_up_w, sh_down_w)
    x = x + jnp.tanh(g_xattn[0]) * _L0_xattn_ref(_layernorm(x, axis=-1), ctx_1024, ctx_1024, L0_xattn_Wq, L0_xattn_bq, L0_xattn_Wk, L0_xattn_bk, L0_xattn_Wv, L0_xattn_bv, L0_xattn_Wo, L0_xattn_bo, 1)
    x = x + jnp.tanh(g_ffn[0]) * _L0_ffn_ref(_layernorm(x, axis=-1), L0_ffn_gate_w, L0_ffn_w1, L0_ffn_w2, L0_ffn_w3)
    x = x + jnp.tanh(g_xattn[1]) * _L1_xattn_ref(_layernorm(x, axis=-1), ctx_1024, ctx_1024, L1_xattn_Wq, L1_xattn_bq, L1_xattn_Wk, L1_xattn_bk, L1_xattn_Wv, L1_xattn_bv, L1_xattn_Wo, L1_xattn_bo)
    x = x + jnp.tanh(g_ffn[1]) * _L1_ffn_ref(_layernorm(x, axis=-1), L1_ffn_router_weight, L1_ffn_e_bias, L1_ffn_gate_w, L1_ffn_up_w, L1_ffn_down_w, L1_ffn_sh_gate_w, L1_ffn_sh_up_w, L1_ffn_sh_down_w)
    return x

_drawn_inputs = setup_inputs


def setup_inputs(seed=0):
    import zlib

    import numpy as np

    out = dict(_drawn_inputs(seed))
    spreads = {'g_ffn': (-1.0, 0.6),
     'L0_xattn_bq': (0.0, 0.341),
     'L0_xattn_bk': (0.0, 0.8),
     'L0_xattn_bv': (0.0, 0.1),
     'L0_xattn_bo': (0.0, 0.1),
     'L1_xattn_bq': (0.0, 0.465),
     'L1_xattn_bk': (0.0, 0.8),
     'L1_xattn_bv': (0.0, 0.1),
     'L1_xattn_bo': (0.0, 0.1),
     'L1_ffn_e_bias': (0.0, 0.8)}
    factors = {'L1_ffn_router_weight': 7.249,
     'L1_ffn_gate_w': 5.701,
     'L1_ffn_up_w': 5.588,
     'L1_ffn_down_w': 5.611,
     'L1_ffn_sh_gate_w': 4.752,
     'L1_ffn_sh_up_w': 4.822,
     'L1_ffn_sh_down_w': 4.698}
    for name, (base, spread) in spreads.items():
        noise = np.random.default_rng([zlib.crc32(name.encode()), seed]).standard_normal(out[name].shape)
        drawn = base * np.exp(spread * noise) if base else spread * noise
        out[name] = jnp.asarray(drawn.astype(out[name].dtype))
    for name, factor in factors.items():
        out[name] = (out[name] * factor).astype(out[name].dtype)
    return out
```

```python
import math
from contextlib import ExitStack

import numpy as np

import concourse.bass as bass
from concourse import mybir

F32 = mybir.dt.float32
F16 = mybir.dt.float16
U32 = mybir.dt.uint32
ACT = mybir.ActivationFunctionType
ALU = mybir.AluOpType
AX = mybir.AxisListType

P = 128
D = 256
KT = D // P
B, S = 16, 256
TT = S // P
NT = B * TT
H, DH = 16, 16
SLOT = 32
GH = P // SLOT
G = H // GH
EPS = 1e-5


def flamingo_kernel(nc, a, out):

    def sb(name, shape, dt):
        return nc.alloc_sbuf_tensor(name, shape, dt)

    sem = nc.alloc_semaphore
    waited = sem("waited")

    def hold(eng, counter, value):
        eng.wait_ge(counter, value)
        eng.sem_inc(waited, 1)

    x = sb("x_res", [P, NT, D], F32)
    mv = sb("mean_var", [P, NT, 2], F32)
    rstd = sb("rstd", [P, NT], F32)
    nwt = sb("newton", [P, NT], F32)
    ident32 = sb("ident32", [P, P], F32)
    ident16 = sb("ident16", [P, P], F16)
    gate = sb("gate", [P, 4], F32)
    graw = sb("gate_raw", [P, 4], F32)
    stats = sb("bn_stats", [P, TT, 6], F32)
    agg = sb("bn_aggregate", [P, TT, 2], F32)
    psum = nc.alloc_psum_tensor("ps", [P, 8, 512], F32)

    x_dram = a["x"].rearrange("b (t p) d -> p (b t) d", p=P)
    ctx_dram = a["ctx"].rearrange("b (t p) d -> b p t d", p=P)
    out_dram = out.rearrange("b (t p) d -> p (b t) d", p=P)

    def token_stats(dve, i, chain):
        for t in range(TT):
            nc.vector.bn_stats(stats[:, t, :], x[:, bass.ds(i * TT + t, 1), :].rearrange("p a d -> p (a d)"))\
              .then_inc(chain, 1)
        hold(dve, chain, (i + 1) * 5 + 2)
        for t in range(TT):
            nc.vector.bn_aggr(agg[:, t, :], stats[:, t, :]).then_inc(chain, 1)
        hold(dve, chain, (i + 1) * 5 + 4)
        nc.vector.tensor_copy(mv[:, bass.ds(i * TT, TT), :], agg[:, :, :]).then_inc(chain, 1)

    x_loaded = sem("x_loaded")
    consts_loaded = sem("consts_loaded")
    setup_chain = sem("setup_chain")
    with nc.Block() as block:

        @block.sync
        def _(sp):
            sp.dma_start(graw[:, :], a["gates"]).then_inc(consts_loaded, 16)
            sp.dma_start(ident32[:, :], a["ident"]).then_inc(consts_loaded, 16)
            for c in range(4):
                sp.dma_start(x[:, c * 8:(c + 1) * 8, :], x_dram[:, c * 8:(c + 1) * 8, :]).then_inc(x_loaded, 16)

        @block.scalar
        def _(act):
            act.wait_ge(consts_loaded, 32)
            nc.scalar.activation(gate[:, :], graw[:, :], ACT.Tanh)
            nc.scalar.activation(ident16[:, :], ident32[:, :], ACT.Copy)

        @block.vector
        def _(dve):
            dve.wait_ge(x_loaded, 64)
            dve.sem_inc(setup_chain, 5)
            with dve.Fori(0, B) as i:
                token_stats(dve, i, setup_chain)

    def layernorm_scale(tag):
        ve = sem(f"{tag}_var_eps")
        sq = sem(f"{tag}_sqrt")
        ch = sem(f"{tag}_rstd_chain")
        with nc.Block() as block:

            @block.vector
            def _(dve):
                nc.vector.tensor_scalar(mv[:, :, 1], mv[:, :, 1], EPS, None, ALU.add).then_inc(ve, 1)
                dve.wait_ge(sq, 1)
                n = 0
                for step in (
                    lambda: nc.vector.reciprocal(rstd[:, :], rstd[:, :]),
                    lambda: nc.vector.tensor_tensor(nwt[:, :], rstd[:, :], rstd[:, :], ALU.mult),
                    lambda: nc.vector.tensor_tensor(nwt[:, :], nwt[:, :], mv[:, :, 1], ALU.mult),
                    lambda: nc.vector.tensor_scalar(nwt[:, :], nwt[:, :], -0.5, 1.5, ALU.mult, ALU.add),
                    lambda: nc.vector.tensor_tensor(rstd[:, :], rstd[:, :], nwt[:, :], ALU.mult),
                ):
                    step().then_inc(ch, 1)
                    n += 1
                    dve.wait_ge(ch, n)

            @block.scalar
            def _(act):
                act.wait_ge(ve, 1)
                nc.scalar.activation(rstd[:, :], mv[:, :, 1], ACT.Sqrt).then_inc(sq, 1)

    def attention_buffers(sb):
      return dict(
        xin=sb("ctx_in", [P, TT, D], F32),
        xn=sb("xn", [P, TT, D], F32),
        xT=sb("xT", [P, 2, KT, S], F16),
        cT=sb("cT", [P, 2, KT, S], F16),
        wq=sb("wq", [P, 2, KT, G, P], F16),
        wk=sb("wk", [P, 2, KT, G, P], F16),
        wv=sb("wv", [P, 2, KT, D], F16),
        wo=sb("wo", [P, 2, KT, D], F16),
        wld=sb("w_load", [P, KT, G * P], F32),
        bq=sb("bq", [P, G], F32),
        bk=sb("bk", [P, G], F32),
        bv=sb("bv", [P, KT], F32),
        bo32=sb("bo32", [1, D], F32),
        bo=sb("bo", [1, 2, D], F16),
        ones=sb("ones_row", [1, P], F16),
        qf=sb("qf", [P, G, S], F32),
        kf=sb("kf", [P, G, S], F32),
        rot=sb("rotated", [P, G, S], F32),
        qh=sb("qh", [P, G, S], F16),
        q1=sb("q1", [P, G, S], F16),
        q2=sb("q2", [P, G, S], F16),
        kh=sb("kh", [P, G, S], F16),
        kl=sb("kl", [P, G, S], F16),
        k1=sb("k1", [P, GH, G, S], F16),
        k2=sb("k2", [P, GH, G, S], F16),
        v=sb("v_ext", [P, TT, H, SLOT], F32),
        m=sb("neg_max", [P, TT, G, P], F32),
        pr=sb("probs", [P, 2, TT, GH, S], F32),
        o=sb("o_slots", [P, G, S], F32),
        on=sb("o_norm", [P, TT, D], F32),
        rd=sb("recip_den", [P, TT, H], F32),
        oT=sb("oT", [P, 2, KT, S], F16),
        hi_rows=sb("hi_rows", [P, 2], F32),
        cos=sb("rope_cos", [P, S], F32),
        sin=sb("rope_sin", [P, S], F32),
        masks=sb("masks16", [P, 4, P], F16),
    )

    def attention(L):
        stack = ExitStack()
        w = attention_buffers(lambda name, shape, dt: stack.enter_context(
            nc.sbuf_tensor(f"a{L}_{name}", shape, dt)))
        causal_band = L == 1
        n = f"A{L}_"
        def pairs(qt):
            return [qt - 1, qt] if causal_band and qt else [qt] if causal_band else list(range(TT))

        wl = sem(n + "weights_loaded")
        ws = sem(n + "weights_split")
        hi_done = sem(n + "weight_hi")
        jobs = [("wq", G * P), ("wk", G * P), ("wv", D), ("wo", D)]
        flat = {k: w[k][:, :, :, :, :].rearrange("p s k g m -> p s k (g m)") for k in ("wq", "wk")}
        flat |= {k: w[k][:, :, :, :] for k in ("wv", "wo")}
        small = [("bq", w["bq"][:, :]), ("bk", w["bk"][:, :]), ("bv", w["bv"][:, :]), ("bo", w["bo32"][0:1, :])]
        with nc.Block() as block:

            @block.sync
            def _(sp):
                for i, (k, dst) in enumerate(small):
                    sp.dma_start(dst, a[f"L{L}_{k}"]).then_inc(wl, 16)
                sp.dma_start(w["masks"][:, :, :], a[f"L{L}_masks"]).then_inc(wl, 16)
                sp.dma_start(w["m"][:, :, :, :], a[f"L{L}_mrows"]).then_inc(wl, 16)
                sp.dma_start(w["hi_rows"][:, :], a["hi_rows"]).then_inc(wl, 16)
                sp.dma_start(w["k2"][:, :, :, :], a[f"L{L}_k2rows"]).then_inc(wl, 16)
                if causal_band:
                    sp.dma_start(w["cos"][:, :], a["cos"]).then_inc(wl, 16)
                    sp.dma_start(w["sin"][:, :], a["sin"]).then_inc(wl, 16)
                base = 16 * (len(small) + 4 + 2 * causal_band)
                for i, (k, width) in enumerate(jobs):
                    sp.wait_ge(wl, base + 16 * i)
                    if i:
                        sp.wait_ge(ws, i)
                    sp.dma_start(w["wld"][:, :, 0:width], a[f"L{L}_{k}"]).then_inc(wl, 16)

            @block.scalar
            def _(act):
                base = 16 * (len(small) + 4 + 2 * causal_band)
                for i, (k, width) in enumerate(jobs):
                    act.wait_ge(wl, base + 16 * (i + 1))
                    nc.scalar.activation(flat[k][:, 0, :, :], w["wld"][:, :, 0:width], ACT.Copy).then_inc(hi_done, 1)
                nc.scalar.activation(w["bo"][0:1, 0, :], w["bo32"][0:1, :], ACT.Copy).then_inc(hi_done, 1)

            @block.gpsimd
            def _(pool):
                pool.memset(w["k1"][:, :, :, :], 0.0)
                pool.memset(w["v"][:, :, :, DH:SLOT], 1.0)
                pool.memset(w["ones"][0:1, :], 1.0)

            @block.vector
            def _(dve):
                for i, (k, width) in enumerate(jobs):
                    dve.wait_ge(hi_done, i + 1)
                    nc.vector.tensor_tensor(flat[k][:, 1, :, :], w["wld"][:, :, 0:width], flat[k][:, 0, :, :],
                                            ALU.subtract).then_inc(ws, 1)
                dve.wait_ge(hi_done, len(jobs) + 1)
                nc.vector.tensor_tensor(w["bo"][0:1, 1, :], w["bo32"][0:1, :], w["bo"][0:1, 0, :], ALU.subtract)

        ctx_loaded = sem(n + "ctx_loaded")
        xn_ready = sem(n + "xn_ready")
        tr_done = sem(n + "transposed")
        tr_hi = sem(n + "transposed_hi")
        tr_lo = sem(n + "transposed_lo")
        proj_done = sem(n + "projected")
        proj_out = sem(n + "projection_taken")
        f_ready = sem(n + "qk_rotated")
        rope = sem(n + "rope_steps")
        qk_hi = sem(n + "qk_hi")
        q1_ready = sem(n + "q1_ready")
        kl_ready = sem(n + "k_lo_ready")
        k1_ready = sem(n + "k1_placed")
        k2_ready = sem(n + "k2_placed")
        mx_scores = sem(n + "max_scores")
        mx_taken = sem(n + "maxima_taken")
        m_done = sem(n + "maxima_transposed")
        q2_ready = sem(n + "q2_ready")
        sc_done = sem(n + "scores_done")
        ex_done = sem(n + "exp_done")
        av_done = sem(n + "av_done")
        o_out = sem(n + "o_taken")
        oT_done = sem(n + "o_natural")
        rd_ready = sem(n + "recip_ready")
        on_ready = sem(n + "o_normalised")
        on_T = sem(n + "o_norm_transposed")
        oh_ready = sem(n + "oT_hi")
        ol_ready = sem(n + "oT_lo")
        y_done = sem(n + "y_done")
        x_new = sem(n + "x_updated")
        st_chain = sem(n + "stats_chain")
        credits = [
            (ctx_loaded, 16),
            (xn_ready, 2),
            (tr_done, 2),
            (tr_hi, 2),
            (tr_lo, 2),
            (proj_done, 5),
            (proj_out, 5),
            (f_ready, 2),
            (rope, 6),
            (qk_hi, 2),
            (q1_ready, 1),
            (kl_ready, 1),
            (k1_ready, 16 * GH),
            (k2_ready, 16 * GH),
            (mx_scores, 8),
            (mx_taken, 8),
            (m_done, 2),
            (q2_ready, 2),
            (sc_done, 8),
            (ex_done, 8),
            (av_done, 4),
            (o_out, 4),
            (oT_done, 2),
            (rd_ready, 2),
            (on_ready, 2),
            (on_T, 1),
            (oh_ready, 1),
            (ol_ready, 1),
            (y_done, 1),
            (x_new, 1),
            (st_chain, 5),
        ]
        with nc.Block() as block:

            @block.sync
            def _(sp):
                for counter, number in credits:
                    sp.sem_inc(counter, number)

        SC = [psum[:, 0:2, :].rearrange("p b n -> p (b n)"), psum[:, 2:4, :].rearrange("p b n -> p (b n)")]
        with nc.Block() as block:

            @block.sync
            def _(sp):
                with sp.Fori(0, B) as i:
                    hold(sp, tr_done, (i + 1) * 2)
                    sp.dma_start(w["xin"][:, :, :], ctx_dram[i, :, :, :]).then_inc(ctx_loaded, 16)
                    hold(sp, qk_hi, (i + 1) * 2 + 2)
                    sp.wait_ge(sc_done, (i + 1) * 8)
                    for j in range(GH):
                        sp.dma_start(w["k1"][j * SLOT:(j + 1) * SLOT, j, :, :],
                                     w["kh"][j * SLOT:(j + 1) * SLOT, :, :]).then_inc(k1_ready, 16)
                    sp.wait_ge(kl_ready, i + 2)
                    for j in range(GH):
                        sp.dma_start(w["k2"][j * SLOT:j * SLOT + DH, j, :, :],
                                     w["kl"][j * SLOT:j * SLOT + DH, :, :]).then_inc(k2_ready, 16)

            @block.tensor
            def _(pe):
                mm = nc.tensor.matmul
                with pe.Fori(0, B) as i:
                    pe.wait_ge(xn_ready, (i + 1) * 2 + 2)
                    pe.wait_ge(x_new, i + 1)
                    for c in range(KT):
                        for t in range(TT):
                            last = nc.tensor.transpose(psum[:, 7, c * S + t * P:c * S + (t + 1) * P],
                                                       w["xn"][:, t, c * P:(c + 1) * P], ident32[:, :])
                    last.then_inc(tr_done, 1)
                    pe.wait_ge(ctx_loaded, (i + 1) * 16 + 16)
                    pe.wait_ge(ol_ready, i + 1)
                    for c in range(KT):
                        for t in range(TT):
                            last = nc.tensor.transpose(psum[:, 6, c * S + t * P:c * S + (t + 1) * P],
                                                       w["xin"][:, t, c * P:(c + 1) * P], ident32[:, :])
                    last.then_inc(tr_done, 1)
                    for which, (wt, src) in enumerate((("wq", "xT"), ("wk", "cT"))):
                        pe.wait_ge(tr_lo, (i + 1) * 2 + which + 1)
                        for half in range(2):
                            n_ = which * 2 + half
                            bank = 4 + n_ % 2
                            if n_ >= 2:
                                pe.wait_ge(proj_out, (i + 1) * 5 + n_ - 1)
                            for g in (2 * half, 2 * half + 1):
                                o_ = psum[:, bank, (g % 2) * S:(g % 2 + 1) * S]
                                k = 0
                                for c in range(KT):
                                    for ws_, xs_ in ((0, 0), (0, 1), (1, 0)):
                                        last = mm(o_, w[wt][:, ws_, c, g, :], w[src][:, xs_, c, :],
                                                  start=k == 0, stop=k == 5)
                                        k += 1
                            last.then_inc(proj_done, 1)
                    pe.wait_ge(tr_lo, (i + 1) * 2 + 2)
                    for t in range(TT):
                        k = 0
                        for c in range(KT):
                            for xs_, ws_ in ((0, 0), (0, 1), (1, 0)):
                                last = mm(psum[:, 7, t * D:(t + 1) * D], w["cT"][:, xs_, c, t * P:(t + 1) * P],
                                          w["wv"][:, ws_, c, :], start=k == 0, stop=k == 5)
                                k += 1
                    last.then_inc(proj_done, 1)
                    pe.wait_ge(k1_ready, (i + 2) * (16 * GH))
                    pe.wait_ge(qk_hi, (i + 1) * 2 + 2)
                    for t in range(TT):
                        for g in range(G):
                            s_ = t * G + g
                            if s_ >= 2:
                                pe.wait_ge(mx_taken, (i + 1) * 8 + s_ - 1)
                            cols = pairs(t)
                            c0, c1 = cols[0] * P, (cols[-1] + 1) * P
                            for j in range(GH):
                                at = SC[s_ % 2][:, j * S + c0:j * S + c1]
                                last = mm(at, w["qh"][:, g, t * P:(t + 1) * P], w["k1"][:, j, g, c0:c1],
                                          start=True, stop=not causal_band)
                                if causal_band:
                                    for e, kt in enumerate(cols):
                                        last = mm(SC[s_ % 2][:, j * S + kt * P:j * S + (kt + 1) * P], ident16[:, :],
                                                  w["masks"][:, 2 if kt == t else 3, :], start=False,
                                                  stop=e == len(cols) - 1)
                            last.then_inc(mx_scores, 1)
                    pe.wait_ge(proj_out, (i + 1) * 5 + 4)
                    for half in range(2):
                        pe.wait_ge(mx_taken, (i + 1) * 8 + 8)
                        for g in (2 * half, 2 * half + 1):
                            for t in range(TT):
                                last = nc.tensor.transpose(
                                    psum[:, 4 + half, (g % 2) * S + t * P:(g % 2) * S + (t + 1) * P],
                                    w["m"][:, t, g, :], ident32[:, :])
                        last.then_inc(m_done, 1)
                    pe.wait_ge(q1_ready, i + 2)
                    pe.wait_ge(k2_ready, (i + 2) * (16 * GH))

                    def values(g):
                        for kt in range(TT):
                            pe.wait_ge(ex_done, (i + 1) * 8 + g * 2 + kt + 1)
                        if g == 0:
                            pe.wait_ge(proj_out, (i + 1) * 5 + 5)
                        if g >= 2:
                            pe.wait_ge(o_out, (i + 1) * 4 + g - 1)
                        q0 = {kt: (kt * P if causal_band else 0) for kt in range(TT)}
                        for kt in range(TT):
                            for j in range(GH):
                                last = mm(psum[j * SLOT:(j + 1) * SLOT, 6 if g % 2 else 7, q0[kt]:S],
                                          w["v"][:, kt, g * GH + j, :], w["pr"][:, g % 2, kt, j, q0[kt]:S],
                                          start=kt == 0, stop=kt == TT - 1, tile_position=(0, j * SLOT))
                        last.then_inc(av_done, 1)

                    for g in range(G):
                        pe.wait_ge(q2_ready, (i + 1) * 2 + g // 2 + 1)
                        for kt in range(TT):
                            s_ = g * TT + kt
                            if s_ >= 2:
                                pe.wait_ge(ex_done, (i + 1) * 8 + s_ - 1)
                            qs = [t for t in range(TT) if kt in pairs(t)]
                            a0, a1 = qs[0] * P, (qs[-1] + 1) * P
                            for j in range(GH):
                                at = SC[s_ % 2][:, j * S + a0:j * S + a1]
                                ks = slice(kt * P, (kt + 1) * P)
                                mm(at, w["k1"][:, j, g, ks], w["q1"][:, g, a0:a1], start=True, stop=False)
                                for t in qs:
                                    if t == kt or causal_band:
                                        mm(SC[s_ % 2][:, j * S + t * P:j * S + (t + 1) * P], ident16[:, :],
                                           w["masks"][:, 0 if t == kt else 1, :], start=False, stop=False)
                                last = mm(at, w["k2"][:, j, g, ks], w["q2"][:, g, a0:a1], start=False, stop=True)
                            last.then_inc(sc_done, 1)
                        if g:
                            values(g - 1)
                    values(G - 1)
                    pe.wait_ge(o_out, (i + 1) * 4 + 4)
                    pe.wait_ge(q2_ready, (i + 1) * 2 + 2)
                    for t in range(TT):
                        for g in range(G):
                            last = nc.tensor.transpose(psum[:, 4 + t, g * P:(g + 1) * P],
                                                       w["o"][:, g, t * P:(t + 1) * P], ident32[:, :])
                        last.then_inc(oT_done, 1)
                    pe.wait_ge(on_ready, (i + 1) * 2 + 2)
                    for c in range(KT):
                        for t in range(TT):
                            last = nc.tensor.transpose(psum[:, 6, c * S + t * P:c * S + (t + 1) * P],
                                                       w["on"][:, t, c * P:(c + 1) * P], ident32[:, :])
                    last.then_inc(on_T, 1)
                    pe.wait_ge(ol_ready, i + 2)
                    for t in range(TT):
                        y = psum[:, 7, t * D:(t + 1) * D]
                        k = 0
                        for c in range(KT):
                            for xs_, ws_ in ((0, 0), (0, 1), (1, 0)):
                                mm(y, w["oT"][:, xs_, c, t * P:(t + 1) * P], w["wo"][:, ws_, c, :],
                                   start=k == 0, stop=False)
                                k += 1
                        mm(y, w["ones"][0:1, :], w["bo"][0:1, 0, :], start=False, stop=False)
                        last = mm(y, w["ones"][0:1, :], w["bo"][0:1, 1, :], start=False, stop=True)
                    last.then_inc(y_done, 1)

            @block.scalar
            def _(act):
                A = nc.scalar.activation
                with act.Fori(0, B) as i:
                    for n_, (dst, bank) in enumerate((("xT", 7), ("cT", 6))):
                        act.wait_ge(tr_done, (i + 1) * 2 + n_ + 1)
                        if n_ == 0:
                            act.wait_ge(proj_done, (i + 1) * 5)
                        A(w[dst][:, 0, :, :], psum[:, bank, :].rearrange("p (c s) -> p c s", c=KT),
                          ACT.Copy).then_inc(tr_hi, 1)
                    for n_ in range(4):
                        act.wait_ge(proj_done, (i + 1) * 5 + n_ + 1)
                        if n_ == 0:
                            act.wait_ge(kl_ready, i + 1)
                            act.wait_ge(q1_ready, i + 1)
                        dst, bias = (w["qf"], w["bq"]) if n_ < 2 else (w["kf"], w["bk"])
                        for g in (n_ % 2 * 2, n_ % 2 * 2 + 1):
                            last = A(dst[:, g, :], psum[:, 4 + n_ % 2, (g % 2) * S:(g % 2 + 1) * S], ACT.Identity,
                                     bias=bias[:, g:g + 1])
                        last.then_inc(proj_out, 1)
                    act.wait_ge(proj_done, (i + 1) * 5 + 5)
                    act.wait_ge(av_done, (i + 1) * 4)
                    A(w["v"][:, :, :, 0:DH], psum[:, 7, :].rearrange("p (t h d) -> p t h d", t=TT, h=H),
                      ACT.Copy).then_inc(proj_out, 1)
                    for g in range(G):
                        for kt in range(TT):
                            s_ = g * TT + kt
                            act.wait_ge(sc_done, (i + 1) * 8 + s_ + 1)
                            if g >= 2:
                                act.wait_ge(av_done, (i + 1) * 4 + g - 1)
                            a0 = kt * P if causal_band else 0
                            A(w["pr"][:, g % 2, kt, :, a0:S],
                              SC[s_ % 2].rearrange("p (j s) -> p j s", j=GH)[:, :, a0:S],
                              ACT.Exp, scale=1.0 / math.sqrt(DH)).then_inc(ex_done, 1)
                        if g:
                            act.wait_ge(av_done, (i + 1) * 4 + g)
                            A(w["o"][:, g - 1, :], psum[:, 6 if (g - 1) % 2 else 7, 0:S], ACT.Copy).then_inc(o_out, 1)
                    act.wait_ge(av_done, (i + 1) * 4 + G)
                    A(w["o"][:, G - 1, :], psum[:, 6, 0:S], ACT.Copy).then_inc(o_out, 1)
                    act.wait_ge(on_T, i + 2)
                    for c in range(KT):
                        last = A(w["oT"][:, 0, c, :], psum[:, 6, c * S:(c + 1) * S], ACT.Identity,
                                 bias=w["bv"][:, c:c + 1])
                    last.then_inc(oh_ready, 1)

            @block.gpsimd
            def _(pool):
                with pool.Fori(0, B) as i:
                    if causal_band:
                        for n_, f in enumerate(("qf", "kf")):
                            hold(pool, f_ready, (i + 1) * 2 + n_ + 1)
                            pool.tensor_copy(w["qh" if n_ == 0 else "kh"][:, :, :], w[f][:, :, :]).then_inc(qk_hi, 1)
                    else:
                        for n_, f in enumerate(("qf", "kf")):
                            pool.wait_ge(proj_out, (i + 1) * 5 + 2 * n_ + 2)
                            if n_ == 0:
                                hold(pool, q2_ready, (i + 1) * 2)
                            else:
                                hold(pool, k1_ready, (i + 1) * (16 * GH))
                            pool.tensor_copy(w["qh" if n_ == 0 else "kh"][:, :, :], w[f][:, :, :]).then_inc(qk_hi, 1)
                    pool.wait_ge(qk_hi, (i + 1) * 2 + 2)
                    pool.wait_ge(k2_ready, (i + 1) * (16 * GH))
                    pool.tensor_tensor(w["kl"][:, :, :], w["kf"][:, :, :], w["kh"][:, :, :],
                                       ALU.subtract).then_inc(kl_ready, 1)

            @block.vector
            def _(dve):
                V = nc.vector
                with dve.Fori(0, B) as i:
                    dve.wait_ge(tr_done, (i + 1) * 2)
                    for t in range(TT):
                        V.tensor_scalar(w["xn"][:, t, :], x[:, i * TT + t, :], mv[:, i * TT + t, 0:1],
                                        rstd[:, bass.ds(i * TT + t, 1)], ALU.subtract, ALU.mult).then_inc(xn_ready, 1)
                    for n_, (dst, bank) in enumerate((("xT", 7), ("cT", 6))):
                        dve.wait_ge(tr_hi, (i + 1) * 2 + n_ + 1)
                        V.tensor_tensor(w[dst][:, 1, :, :], psum[:, bank, :].rearrange("p (c s) -> p c s", c=KT),
                                        w[dst][:, 0, :, :], ALU.subtract).then_inc(tr_lo, 1)
                    if causal_band:
                        swap = [(r // DH) * DH + (r % DH + DH // 2) % DH for r in range(SLOT)]
                        for n_, f in enumerate(("qf", "kf")):
                            dve.wait_ge(proj_out, (i + 1) * 5 + 2 * n_ + 2)
                            if n_:
                                dve.wait_ge(f_ready, (i + 1) * 2 + 1)
                            dve.sem_inc(waited, 1)
                            V.stream_shuffle(w["rot"][:, :, :], w[f][:, :, :], swap).then_inc(rope, 1)
                            dve.wait_ge(rope, (i + 1) * 6 + n_ * 3 + 1)
                            cosb = w["cos"][:, :].unsqueeze(1).broadcast_to([P, G, S])
                            sinb = w["sin"][:, :].unsqueeze(1).broadcast_to([P, G, S])
                            V.tensor_tensor(w["rot"][:, :, :], w["rot"][:, :, :], sinb, ALU.mult).then_inc(rope, 1)
                            V.tensor_tensor(w[f][:, :, :], w[f][:, :, :], cosb, ALU.mult).then_inc(rope, 1)
                            dve.wait_ge(rope, (i + 1) * 6 + n_ * 3 + 3)
                            if n_ == 0:
                                dve.wait_ge(q2_ready, (i + 1) * 2)
                            else:
                                dve.wait_ge(k1_ready, (i + 1) * (16 * GH))
                            V.tensor_tensor(w[f][:, :, :], w[f][:, :, :], w["rot"][:, :, :],
                                            ALU.add).then_inc(f_ready, 1)
                    dve.wait_ge(qk_hi, (i + 1) * 2 + 1)
                    dve.wait_ge(sc_done, (i + 1) * 8)
                    V.scalar_tensor_tensor(w["q1"][:, :, :], w["qh"][:, :, :], w["hi_rows"][:, 0:1], w["qf"][:, :, :],
                                           ALU.mult, ALU.add).then_inc(q1_ready, 1)
                    for t in range(TT):
                        for g in range(G):
                            s_ = t * G + g
                            dve.wait_ge(mx_scores, (i + 1) * 8 + s_ + 1)
                            cols = pairs(t)
                            src = SC[s_ % 2].rearrange("p (j s) -> p j s", j=GH)[:, :, cols[0] * P:(cols[-1] + 1) * P]
                            V.tensor_reduce(w["m"][:, t, g, DH::SLOT], src, AX.X, ALU.max,
                                            negate=True).then_inc(mx_taken, 1)
                    for half in range(2):
                        dve.wait_ge(m_done, (i + 1) * 2 + half + 1)
                        V.scalar_tensor_tensor(w["q2"][:, 2 * half:2 * half + 2, :], w["qh"][:, 2 * half:2 * half + 2, :],
                                               w["hi_rows"][:, 1:2],
                                               psum[:, 4 + half, :].rearrange("p (g s) -> p g s", g=2),
                                               ALU.mult, ALU.add).then_inc(q2_ready, 1)
                    for t in range(TT):
                        dve.wait_ge(oT_done, (i + 1) * 2 + t + 1)
                        heads = psum[:, 4 + t, :].rearrange("p (h r) -> p h r", r=SLOT)
                        V.reciprocal(w["rd"][:, t, :], heads[:, :, DH]).then_inc(rd_ready, 1)
                        dve.wait_ge(rd_ready, (i + 1) * 2 + t + 1)
                        V.tensor_tensor(w["on"][:, t, :].rearrange("p (h d) -> p h d", h=H), heads[:, :, 0:DH],
                                        w["rd"][:, t, :].unsqueeze(2).broadcast_to([P, H, DH]),
                                        ALU.mult).then_inc(on_ready, 1)
                    dve.wait_ge(oh_ready, i + 2)
                    for c in range(KT):
                        last = V.scalar_tensor_tensor(w["oT"][:, 1, c, :], psum[:, 6, c * S:(c + 1) * S],
                                                      w["bv"][:, c:c + 1], w["oT"][:, 0, c, :],
                                                      ALU.add, ALU.subtract)
                    last.then_inc(ol_ready, 1)
                    dve.wait_ge(y_done, i + 2)
                    for t in range(TT):
                        last = V.scalar_tensor_tensor(x[:, i * TT + t, :], psum[:, 7, t * D:(t + 1) * D],
                                                      gate[:, 2 * L:2 * L + 1], x[:, i * TT + t, :],
                                                      ALU.mult, ALU.add)
                    last.then_inc(x_new, 1)
                    hold(dve, x_new, i + 2)
                    token_stats(dve, i, st_chain)
        stack.close()

    def moe0():
        E0, F0, CAP = 8, 896, 80
        FT = F0 // P
        ROWS = B * CAP
        CH = 256
        NC = ROWS // CH
        CT = CH // P
        STEPS = E0 * NC
        WP = KT * F0
        disp = nc.dram_tensor("dispatched", (E0 * ROWS, D), F32, kind="Internal").ap()
        eo = nc.dram_tensor("expert_out", (E0 * ROWS, D), F32, kind="Internal").ap()
        stack = ExitStack()

        def sb(name, shape, dt):
            return stack.enter_context(nc.sbuf_tensor("m0_" + name, shape, dt))

        gidx = sb("gather_row", [P, NT, 2], U32)
        gw = sb("gather_weight", [P, NT, 2], F32)

        r = ExitStack()

        def rb(name, shape, dt):
            return r.enter_context(nc.sbuf_tensor("m0_" + name, shape, dt))

        zero = rb("zero", [P, 8, D], F32)
        xn = rb("xn", [P, 2, TT, D], F32)
        xT = rb("xT32", [P, KT, S], F32)
        gate_w = rb("router", [P, KT, E0], F32)
        tri = rb("tri", [P, 2, P], F16)
        iota = rb("iota", [P, E0], F32)
        base = rb("seq_base", [P, 1], F32)
        lg = rb("logits", [P, TT, E0], F32)
        mx = rb("row_max", [P, TT], F32)
        pr = rb("probs", [P, TT, E0], F32)
        rs = rb("row_sum", [P, TT], F32)
        top = rb("top", [P, TT, 8], F32)
        ti = rb("top_index", [P, TT, 8], U32)
        tf = rb("top_index_f", [P, TT, 2], F32)
        oh = rb("one_hot", [P, 2, TT, E0], F32)
        msk = rb("chosen", [P, TT, E0], F16)
        pos = rb("position", [P, TT, E0], F32)
        tmp = rb("picked", [P, 2, 2, TT, E0], F32)
        pk = rb("picked_sum", [P, 2, 2, TT], F32)
        keep = rb("kept", [P, 2, TT], F32)
        row = rb("row", [P, 2, TT], F32)
        far = rb("row_or_far", [P, 2, TT], F32)
        sidx = rb("scatter_row", [P, 2, 2, TT], U32)
        ld = sem("m0_loaded")
        zr = sem("m0_zeroed")
        zset = sem("m0_zero_set")
        with nc.Block() as block:

            @block.sync
            def _(sp):
                sp.dma_start(gate_w[:, :, :], a["L0_router"]).then_inc(ld, 16)
                sp.dma_start(tri[:, :, :], a["tri"]).then_inc(ld, 16)
                sp.dma_start(iota[:, :], a["iota"][:, 0:E0]).then_inc(ld, 16)
                sp.wait_ge(ld, 48)
                sp.wait_ge(zset, 2)
                for c in range(E0 * ROWS // (P * 8)):
                    sp.dma_start(disp[c * P * 8:(c + 1) * P * 8, :].rearrange("(p t) d -> p t d", p=P),
                                 zero[:, :, :]).then_inc(zr, 16)
                sp.wait_ge(zr, 16 * (E0 * ROWS // (P * 8)))

            @block.gpsimd
            def _(pool):
                pool.memset(zero[:, :, :], 0.0).then_inc(zset, 1)
                pool.memset(base[:, :], -1.0).then_inc(zset, 1)

        xn_ready = sem("m0_xn_ready")
        xT_done = sem("m0_xT_done")
        xT_out = sem("m0_xT_out")
        lg_done = sem("m0_logits_done")
        sh_ready = sem("m0_shifted")
        ex_ready = sem("m0_exp")
        m_ready = sem("m0_chosen")
        pos_done = sem("m0_positions")
        idx_ready = sem("m0_rows_ready")
        sent = sem("m0_sent")
        sent_seq = sem("m0_sent_seq")
        ch = sem("m0_chain")
        CHN = 20
        with nc.Block() as block:

            @block.sync
            def _(sp):
                for counter, number in ((xn_ready, 1), (xT_done, 1), (xT_out, 1), (lg_done, 1), (sh_ready, 1),
                                        (ex_ready, 1), (m_ready, 1), (pos_done, 1), (idx_ready, 1), (sent_seq, 2),
                                        (ch, CHN)):
                    sp.sem_inc(counter, number)

        with nc.Block() as block:

            @block.tensor
            def _(pe):
                with pe.Fori(0, B // 2) as i:
                    for u in range(2):
                        n = i * 2 + u
                        pe.wait_ge(xn_ready, n + 2)
                        pe.wait_ge(xT_out, n + 1)
                        for c in range(KT):
                            for t in range(TT):
                                last = nc.tensor.transpose(psum[:, 0, c * S + t * P:c * S + (t + 1) * P],
                                                           xn[:, u, t, c * P:(c + 1) * P], ident32[:, :])
                        last.then_inc(xT_done, 1)
                        pe.wait_ge(xT_out, n + 2)
                        pe.wait_ge(sh_ready, n + 1)
                        for t in range(TT):
                            for c in range(KT):
                                last = nc.tensor.matmul(psum[:, 1, t * E0:(t + 1) * E0], xT[:, c, t * P:(t + 1) * P],
                                                        gate_w[:, c, :], start=c == 0, stop=c == KT - 1)
                        last.then_inc(lg_done, 1)
                        pe.wait_ge(m_ready, n + 2)
                        nc.tensor.matmul(psum[:, 2, 0:E0], tri[:, 0, :], msk[:, 0, :], start=True, stop=True)
                        nc.tensor.matmul(psum[:, 2, E0:2 * E0], tri[:, 0, :], msk[:, 1, :], start=True, stop=False)
                        nc.tensor.matmul(psum[:, 2, E0:2 * E0], tri[:, 1, :], msk[:, 0, :], start=False,
                                         stop=True).then_inc(pos_done, 1)

            @block.scalar
            def _(act):
                with act.Fori(0, B) as n:
                    act.wait_ge(xT_done, n + 2)
                    act.wait_ge(lg_done, n + 1)
                    nc.scalar.activation(xT[:, :, :], psum[:, 0, :].rearrange("p (c s) -> p c s", c=KT),
                                         ACT.Copy).then_inc(xT_out, 1)
                    act.wait_ge(sh_ready, n + 2)
                    nc.scalar.activation(pr[:, :, :], lg[:, :, :], ACT.Exp).then_inc(ex_ready, 1)

            @block.gpsimd
            def _(pool):
                with pool.Fori(0, B // 2) as i:
                    for u in range(2):
                        hold(pool, idx_ready, i * 2 + u + 2)
                        for t in range(TT):
                            for k in range(2):
                                pool.indirect_dma_start(
                                    disp, bass.IndirectOffsetOnAxis(ap=sidx[:, u, k, t:t + 1], axis=0),
                                    xn[:, u, t, :], None, bounds_check=E0 * ROWS - 1, oob_is_err=False)\
                                    .then_inc(sent, 16)
                        hold(pool, sent, (i * 2 + u + 1) * 64)
                        pool.sem_inc(sent_seq, 1)

            @block.vector
            def _(dve):
                V = nc.vector

                with dve.Fori(0, B // 2) as i:
                    for u in range(2):
                        n = i * 2 + u
                        step = [0]

                        def link(ins, step=step, n=n):
                            step[0] += 1
                            ins.then_inc(ch, 1)
                            hold(dve, ch, (n + 1) * CHN + step[0])

                        hold(dve, sent_seq, n + 1)
                        for t in range(TT):
                            nt = n * TT + t
                            last = V.tensor_scalar(xn[:, u, t, :],
                                                   x[:, bass.ds(nt, 1), :].rearrange("p a d -> p (a d)"),
                                                   mv[:, bass.ds(nt, 1), 0], rstd[:, bass.ds(nt, 1)],
                                                   ALU.subtract, ALU.mult)
                        last.then_inc(xn_ready, 1)
                        dve.wait_ge(lg_done, n + 2)
                        link(V.tensor_reduce(mx[:, :], psum[:, 1, 0:TT * E0].rearrange("p (t e) -> p t e", e=E0),
                                             AX.X, ALU.max))
                        V.tensor_tensor(lg[:, :, :], psum[:, 1, 0:TT * E0].rearrange("p (t e) -> p t e", e=E0),
                                        mx[:, :].unsqueeze(2).broadcast_to([P, TT, E0]),
                                        ALU.subtract).then_inc(sh_ready, 1)
                        dve.wait_ge(ex_ready, n + 2)
                        link(V.tensor_reduce(rs[:, :], pr[:, :, :], AX.X, ALU.add))
                        link(V.reciprocal(rs[:, :], rs[:, :]))
                        link(V.tensor_tensor(pr[:, :, :], pr[:, :, :], rs[:, :].unsqueeze(2).broadcast_to([P, TT, E0]),
                                             ALU.mult))
                        V.max(top[:, 0, :], pr[:, 0, :])
                        link(V.max(top[:, 1, :], pr[:, 1, :]))
                        V.max_index(ti[:, 0, :], top[:, 0, :], pr[:, 0, :])
                        link(V.max_index(ti[:, 1, :], top[:, 1, :], pr[:, 1, :]))
                        link(V.tensor_copy(tf[:, :, :], ti[:, :, 0:2]))
                        for k in range(2):
                            last = V.tensor_tensor(oh[:, k, :, :], iota[:, :].unsqueeze(1).broadcast_to([P, TT, E0]),
                                                   tf[:, :, k:k + 1].broadcast_to([P, TT, E0]), ALU.is_equal)
                        link(last)
                        V.tensor_tensor(msk[:, :, :], oh[:, 0, :, :], oh[:, 1, :, :], ALU.add).then_inc(m_ready, 1)
                        for k in range(2):
                            V.tensor_tensor(tmp[:, 1, k, :, :], oh[:, k, :, :], pr[:, :, :], ALU.mult)
                        dve.wait_ge(pos_done, n + 2)
                        for k in range(2):
                            last = V.tensor_tensor(tmp[:, 0, k, :, :], oh[:, k, :, :],
                                                   psum[:, 2, 0:TT * E0].rearrange("p (t e) -> p t e", e=E0), ALU.mult)
                        link(last)
                        link(V.tensor_reduce(pk[:, :, :, :].rearrange("p a k t -> p (a k t)"),
                                             tmp[:, :, :, :, :].rearrange("p a k t e -> p (a k t) e"), AX.X, ALU.add))
                        V.tensor_scalar(keep[:, :, :], pk[:, 0, :, :], float(CAP), None, ALU.is_le)
                        link(V.scalar_tensor_tensor(row[:, :, :], tf[:, :, :].rearrange("p t k -> p k t"), float(ROWS),
                                                    pk[:, 0, :, :], ALU.mult, ALU.add))
                        link(V.tensor_scalar(row[:, :, :], row[:, :, :], base[:, :], None, ALU.add))
                        link(V.tensor_scalar(far[:, :, :], keep[:, :, :], -float(1 << 20), float(1 << 20),
                                             ALU.mult, ALU.add))
                        V.tensor_tensor(sidx[:, u, :, :], row[:, :, :], far[:, :, :], ALU.add).then_inc(idx_ready, 1)
                        V.tensor_tensor(gidx[:, bass.ds(n * TT, TT), :].rearrange("p t k -> p k t"), row[:, :, :],
                                        keep[:, :, :], ALU.mult)
                        link(V.tensor_tensor(pk[:, 1, :, :], pk[:, 1, :, :], keep[:, :, :], ALU.mult))
                        V.tensor_scalar(gw[:, bass.ds(n * TT, TT), :].rearrange("p t k -> p k t"), pk[:, 1, :, :],
                                        gate[:, 1:2], None, ALU.mult)
                        link(V.tensor_scalar(base[:, :], base[:, :], float(CAP), None, ALU.add))
                        while step[0] < CHN:
                            dve.sem_inc(ch, 1)
                            step[0] += 1
        r.close()

        f = ExitStack()

        def fb(name, shape, dt):
            return f.enter_context(nc.sbuf_tensor("m0_" + name, shape, dt))

        wl = fb("w_load", [P, 3, WP], F32)
        wh = fb("w_halves", [P, 2, 2, 3, WP], F16)
        rows = fb("rows", [P, CT, D], F32)
        xT = fb("xT", [P, 2, 2, KT, ROWS], F16)
        hsb = fb("silu", [P, 2, CH], F32)
        hp = fb("hidden", [P, 2, CH], F32)
        hT = fb("hiddenT", [P, 2, FT, CH], F16)
        y = fb("y", [P, CT, D], F32)
        w_dram = [a["L0_w1"], a["L0_w3"], a["L0_w2"]]
        w_loaded = sem("m0f_w_loaded")
        w_hi = sem("m0f_w_hi")
        w_lo = sem("m0f_w_lo")
        rows_in = sem("m0f_rows_in")
        rT_done = sem("m0f_rows_transposed")
        xT_hi = sem("m0f_xT_hi")
        xT_lo = sem("m0f_xT_lo")
        h_done = sem("m0f_h_done")
        s_done = sem("m0f_silu")
        g_done = sem("m0f_gated")
        hh = sem("m0f_hidden_hi")
        hl = sem("m0f_hidden_lo")
        y_done = sem("m0f_y_done")
        y_out = sem("m0f_y_out")
        y_sent = sem("m0f_y_sent")
        y_free = sem("m0f_y_free")
        with nc.Block() as block:

            @block.sync
            def _(sp):
                for counter, number in ((w_loaded, 48), (w_hi, 3), (w_lo, 3), (rows_in, 16), (rT_done, 1),
                                        (xT_hi, 1), (xT_lo, 1), (h_done, FT), (s_done, FT), (g_done, FT), (hh, FT),
                                        (hl, FT), (y_done, 1), (y_out, 1), (y_free, 1)):
                    sp.sem_inc(counter, number)

        def both_(eng, prepare, compute, e, u, c, n):
            compute(u, c, n, lambda: prepare(e + 1, 1 - u, c, n + NC))

        with nc.Block() as block:

            @block.sync
            def _(sp):
                with sp.Fori(0, E0) as e:
                    hold(sp, w_lo, (e + 1) * 3)
                    for m in range(3):
                        sp.dma_start(wl[:, m, :], w_dram[m][e, :, :]).then_inc(w_loaded, 16)
                    with sp.Fori(0, NC) as c:
                        q = e * NC + c
                        hold(sp, rT_done, q + 1)
                        sp.dma_start(rows[:, :, :],
                                     disp[bass.ds(q * CH, CH), :].rearrange("(t p) d -> p t d", p=P))\
                            .then_inc(rows_in, 16)

            @block.gpsimd
            def _(pool):
                with pool.Fori(0, STEPS) as n:
                    hold(pool, y_out, n + 2)
                    pool.dma_start(eo[bass.ds(n * CH, CH), :].rearrange("(t p) d -> p t d", p=P), y[:, :, :])\
                        .then_inc(y_sent, 16)
                    hold(pool, y_sent, (n + 1) * 16)
                    pool.sem_inc(y_free, 1)

            @block.tensor
            def _(pe):
                mm = nc.tensor.matmul

                def prepare(e, u, c, q):
                    pe.wait_ge(rows_in, (q + 2) * 16)
                    pe.wait_ge(xT_lo, q + 1)
                    for d_ in range(KT):
                        for t in range(CT):
                            last = nc.tensor.transpose(psum[:, 3, d_ * CH + t * P:d_ * CH + (t + 1) * P],
                                                       rows[:, t, d_ * P:(d_ + 1) * P], ident32[:, :])
                    last.then_inc(rT_done, 1)

                def compute(u, c, n, fill):
                    pe.wait_ge(xT_lo, n + 2)

                    def hidden(f_):
                        if f_ >= 3:
                            pe.wait_ge(g_done, (n + 1) * FT + f_ - 2)
                        else:
                            pe.wait_ge(g_done, (n + 1) * FT)
                        for m in range(2):
                            k = 0
                            for d_ in range(KT):
                                for ws_, xs_ in ((0, 0), (0, 1), (1, 0)):
                                    last = mm(psum[:, f_ % 3, m * CH:(m + 1) * CH],
                                              wh[:, u, ws_, m, d_ * F0 + f_ * P:d_ * F0 + (f_ + 1) * P],
                                              xT[:, u, xs_, d_, bass.ds(c * CH, CH)],
                                              start=k == 0, stop=k == 5)
                                    k += 1
                        last.then_inc(h_done, 1)

                    def down(f_):
                        pe.wait_ge(hl, (n + 1) * FT + f_ + 1)
                        if f_ == 0:
                            pe.wait_ge(y_out, n + 1)
                        for t in range(CT):
                            k = 0
                            for hs_, ws_ in ((0, 0), (0, 1), (1, 0)):
                                last = mm(psum[:, 4 + t, 0:D], hT[:, hs_, f_, t * P:(t + 1) * P],
                                          wh[:, u, ws_, 2, f_ * D:(f_ + 1) * D],
                                          start=f_ == 0 and k == 0, stop=f_ == FT - 1 and k == 2)
                                k += 1
                        if f_ == FT - 1:
                            last.then_inc(y_done, 1)

                    for f_ in range(FT):
                        hidden(f_)
                        if f_:
                            down(f_ - 1)
                    fill()
                    down(FT - 1)

                with pe.Fori(0, NC) as c:
                    prepare(0, 0, c, c)
                pe.wait_ge(w_lo, 6)
                with pe.Fori(0, E0 // 2 - 1) as i:
                    for u in range(2):
                        hold(pe, w_lo, (i * 2 + u + 2) * 3)
                        with pe.Fori(0, NC) as c:
                            both_(pe, prepare, compute, i * 2 + u, u, c, (i * 2 + u) * NC + c)
                pe.wait_ge(w_lo, E0 * 3)
                with pe.Fori(0, NC) as c:
                    both_(pe, prepare, compute, E0 - 2, 0, c, (E0 - 2) * NC + c)
                pe.wait_ge(w_lo, (E0 + 1) * 3)
                with pe.Fori(0, NC) as c:
                    compute(1, c, (E0 - 1) * NC + c, lambda: None)

            @block.scalar
            def _(act):
                A = nc.scalar.activation

                def prepare(e, u, c, q):
                    act.wait_ge(rT_done, q + 2)
                    A(xT[:, u, 0, :, bass.ds(c * CH, CH)], psum[:, 3, :].rearrange("p (c s) -> p c s", c=KT),
                      ACT.Copy).then_inc(xT_hi, 1)

                def weights(e, u):
                    for m in range(3):
                        act.wait_ge(w_loaded, (e + 2) * 48)
                        A(wh[:, u, 0, m, :], wl[:, m, :], ACT.Copy).then_inc(w_hi, 1)

                def compute(u, c, n, fill):
                    for f_ in range(FT):
                        act.wait_ge(h_done, (n + 1) * FT + f_ + 1)
                        act.wait_ge(g_done, (n + 1) * FT + f_ - 1)
                        A(hsb[:, f_ % 2, :], psum[:, f_ % 3, 0:CH], ACT.Silu).then_inc(s_done, 1)
                        if f_:
                            upper(n, f_ - 1)
                    fill()
                    upper(n, FT - 1)

                def upper(n, f_):
                    act.wait_ge(g_done, (n + 1) * FT + f_ + 1)
                    if f_ == 0:
                        act.wait_ge(y_done, n + 1)
                    A(hT[:, 0, f_, :], hp[:, f_ % 2, :], ACT.Copy).then_inc(hh, 1)

                weights(0, 0)
                with act.Fori(0, NC) as c:
                    prepare(0, 0, c, c)
                with act.Fori(0, E0 // 2 - 1) as i:
                    for u in range(2):
                        act.wait_ge(y_done, (i * 2 + u) * NC + 1)
                        weights(i * 2 + u + 1, 1 - u)
                        with act.Fori(0, NC) as c:
                            both_(act, prepare, compute, i * 2 + u, u, c, (i * 2 + u) * NC + c)
                act.wait_ge(y_done, (E0 - 2) * NC + 1)
                weights(E0 - 1, 1)
                with act.Fori(0, NC) as c:
                    both_(act, prepare, compute, E0 - 2, 0, c, (E0 - 2) * NC + c)
                with act.Fori(0, NC) as c:
                    compute(1, c, (E0 - 1) * NC + c, lambda: None)

            @block.vector
            def _(dve):
                V = nc.vector

                def prepare(e, u, c, q):
                    dve.wait_ge(xT_hi, q + 2)
                    V.tensor_tensor(xT[:, u, 1, :, bass.ds(c * CH, CH)],
                                    psum[:, 3, :].rearrange("p (c s) -> p c s", c=KT),
                                    xT[:, u, 0, :, bass.ds(c * CH, CH)], ALU.subtract).then_inc(xT_lo, 1)

                def weights(e, u):
                    for m in range(3):
                        dve.wait_ge(w_hi, (e + 1) * 3 + m + 1)
                        V.tensor_tensor(wh[:, u, 1, m, :], wl[:, m, :], wh[:, u, 0, m, :],
                                        ALU.subtract).then_inc(w_lo, 1)

                def lower(n, f_):
                    dve.wait_ge(hh, (n + 1) * FT + f_ + 1)
                    V.tensor_tensor(hT[:, 1, f_, :], hp[:, f_ % 2, :], hT[:, 0, f_, :], ALU.subtract).then_inc(hl, 1)

                def compute(u, c, n, fill):
                    for f_ in range(FT):
                        dve.wait_ge(s_done, (n + 1) * FT + f_ + 1)
                        dve.wait_ge(hl, (n + 1) * FT + f_ - 1)
                        V.tensor_tensor(hp[:, f_ % 2, :], psum[:, f_ % 3, CH:2 * CH], hsb[:, f_ % 2, :],
                                        ALU.mult).then_inc(g_done, 1)
                        if f_:
                            lower(n, f_ - 1)
                    fill()
                    lower(n, FT - 1)
                    dve.wait_ge(y_done, n + 2)
                    dve.wait_ge(y_free, n + 1)
                    V.tensor_copy(y[:, :, :], psum[:, 4:4 + CT, 0:D]).then_inc(y_out, 1)

                weights(0, 0)
                with dve.Fori(0, NC) as c:
                    prepare(0, 0, c, c)
                with dve.Fori(0, E0 // 2 - 1) as i:
                    for u in range(2):
                        weights(i * 2 + u + 1, 1 - u)
                        with dve.Fori(0, NC) as c:
                            both_(dve, prepare, compute, i * 2 + u, u, c, (i * 2 + u) * NC + c)
                weights(E0 - 1, 1)
                with dve.Fori(0, NC) as c:
                    both_(dve, prepare, compute, E0 - 2, 0, c, (E0 - 2) * NC + c)
                with dve.Fori(0, NC) as c:
                    compute(1, c, (E0 - 1) * NC + c, lambda: None)
        f.close()

        g_ = ExitStack()
        NB = 4
        yb = g_.enter_context(nc.sbuf_tensor("m0_gathered", [P, NB, TT, 2, D], F32))
        gi = g_.enter_context(nc.sbuf_tensor("m0_rows_of_seq", [P, NB, TT, 2], U32))
        gi_ready = sem("m0g_rows")
        got = [sem(f"m0g_gathered{u}") for u in range(NB)]
        used = sem("m0g_used")
        st_chain = sem("m0g_stats")
        with nc.Block() as block:

            @block.sync
            def _(sp):
                for counter, number in ((gi_ready, 1), (used, NB * 2 * TT), (st_chain, 5)):
                    sp.sem_inc(counter, number)

        with nc.Block() as block:

            @block.gpsimd
            def _(pool):
                with pool.Fori(0, B // NB) as i:
                    for u in range(NB):
                        n = i * NB + u
                        hold(pool, used, (n + 1) * 2 * TT)
                        pool.tensor_copy(gi[:, u, :, :], gidx[:, bass.ds(n * TT, TT), :]).then_inc(gi_ready, 1)
                        hold(pool, gi_ready, n + 2)
                        for t in range(TT):
                            for k in range(2):
                                pool.indirect_dma_start(
                                    yb[:, u, t, k, :], None, eo,
                                    bass.IndirectOffsetOnAxis(ap=gi[:, u, t, k:k + 1], axis=0)).then_inc(got[u], 16)

            @block.vector
            def _(dve):
                with dve.Fori(0, B // NB) as i:
                    for u in range(NB):
                        n = i * NB + u
                        dve.wait_ge(got[u], (i + 1) * 64)
                        for k in range(2):
                            for t in range(TT):
                                xt = x[:, bass.ds(n * TT + t, 1), :].rearrange("p a d -> p (a d)")
                                nc.vector.scalar_tensor_tensor(xt, yb[:, u, t, k, :],
                                                               gw[:, bass.ds(n * TT + t, 1), k], xt,
                                                               ALU.mult, ALU.add).then_inc(used, 1)
                            hold(dve, used, (n + NB) * 2 * TT + (k + 1) * TT)
                        token_stats(dve, n, st_chain)
        g_.close()
        stack.close()

    def moe1():
        E1, K1, NG = 16, 4, 4
        EG = E1 // NG
        NE = E1 + 2
        CH = 512
        CT = CH // P
        NC = B * S // CH
        WE = (2 * KT + 2) * P
        SCALE = 2.5
        stack = ExitStack()

        def sb(name, shape, dt):
            return stack.enter_context(nc.sbuf_tensor("m1_" + name, shape, dt))

        ew = sb("expert_weight", [P, NT, NE], F32)
        xTa = sb("xT_all", [P, 2, KT, B * S], F16)
        wh = sb("w_halves", [P, 2, NE, WE], F16)
        NL = 3
        r = ExitStack()

        def rb(name, shape, dt):
            return r.enter_context(nc.sbuf_tensor("m1_" + name, shape, dt))

        wl = rb("w_load", [P, NE // NL, WE], F32)
        xn = rb("xn", [P, 2, TT, D], F32)
        xT = rb("xT32", [P, KT, S], F32)
        router = rb("router", [P, KT, E1], F32)
        e_bias = rb("e_bias", [P, E1], F32)
        iota = rb("iota", [P, E1], F32)
        less = rb("less", [P, NG, NG], F32)
        sg = rb("scores", [P, TT, E1], F32)
        sc = rb("biased", [P, TT, E1], F32)
        hi2 = rb("pair_max", [P, TT * NG, 2], F32)
        lo2 = rb("pair_min", [P, TT * NG, 2], F32)
        g1 = rb("group_first", [P, TT * NG], F32)
        g2 = rb("group_second", [P, TT * NG], F32)
        g3 = rb("group_third", [P, TT * NG], F32)
        gt = rb("above", [P, TT, NG, NG], F32)
        eq = rb("equal", [P, TT, NG, NG], F32)
        rank = rb("rank", [P, TT, NG], F32)
        top = rb("top", [P, TT, 8], F32)
        ti = rb("top_index", [P, TT, 8], U32)
        tf = rb("top_index_f", [P, TT, K1], F32)
        oh = rb("one_hot", [P, TT, K1, E1], F32)
        sel = rb("chosen", [P, TT, E1], F32)
        den = rb("denominator", [P, TT], F32)
        ld = sem("m1_loaded")
        w_loaded = sem("m1_w_loaded")
        w_hi = sem("m1_w_hi")
        w_lo = sem("m1_w_lo")
        xn_ready = sem("m1_xn_ready")
        xT_done = sem("m1_xT_done")
        xT_out = sem("m1_xT_out")
        xT_hi = sem("m1_xT_hi")
        xT_lo = sem("m1_xT_lo")
        lg_done = sem("m1_logits_done")
        sg_ready = sem("m1_scores")
        ch = sem("m1_chain")
        ew_chain = sem("m1_weights_chain")
        CHN = 21
        with nc.Block() as block:

            @block.sync
            def _(sp):
                for counter, number in ((xn_ready, 1), (xT_done, 1), (xT_out, 1), (xT_hi, 1), (xT_lo, 1),
                                        (lg_done, 1), (sg_ready, 1), (ch, CHN)):
                    sp.sem_inc(counter, number)
                for dst, k in ((router[:, :, :], "L1_router"), (e_bias[:, :], "L1_e_bias"), (iota[:, :], "iota"),
                               (less[:, :, :], "less")):
                    sp.dma_start(dst, a[k]).then_inc(ld, 16)
                sp.wait_ge(ld, 64)

            @block.vector
            def _(dve):
                nc.vector.tensor_scalar(ew[:, :, E1:NE], mv[:, :, 0:NE - E1], 0.0, gate[:, 3:4], ALU.mult, ALU.add)

        with nc.Block() as block:

            @block.sync
            def _(sp):
                n = NE // NL
                for c in range(NL):
                    if c:
                        sp.wait_ge(w_lo, c)
                    sp.dma_start(wl[:, :, :], a["L1_experts"][:, c * n:(c + 1) * n, :]).then_inc(w_loaded, 16)

            @block.tensor
            def _(pe):
                with pe.Fori(0, B // 2) as i:
                    for u in range(2):
                        n = i * 2 + u
                        pe.wait_ge(xn_ready, n + 2)
                        pe.wait_ge(xT_lo, n + 1)
                        for c in range(KT):
                            for t in range(TT):
                                last = nc.tensor.transpose(psum[:, 0, c * S + t * P:c * S + (t + 1) * P],
                                                           xn[:, u, t, c * P:(c + 1) * P], ident32[:, :])
                        last.then_inc(xT_done, 1)
                        pe.wait_ge(xT_out, n + 2)
                        pe.wait_ge(sg_ready, n + 1)
                        for t in range(TT):
                            for c in range(KT):
                                last = nc.tensor.matmul(psum[:, 1, t * E1:(t + 1) * E1], xT[:, c, t * P:(t + 1) * P],
                                                        router[:, c, :], start=c == 0, stop=c == KT - 1)
                        last.then_inc(lg_done, 1)

            @block.scalar
            def _(act):
                A = nc.scalar.activation
                n_ = NE // NL
                for c in range(NL):
                    act.wait_ge(w_loaded, 16 * (c + 1))
                    A(wh[:, 0, c * n_:(c + 1) * n_, :], wl[:, :, :], ACT.Copy).then_inc(w_hi, 1)
                with act.Fori(0, B) as n:
                    act.wait_ge(xT_done, n + 2)
                    act.wait_ge(lg_done, n + 1)
                    A(xT[:, :, :], psum[:, 0, :].rearrange("p (c s) -> p c s", c=KT), ACT.Copy).then_inc(xT_out, 1)
                    A(xTa[:, 0, :, bass.ds(n * S, S)], psum[:, 0, :].rearrange("p (c s) -> p c s", c=KT),
                      ACT.Copy).then_inc(xT_hi, 1)
                    act.wait_ge(lg_done, n + 2)
                    A(sg[:, :, :], psum[:, 1, 0:TT * E1].rearrange("p (t e) -> p t e", e=E1),
                      ACT.Sigmoid).then_inc(sg_ready, 1)

            @block.vector
            def _(dve):
                V = nc.vector
                n_ = NE // NL
                for c in range(NL):
                    dve.wait_ge(w_hi, c + 1)
                    V.tensor_tensor(wh[:, 1, c * n_:(c + 1) * n_, :], wl[:, :, :], wh[:, 0, c * n_:(c + 1) * n_, :],
                                    ALU.subtract).then_inc(w_lo, 1)
                with dve.Fori(0, B // 2) as i:
                    for u in range(2):
                        n = i * 2 + u
                        step = [0]

                        def link(ins, step=step, n=n):
                            step[0] += 1
                            ins.then_inc(ch, 1)
                            hold(dve, ch, (n + 1) * CHN + step[0])

                        for t in range(TT):
                            nt = n * TT + t
                            last = V.tensor_scalar(xn[:, u, t, :],
                                                   x[:, bass.ds(nt, 1), :].rearrange("p a d -> p (a d)"),
                                                   mv[:, bass.ds(nt, 1), 0], rstd[:, bass.ds(nt, 1)],
                                                   ALU.subtract, ALU.mult)
                        last.then_inc(xn_ready, 1)
                        dve.wait_ge(xT_hi, n + 2)
                        V.tensor_tensor(xTa[:, 1, :, bass.ds(n * S, S)],
                                        psum[:, 0, :].rearrange("p (c s) -> p c s", c=KT),
                                        xTa[:, 0, :, bass.ds(n * S, S)], ALU.subtract).then_inc(xT_lo, 1)
                        dve.wait_ge(sg_ready, n + 2)
                        link(V.tensor_tensor(sc[:, :, :], sg[:, :, :], e_bias[:, :].unsqueeze(1)
                                             .broadcast_to([P, TT, E1]), ALU.add))
                        four = sc[:, :, :].rearrange("p t (g h r) -> p (t g) h r", h=2, r=2)
                        V.tensor_tensor(hi2[:, :, :], four[:, :, :, 0], four[:, :, :, 1], ALU.max)
                        link(V.tensor_tensor(lo2[:, :, :], four[:, :, :, 0], four[:, :, :, 1], ALU.min))
                        V.tensor_tensor(g1[:, :], hi2[:, :, 0], hi2[:, :, 1], ALU.max)
                        V.tensor_tensor(g2[:, :], hi2[:, :, 0], hi2[:, :, 1], ALU.min)
                        link(V.tensor_tensor(g3[:, :], lo2[:, :, 0], lo2[:, :, 1], ALU.max))
                        link(V.tensor_tensor(g2[:, :], g2[:, :], g3[:, :], ALU.max))
                        link(V.tensor_tensor(g1[:, :], g1[:, :], g2[:, :], ALU.add))
                        gs = g1[:, :].rearrange("p (t g) -> p t g", g=NG)
                        other = gs.unsqueeze(2).broadcast_to([P, TT, NG, NG])
                        own = gs.unsqueeze(3).broadcast_to([P, TT, NG, NG])
                        V.tensor_tensor(gt[:, :, :, :], other, own, ALU.is_gt)
                        link(V.tensor_tensor(eq[:, :, :, :], other, own, ALU.is_equal))
                        link(V.tensor_tensor(eq[:, :, :, :], eq[:, :, :, :],
                                             less[:, :, :].unsqueeze(1).broadcast_to([P, TT, NG, NG]), ALU.mult))
                        link(V.tensor_tensor(gt[:, :, :, :], gt[:, :, :, :], eq[:, :, :, :], ALU.add))
                        link(V.tensor_reduce(rank[:, :, :], gt[:, :, :, :], AX.X, ALU.add))
                        link(V.tensor_scalar(rank[:, :, :], rank[:, :, :], 1.5, None, ALU.is_lt))
                        link(V.tensor_tensor(sc[:, :, :].rearrange("p t (g h) -> p t g h", g=NG),
                                             sc[:, :, :].rearrange("p t (g h) -> p t g h", g=NG),
                                             rank[:, :, :].unsqueeze(3).broadcast_to([P, TT, NG, EG]), ALU.mult))
                        link(V.tensor_scalar(sc[:, :, :], sc[:, :, :], 0.0, None, ALU.add))
                        V.max(top[:, 0, :], sc[:, 0, :])
                        link(V.max(top[:, 1, :], sc[:, 1, :]))
                        V.max_index(ti[:, 0, :], top[:, 0, :], sc[:, 0, :])
                        link(V.max_index(ti[:, 1, :], top[:, 1, :], sc[:, 1, :]))
                        link(V.tensor_copy(tf[:, :, :], ti[:, :, 0:K1]))
                        link(V.tensor_tensor(oh[:, :, :, :],
                                             iota[:, :].unsqueeze(1).unsqueeze(1).broadcast_to([P, TT, K1, E1]),
                                             tf[:, :, :].unsqueeze(3).broadcast_to([P, TT, K1, E1]), ALU.is_equal))
                        link(V.tensor_reduce(sel[:, :, :], oh[:, :, :, :].rearrange("p t k e -> p t e k"), AX.X, ALU.add))
                        link(V.tensor_tensor(sel[:, :, :], sel[:, :, :], sg[:, :, :], ALU.mult))
                        link(V.tensor_reduce(den[:, :], sel[:, :, :], AX.X, ALU.add))
                        link(V.tensor_scalar(den[:, :], den[:, :], 1e-20, None, ALU.add))
                        link(V.reciprocal(den[:, :], den[:, :]))
                        assert step[0] == CHN, step
                        V.tensor_tensor(sel[:, :, :], sel[:, :, :], den[:, :].unsqueeze(2).broadcast_to([P, TT, E1]),
                                        ALU.mult).then_inc(ew_chain, 1)
                        hold(dve, ew_chain, n + 1)
                        V.tensor_scalar(ew[:, bass.ds(n * TT, TT), 0:E1], sel[:, :, :], SCALE, gate[:, 3:4],
                                        ALU.mult, ALU.mult)
        r.close()

        f = ExitStack()

        def fb(name, shape, dt):
            return f.enter_context(nc.sbuf_tensor("m1_" + name, shape, dt))

        hsb = fb("silu", [P, 2, CH], F32)
        hp = fb("hidden", [P, 2, CH], F32)
        hT = fb("hiddenT", [P, 2, 2, CH], F16)
        h_done = sem("m1f_h_done")
        s_done = sem("m1f_silu")
        g_done = sem("m1f_gated")
        hh = sem("m1f_hidden_hi")
        hl = sem("m1f_hidden_lo")
        y_done = sem("m1f_y_done")
        y_add = sem("m1f_y_added")
        with nc.Block() as block:

            @block.sync
            def _(sp):
                for counter, number in ((h_done, 2), (s_done, 2), (g_done, 2), (hh, 2), (hl, 2), (y_done, 2),
                                        (y_add, 2 * CT)):
                    sp.sem_inc(counter, number)

        def steps(eng, first, both, last):
            with eng.Fori(0, NC) as c:
                first(c, c * NE)
                with eng.Fori(0, NE // 2 - 1) as j:
                    for u in range(2):
                        both(c, j * 2 + u, u, c * NE + j * 2 + u)
                last(c, c * NE + NE - 2)

        with nc.Block() as block:

            @block.tensor
            def _(pe):
                mm = nc.tensor.matmul

                def wt(half, e, m):
                    return wh[:, half, bass.ds(e, 1), m * P:(m + 1) * P].rearrange("p a n -> p (a n)")

                def hidden(c, e, u, n):
                    pe.wait_ge(g_done, n + 1)
                    for m in range(2):
                        k = 0
                        for d_ in range(KT):
                            for ws_, xs_ in ((0, 0), (0, 1), (1, 0)):
                                last = mm(psum[:, 2 * u + m, :], wt(ws_, e, m * KT + d_),
                                          xTa[:, xs_, d_, bass.ds(c * CH, CH)], start=k == 0, stop=k == 5)
                                k += 1
                    last.then_inc(h_done, 1)

                def down(e, u, n):
                    pe.wait_ge(hl, n + 3)
                    pe.wait_ge(y_add, (n + 1) * CT)
                    for t in range(CT):
                        k = 0
                        for hs_, ws_ in ((0, 0), (0, 1), (1, 0)):
                            w2 = wh[:, ws_, bass.ds(e, 1), 2 * KT * P:WE].rearrange("p a n -> p (a n)")
                            last = mm(psum[:, 4 + 2 * u + t // 2, (t % 2) * D:(t % 2 + 1) * D],
                                      hT[:, u, hs_, t * P:(t + 1) * P], w2, start=k == 0, stop=k == 2)
                            k += 1
                    last.then_inc(y_done, 1)

                def both(c, e, u, n):
                    hidden(c, e + 1, 1 - u, n + 1)
                    down(e, u, n)

                def last_(c, n):
                    hidden(c, NE - 1, 1, n + 1)
                    down(NE - 2, 0, n)
                    down(NE - 1, 1, n + 1)

                steps(pe, lambda c, n: hidden(c, 0, 0, n), both, last_)

            @block.scalar
            def _(act):
                A = nc.scalar.activation

                def silu(u, n):
                    act.wait_ge(h_done, n + 3)
                    act.wait_ge(g_done, n + 1)
                    A(hsb[:, u, :], psum[:, 2 * u, :], ACT.Silu).then_inc(s_done, 1)

                def upper(u, n):
                    act.wait_ge(g_done, n + 3)
                    act.wait_ge(y_done, n + 1)
                    A(hT[:, u, 0, :], hp[:, u, :], ACT.Copy).then_inc(hh, 1)

                def both(c, e, u, n):
                    silu(1 - u, n + 1)
                    upper(u, n)

                def last_(c, n):
                    silu(1, n + 1)
                    upper(0, n)
                    upper(1, n + 1)

                steps(act, lambda c, n: silu(0, n), both, last_)

            @block.vector
            def _(dve):
                V = nc.vector

                def gated(u, n):
                    dve.wait_ge(s_done, n + 3)
                    dve.wait_ge(hl, n + 1)
                    V.tensor_tensor(hp[:, u, :], psum[:, 2 * u + 1, :], hsb[:, u, :], ALU.mult).then_inc(g_done, 1)

                def lower(u, n):
                    dve.wait_ge(hh, n + 3)
                    V.tensor_tensor(hT[:, u, 1, :], hp[:, u, :], hT[:, u, 0, :], ALU.subtract).then_inc(hl, 1)

                def add(c, e, u, n):
                    dve.wait_ge(y_done, n + 3)
                    for t in range(CT):
                        dve.wait_ge(y_add, (n + 1) * CT + t + 1)
                        xt = x[:, bass.ds(c * CT + t, 1), :].rearrange("p a d -> p (a d)")
                        V.scalar_tensor_tensor(xt, psum[:, 4 + 2 * u + t // 2, (t % 2) * D:(t % 2 + 1) * D],
                                               ew[:, bass.ds(c * CT + t, 1), bass.ds(e, 1)].rearrange("p a b -> p (a b)"),
                                               xt, ALU.mult, ALU.add).then_inc(y_add, 1)

                def both(c, e, u, n):
                    gated(1 - u, n + 1)
                    lower(u, n)
                    add(c, e, u, n)

                def last_(c, n):
                    gated(1, n + 1)
                    lower(0, n)
                    add(c, NE - 2, 0, n)
                    lower(1, n + 1)
                    add(c, NE - 1, 1, n + 1)

                steps(dve, lambda c, n: gated(0, n), both, last_)
        f.close()
        stack.close()

    layernorm_scale("n0")
    attention(0)
    layernorm_scale("n1")
    moe0()
    layernorm_scale("n2")
    attention(1)
    layernorm_scale("n3")
    moe1()
    stored = sem("stored")
    with nc.Block() as block:

        @block.sync
        def _(sp):
            for c in range(4):
                sp.dma_start(out_dram[:, c * 8:(c + 1) * 8, :], x[:, c * 8:(c + 1) * 8, :]).then_inc(stored, 16)
            sp.wait_ge(stored, 64)


def _slots(w):
    w = w.reshape(KT, P, G, GH, 1, DH)
    w = np.broadcast_to(w, (KT, P, G, GH, SLOT // DH, DH))
    return np.ascontiguousarray(w.reshape(KT, P, G * P).transpose(1, 0, 2))


def _rows(w):
    return np.ascontiguousarray(w.reshape(-1, P, *w.shape[1:]).swapaxes(0, 1))


def _constants():
    c = {"ident": np.eye(P, dtype=np.float32)}
    r = np.arange(P) % SLOT
    c["hi_rows"] = np.stack([-(r >= DH).astype(np.float32), (r < DH).astype(np.float32)], 1)
    exact = -math.sqrt(DH) * math.log(2.0)
    soft = np.float16(exact)
    rest = np.float16(float(soft) - exact)
    a_, b_ = np.arange(P)[:, None], np.arange(P)[None, :]
    masks = np.zeros((2, P, 4, P), np.float16)
    masks[0, :, 0] = np.where(a_ > b_, soft, rest)
    off = np.float16(-60000.0)
    masks[1, :, 0] = np.where(a_ > b_, off, 0)
    masks[1, :, 1] = np.where(a_ < b_, off, 0)
    masks[1, :, 2] = masks[1, :, 0].T
    masks[1, :, 3] = masks[1, :, 1].T
    k2 = np.zeros((2, GH, SLOT, GH, G, S), np.float16)
    mrows = np.zeros((2, P, TT, G, GH, SLOT), np.float32)
    for j in range(GH):
        k2[:, j, DH, j] = 0.5
        k2[0, j, DH + 1, j, :, P:] = soft
        k2[0, j, DH + 2, j, :, :P] = rest
    mrows[0, :, 0, :, :, DH + 1] = 1.0
    mrows[0, :, 1, :, :, DH + 2] = 1.0
    for L in range(2):
        c[f"L{L}_masks"] = masks[L]
        c[f"L{L}_k2rows"] = k2[L].reshape(P, GH, G, S)
        c[f"L{L}_mrows"] = mrows[L].reshape(P, TT, G, P)
    half = DH // 2
    inv = np.float32(1.0) / np.float32(10000.0) ** (np.arange(half, dtype=np.float32) / np.float32(half))
    ang = np.arange(S, dtype=np.float32)[:, None] * inv[None, :]
    c["iota"] = np.broadcast_to(np.arange(16, dtype=np.float32), (P, 16))
    c["tri"] = np.stack([np.triu(np.ones((P, P))), np.ones((P, P))], 1).astype(np.float16)
    c["less"] = np.broadcast_to((np.arange(4)[None, :] < np.arange(4)[:, None]).astype(np.float32), (P, 4, 4))
    row = np.arange(P) % DH
    c["cos"] = np.cos(ang).astype(np.float32).T[row % half]
    c["sin"] = (np.where(row < half, -1, 1)[:, None] * np.sin(ang).T[row % half]).astype(np.float32)
    return {k: np.ascontiguousarray(v) for k, v in c.items()}


def _layout(inputs):
    i = {k: np.asarray(v) for k, v in inputs.items()}
    n = {"x": i["x"], "ctx": i["ctx_1024"]}
    gates = np.stack([i["g_xattn"][0], i["g_ffn"][0], i["g_xattn"][1], i["g_ffn"][1]])
    n["gates"] = np.ascontiguousarray(np.broadcast_to(gates[None, :], (P, 4)))
    for L in range(2):
        w = {k: i[f"L{L}_xattn_{k}"] for k in ("Wq", "Wk", "Wv", "Wo", "bq", "bk", "bv", "bo")}
        if L:
            w |= {k: w[k].T for k in ("Wq", "Wk", "Wv", "Wo")}
        n[f"L{L}_wq"], n[f"L{L}_wk"] = _slots(w["Wq"]), _slots(w["Wk"])
        n[f"L{L}_wv"], n[f"L{L}_wo"] = _rows(w["Wv"]), _rows(w["Wo"])
        for k in ("bq", "bk"):
            dup = np.broadcast_to(w[k].reshape(G, GH, 1, DH), (G, GH, SLOT // DH, DH))
            n[f"L{L}_{k}"] = np.ascontiguousarray(dup.reshape(G, P).T)
        n[f"L{L}_bv"] = np.ascontiguousarray(w["bv"].reshape(KT, P).T)
        n[f"L{L}_bo"] = np.ascontiguousarray(w["bo"].reshape(1, D))
    n["L0_router"] = _rows(i["L0_ffn_gate_w"].T)
    for k in ("w1", "w3", "w2"):
        w = i[f"L0_ffn_{k}"]
        n[f"L0_{k}"] = np.ascontiguousarray(w.reshape(w.shape[0], -1, P, w.shape[2]).transpose(0, 2, 1, 3)
                                            .reshape(w.shape[0], P, -1))
    n["L1_router"] = _rows(i["L1_ffn_router_weight"].T)
    n["L1_e_bias"] = np.ascontiguousarray(np.broadcast_to(i["L1_ffn_e_bias"][None, :], (P, 16)))
    up = [np.concatenate([i[f"L1_ffn_{k}_w"], i[f"L1_ffn_sh_{k}_w"].reshape(2, P, D)]) for k in ("gate", "up")]
    down = np.concatenate([i["L1_ffn_down_w"], i["L1_ffn_sh_down_w"].reshape(D, 2, P).transpose(1, 0, 2)])
    up = [w.reshape(-1, P, KT, P).transpose(3, 0, 2, 1).reshape(P, -1, KT * P) for w in up]
    n["L1_experts"] = np.ascontiguousarray(np.concatenate(up + [down.transpose(2, 0, 1)], axis=2))
    return n | _constants()


def kernel(**inputs):
    import concourse.bacc as _bacc
    from concourse.bass_utils import run_bass_kernel_spmd as _run

    arrays = _layout(inputs)
    nc = _bacc.Bacc("TRN2", target_bir_lowering=False, num_devices=1)
    args = {k: nc.dram_tensor(f"in_{k}", v.shape, mybir.dt.from_np(v.dtype), kind="ExternalInput").ap()
            for k, v in arrays.items()}
    out = nc.dram_tensor("out_x", (B, S, D), F32, kind="ExternalOutput").ap()
    flamingo_kernel(nc, args, out)
    r = _run(nc, [{f"in_{k}": v for k, v in arrays.items()}], core_ids=[0])
    return r.results[0]["out_x"]
```

```python
import math
from contextlib import ExitStack

import numpy as np

import concourse.bass as bass
from concourse import mybir

F32 = mybir.dt.float32
F16 = mybir.dt.float16
U32 = mybir.dt.uint32
ACT = mybir.ActivationFunctionType
ALU = mybir.AluOpType
AX = mybir.AxisListType

P = 128
D = 256
KT = D // P
B, S = 16, 256
TT = S // P
NT = B * TT
H, DH = 16, 16
SLOT = 32
GH = P // SLOT
G = H // GH
EPS = 1e-5


def flamingo_kernel(nc, a, out):

    def sb(name, shape, dt):
        return nc.alloc_sbuf_tensor(name, shape, dt)

    sem = nc.alloc_semaphore
    waited = sem("waited")

    def hold(eng, counter, value):
        eng.wait_ge(counter, value)
        eng.sem_inc(waited, 1)

    x = sb("x_res", [P, NT, D], F32)
    mv = sb("mean_var", [P, NT, 2], F32)
    rstd = sb("rstd", [P, NT], F32)
    nwt = sb("newton", [P, NT], F32)
    ident32 = sb("ident32", [P, P], F32)
    ident16 = sb("ident16", [P, P], F16)
    gate = sb("gate", [P, 4], F32)
    graw = sb("gate_raw", [P, 4], F32)
    stats = sb("bn_stats", [P, TT, 6], F32)
    agg = sb("bn_aggregate", [P, TT, 2], F32)
    psum = nc.alloc_psum_tensor("ps", [P, 8, 512], F32)

    x_dram = a["x"].rearrange("b (t p) d -> p (b t) d", p=P)
    ctx_dram = a["ctx"].rearrange("b (t p) d -> b p t d", p=P)
    out_dram = out.rearrange("b (t p) d -> p (b t) d", p=P)

    def token_stats(dve, i, chain):
        for t in range(TT):
            nc.vector.bn_stats(stats[:, t, :], x[:, bass.ds(i * TT + t, 1), :].rearrange("p a d -> p (a d)"))\
              .then_inc(chain, 1)
        hold(dve, chain, (i + 1) * 5 + 2)
        for t in range(TT):
            nc.vector.bn_aggr(agg[:, t, :], stats[:, t, :]).then_inc(chain, 1)
        hold(dve, chain, (i + 1) * 5 + 4)
        nc.vector.tensor_copy(mv[:, bass.ds(i * TT, TT), :], agg[:, :, :]).then_inc(chain, 1)

    x_loaded = sem("x_loaded")
    consts_loaded = sem("consts_loaded")
    setup_chain = sem("setup_chain")
    with nc.Block() as block:

        @block.sync
        def _(sp):
            sp.dma_start(graw[:, :], a["gates"]).then_inc(consts_loaded, 16)
            sp.dma_start(ident32[:, :], a["ident"]).then_inc(consts_loaded, 16)
            for c in range(4):
                sp.dma_start(x[:, c * 8:(c + 1) * 8, :], x_dram[:, c * 8:(c + 1) * 8, :]).then_inc(x_loaded, 16)

        @block.scalar
        def _(act):
            act.wait_ge(consts_loaded, 32)
            nc.scalar.activation(gate[:, :], graw[:, :], ACT.Tanh)
            nc.scalar.activation(ident16[:, :], ident32[:, :], ACT.Copy)

        @block.vector
        def _(dve):
            dve.wait_ge(x_loaded, 64)
            dve.sem_inc(setup_chain, 5)
            with dve.Fori(0, B) as i:
                token_stats(dve, i, setup_chain)

    def layernorm_scale(tag):
        ve = sem(f"{tag}_var_eps")
        sq = sem(f"{tag}_sqrt")
        ch = sem(f"{tag}_rstd_chain")
        with nc.Block() as block:

            @block.vector
            def _(dve):
                nc.vector.tensor_scalar(mv[:, :, 1], mv[:, :, 1], EPS, None, ALU.add).then_inc(ve, 1)
                dve.wait_ge(sq, 1)
                n = 0
                for step in (
                    lambda: nc.vector.reciprocal(rstd[:, :], rstd[:, :]),
                    lambda: nc.vector.tensor_tensor(nwt[:, :], rstd[:, :], rstd[:, :], ALU.mult),
                    lambda: nc.vector.tensor_tensor(nwt[:, :], nwt[:, :], mv[:, :, 1], ALU.mult),
                    lambda: nc.vector.tensor_scalar(nwt[:, :], nwt[:, :], -0.5, 1.5, ALU.mult, ALU.add),
                    lambda: nc.vector.tensor_tensor(rstd[:, :], rstd[:, :], nwt[:, :], ALU.mult),
                ):
                    step().then_inc(ch, 1)
                    n += 1
                    dve.wait_ge(ch, n)

            @block.scalar
            def _(act):
                act.wait_ge(ve, 1)
                nc.scalar.activation(rstd[:, :], mv[:, :, 1], ACT.Sqrt).then_inc(sq, 1)

    def attention_buffers(sb):
        return dict(
            xin=sb("ctx_in", [P, TT, D], F32),
            xn=sb("xn", [P, TT, D], F32),
            xT=sb("xT", [P, 2, KT, S], F16),
            cT=sb("cT", [P, 2, KT, S], F16),
            wq=sb("wq", [P, 2, KT, G, P], F16),
            wk=sb("wk", [P, 2, KT, G, P], F16),
            wv=sb("wv", [P, 2, KT, D], F16),
            wo=sb("wo", [P, 2, KT, D], F16),
            wld=sb("w_load", [P, KT, G * P], F32),
            bq=sb("bq", [P, G], F32),
            bk=sb("bk", [P, G], F32),
            bv=sb("bv", [P, KT], F32),
            bo32=sb("bo32", [1, D], F32),
            bo=sb("bo", [1, 2, D], F16),
            ones=sb("ones_row", [1, P], F16),
            qf=sb("qf", [P, G, S], F32),
            kf=sb("kf", [P, G, S], F32),
            rot=sb("rotated", [P, G, S], F32),
            qh=sb("qh", [P, 2, G, S], F16),
            q1=sb("q1", [P, 2, G, S], F16),
            q2=sb("q2", [P, G, S], F16),
            kh=sb("kh", [P, G, S], F16),
            kl=sb("kl", [P, G, S], F16),
            k1=sb("k1", [P, 2, GH, G, S], F16),
            k2=sb("k2", [P, 2, GH, G, S], F16),
            v=sb("v_ext", [P, 2, TT, H, SLOT], F32),
            m=sb("neg_max", [P, TT, G, P], F32),
            pr=sb("probs", [P, 2, TT, GH, S], F32),
            o=sb("o_slots", [P, G, S], F32),
            on=sb("o_norm", [P, TT, D], F32),
            rd=sb("recip_den", [P, TT, H], F32),
            oT=sb("oT", [P, 2, KT, S], F16),
            hi_rows=sb("hi_rows", [P, 2], F32),
            cos=sb("rope_cos", [P, S], F32),
            sin=sb("rope_sin", [P, S], F32),
            masks=sb("masks16", [P, 4, P], F16),
        )

    def attention(L):
        stack = ExitStack()
        w = attention_buffers(lambda name, shape, dt: stack.enter_context(
            nc.sbuf_tensor(f"a{L}_{name}", shape, dt)))
        causal_band = L == 1
        n = f"A{L}_"
        def pairs(qt):
            return [qt - 1, qt] if causal_band and qt else [qt] if causal_band else list(range(TT))

        wl = sem(n + "weights_loaded")
        ws = sem(n + "weights_split")
        hi_done = sem(n + "weight_hi")
        jobs = [("wq", G * P), ("wk", G * P), ("wv", D), ("wo", D)]
        flat = {k: w[k][:, :, :, :, :].rearrange("p s k g m -> p s k (g m)") for k in ("wq", "wk")}
        flat |= {k: w[k][:, :, :, :] for k in ("wv", "wo")}
        small = [("bq", w["bq"][:, :]), ("bk", w["bk"][:, :]), ("bv", w["bv"][:, :]), ("bo", w["bo32"][0:1, :])]
        with nc.Block() as block:

            @block.sync
            def _(sp):
                for i, (k, dst) in enumerate(small):
                    sp.dma_start(dst, a[f"L{L}_{k}"]).then_inc(wl, 16)
                sp.dma_start(w["masks"][:, :, :], a[f"L{L}_masks"]).then_inc(wl, 16)
                sp.dma_start(w["m"][:, :, :, :], a[f"L{L}_mrows"]).then_inc(wl, 16)
                sp.dma_start(w["hi_rows"][:, :], a["hi_rows"]).then_inc(wl, 16)
                for u in range(2):
                    sp.dma_start(w["k2"][:, u, :, :, :], a[f"L{L}_k2rows"]).then_inc(wl, 16)
                if causal_band:
                    sp.dma_start(w["cos"][:, :], a["cos"]).then_inc(wl, 16)
                    sp.dma_start(w["sin"][:, :], a["sin"]).then_inc(wl, 16)
                base = 16 * (len(small) + 5 + 2 * causal_band)
                for i, (k, width) in enumerate(jobs):
                    sp.wait_ge(wl, base + 16 * i)
                    if i:
                        sp.wait_ge(ws, i)
                    sp.dma_start(w["wld"][:, :, 0:width], a[f"L{L}_{k}"]).then_inc(wl, 16)

            @block.scalar
            def _(act):
                base = 16 * (len(small) + 5 + 2 * causal_band)
                for i, (k, width) in enumerate(jobs):
                    act.wait_ge(wl, base + 16 * (i + 1))
                    nc.scalar.activation(flat[k][:, 0, :, :], w["wld"][:, :, 0:width], ACT.Copy).then_inc(hi_done, 1)
                nc.scalar.activation(w["bo"][0:1, 0, :], w["bo32"][0:1, :], ACT.Copy).then_inc(hi_done, 1)

            @block.gpsimd
            def _(pool):
                pool.memset(w["k1"][:, :, :, :, :], 0.0)
                pool.memset(w["v"][:, :, :, :, DH:SLOT], 1.0)
                pool.memset(w["ones"][0:1, :], 1.0)

            @block.vector
            def _(dve):
                for i, (k, width) in enumerate(jobs):
                    dve.wait_ge(hi_done, i + 1)
                    nc.vector.tensor_tensor(flat[k][:, 1, :, :], w["wld"][:, :, 0:width], flat[k][:, 0, :, :],
                                            ALU.subtract).then_inc(ws, 1)
                dve.wait_ge(hi_done, len(jobs) + 1)
                nc.vector.tensor_tensor(w["bo"][0:1, 1, :], w["bo32"][0:1, :], w["bo"][0:1, 0, :], ALU.subtract)

        counts = {}

        def counter(name, number):
            s_ = sem(n + name)
            counts[name] = (s_, number)
            return s_

        ctx_loaded = counter("ctx_loaded", 16)
        xn_ready = counter("xn_ready", 1)
        tr_done = counter("transposed", 2)
        tr_hi = counter("transposed_hi", 2)
        tr_lo = counter("transposed_lo", 2)
        proj_done = counter("projected", 5)
        proj_out = counter("projection_taken", 5)
        f_ready = counter("qk_rotated", 2)
        rope = counter("rope_steps", 6)
        qk_hi = counter("qk_hi", 2)
        q1_ready = counter("q1_ready", 1)
        kl_ready = counter("k_lo_ready", 1)
        k1_ready = counter("k1_placed", 16 * GH)
        k2_ready = counter("k2_placed", 16 * GH)
        mx_scores = counter("max_scores", 8)
        mx_taken = counter("maxima_taken", 8)
        m_done = counter("maxima_transposed", 2)
        q2_ready = counter("q2_ready", 2)
        sc_done = counter("scores_done", 8)
        ex_done = counter("exp_done", 8)
        av_done = counter("av_done", 4)
        o_out = counter("o_taken", 4)
        oT_done = counter("o_natural", 2)
        rd_ready = counter("recip_ready", 2)
        on_ready = counter("o_normalised", 2)
        on_T = counter("o_norm_transposed", 1)
        oh_ready = counter("oT_hi", 1)
        ol_ready = counter("oT_lo", 1)
        y_done = counter("y_done", 1)
        x_new = counter("x_updated", 1)
        st_chain = counter("stats_chain", 5)
        with nc.Block() as block:

            @block.sync
            def _(sp):
                for s_, number in counts.values():
                    sp.sem_inc(s_, number if s_ is st_chain else 2 * number)

        SC = [psum[:, 0:2, :].rearrange("p b n -> p (b n)"), psum[:, 2:4, :].rearrange("p b n -> p (b n)")]

        def sequences(eng, ahead, body):
            ahead(0, 0)
            with eng.Fori(0, B // 2 - 1) as i:
                for u in range(2):
                    body(i * 2 + u, u, True)
            body(B - 2, 0, True)
            body(B - 1, 1, False)

        with nc.Block() as block:

            @block.sync
            def _(sp):
                def stage(m, u):
                    hold(sp, tr_done, (m + 2) * 2)
                    sp.dma_start(w["xin"][:, :, :], ctx_dram[m, :, :, :]).then_inc(ctx_loaded, 16)
                    hold(sp, qk_hi, (m + 2) * 2 + 1)
                    hold(sp, sc_done, (m + 1) * 8)
                    for j in range(GH):
                        sp.dma_start(w["k1"][j * SLOT:(j + 1) * SLOT, u, j, :, :],
                                     w["kh"][j * SLOT:(j + 1) * SLOT, :, :]).then_inc(k1_ready, 16)
                    hold(sp, kl_ready, m + 3)
                    for j in range(GH):
                        sp.dma_start(w["k2"][j * SLOT:j * SLOT + DH, u, j, :, :],
                                     w["kl"][j * SLOT:j * SLOT + DH, :, :]).then_inc(k2_ready, 16)

                with sp.Fori(0, B // 2) as i:
                    for u in range(2):
                        stage(i * 2 + u, u)

            @block.tensor
            def _(pe):
                mm = nc.tensor.matmul

                def transposes(m):
                    for n_, (src, ready) in enumerate((("xn", None), ("xin", None))):
                        if n_ == 0:
                            pe.wait_ge(xn_ready, m + 3)
                            pe.wait_ge(proj_out, (m + 2) * 5)
                        else:
                            pe.wait_ge(ctx_loaded, (m + 3) * 16)
                        for c in range(KT):
                            for t in range(TT):
                                last = nc.tensor.transpose(psum[:, 4 + n_, c * S + t * P:c * S + (t + 1) * P],
                                                           w[src][:, t, c * P:(c + 1) * P], ident32[:, :])
                        last.then_inc(tr_done, 1)

                def project(m, n_):
                    wt, src = ("wk", "cT") if n_ < 2 else ("wq", "xT")
                    if n_ < 2:
                        pe.wait_ge(tr_lo, (m + 2) * 2 + 2)
                    else:
                        pe.wait_ge(proj_out, (m + 2) * 5 + n_ - 1)
                    for g in (n_ % 2 * 2, n_ % 2 * 2 + 1):
                        o_ = psum[:, 4 + n_ % 2, (g % 2) * S:(g % 2 + 1) * S]
                        k = 0
                        for c in range(KT):
                            for ws_, xs_ in ((0, 0), (0, 1), (1, 0)):
                                last = mm(o_, w[wt][:, ws_, c, g, :], w[src][:, xs_, c, :], start=k == 0, stop=k == 5)
                                k += 1
                    last.then_inc(proj_done, 1)

                def project_v(m):
                    pe.wait_ge(proj_out, (m + 2) * 5 + 3)
                    for t in range(TT):
                        k = 0
                        for c in range(KT):
                            for xs_, ws_ in ((0, 0), (0, 1), (1, 0)):
                                last = mm(psum[:, 4, t * D:(t + 1) * D], w["cT"][:, xs_, c, t * P:(t + 1) * P],
                                          w["wv"][:, ws_, c, :], start=k == 0, stop=k == 5)
                                k += 1
                    last.then_inc(proj_done, 1)

                def ahead(m, u):
                    transposes(m)
                    for n_ in range(4):
                        project(m, n_)
                    project_v(m)

                def max_scores(m, u, s_):
                    t, g = s_ // G, s_ % G
                    if s_ == 0:
                        pe.wait_ge(k1_ready, (m + 3) * (16 * GH))
                        pe.wait_ge(qk_hi, (m + 3) * 2)
                    if s_ == 1:
                        pe.wait_ge(x_new, m + 2)
                    if s_ >= 2:
                        pe.wait_ge(mx_taken, (m + 2) * 8 + s_ - 1)
                    cols = pairs(t)
                    c0, c1 = cols[0] * P, (cols[-1] + 1) * P
                    for j in range(GH):
                        last = mm(SC[s_ % 2][:, j * S + c0:j * S + c1], w["qh"][:, u, g, t * P:(t + 1) * P],
                                  w["k1"][:, u, j, g, c0:c1], start=True, stop=not causal_band)
                        if causal_band:
                            for e, kt in enumerate(cols):
                                last = mm(SC[s_ % 2][:, j * S + kt * P:j * S + (kt + 1) * P], ident16[:, :],
                                          w["masks"][:, 2 if kt == t else 3, :], start=False, stop=e == len(cols) - 1)
                    last.then_inc(mx_scores, 1)

                def max_transposes(m):
                    pe.wait_ge(mx_taken, (m + 3) * 8)
                    pe.wait_ge(o_out, (m + 2) * 4)
                    for half in range(2):
                        for g in (2 * half, 2 * half + 1):
                            for t in range(TT):
                                last = nc.tensor.transpose(
                                    psum[:, 6 + half, (g % 2) * S + t * P:(g % 2) * S + (t + 1) * P],
                                    w["m"][:, t, g, :], ident32[:, :])
                        last.then_inc(m_done, 1)

                def scores(m, u, g):
                    pe.wait_ge(q2_ready, (m + 2) * 2 + g // 2 + 1)
                    for kt in range(TT):
                        s_ = g * TT + kt
                        if s_ >= 2:
                            pe.wait_ge(ex_done, (m + 2) * 8 + s_ - 1)
                        qs = [t for t in range(TT) if kt in pairs(t)]
                        a0, a1 = qs[0] * P, (qs[-1] + 1) * P
                        for j in range(GH):
                            at = SC[s_ % 2][:, j * S + a0:j * S + a1]
                            ks = slice(kt * P, (kt + 1) * P)
                            mm(at, w["k1"][:, u, j, g, ks], w["q1"][:, u, g, a0:a1], start=True, stop=False)
                            for t in qs:
                                if t == kt or causal_band:
                                    mm(SC[s_ % 2][:, j * S + t * P:j * S + (t + 1) * P], ident16[:, :],
                                       w["masks"][:, 0 if t == kt else 1, :], start=False, stop=False)
                            last = mm(at, w["k2"][:, u, j, g, ks], w["q2"][:, g, a0:a1], start=False, stop=True)
                        last.then_inc(sc_done, 1)

                def values(m, u, g):
                    pe.wait_ge(ex_done, (m + 2) * 8 + g * 2 + 2)
                    if g == 0:
                        pe.wait_ge(q2_ready, (m + 3) * 2)
                        pe.wait_ge(proj_out, (m + 3) * 5)
                    if g >= 2:
                        pe.wait_ge(o_out, (m + 2) * 4 + g - 1)
                    for kt in range(TT):
                        q0 = kt * P if causal_band else 0
                        for j in range(GH):
                            last = mm(psum[j * SLOT:(j + 1) * SLOT, 6 + g % 2, q0:S],
                                      w["v"][:, u, kt, g * GH + j, :], w["pr"][:, g % 2, kt, j, q0:S],
                                      start=kt == 0, stop=kt == TT - 1, tile_position=(0, j * SLOT))
                    last.then_inc(av_done, 1)

                def body(m, u, more):
                    for s_ in range(8):
                        max_scores(m, u, s_)
                        if more and s_ == 1:
                            transposes(m + 1)
                        if more and s_ in (4, 6):
                            project(m + 1, s_ // 2 - 2)
                    if more:
                        project(m + 1, 2)
                    max_transposes(m)
                    if more:
                        project(m + 1, 3)
                    pe.wait_ge(q1_ready, m + 3)
                    pe.wait_ge(k2_ready, (m + 3) * (16 * GH))
                    for g in range(G):
                        scores(m, u, g)
                        if g:
                            values(m, u, g - 1)
                    values(m, u, G - 1)
                    pe.wait_ge(o_out, (m + 3) * 4)
                    for t in range(TT):
                        for g in range(G):
                            last = nc.tensor.transpose(psum[:, t, g * P:(g + 1) * P],
                                                       w["o"][:, g, t * P:(t + 1) * P], ident32[:, :])
                        last.then_inc(oT_done, 1)
                    if more:
                        project_v(m + 1)
                    pe.wait_ge(on_ready, (m + 3) * 2)
                    for c in range(KT):
                        for t in range(TT):
                            last = nc.tensor.transpose(psum[:, 2, c * S + t * P:c * S + (t + 1) * P],
                                                       w["on"][:, t, c * P:(c + 1) * P], ident32[:, :])
                    last.then_inc(on_T, 1)
                    pe.wait_ge(ol_ready, m + 3)
                    for t in range(TT):
                        y = psum[:, 3, t * D:(t + 1) * D]
                        k = 0
                        for c in range(KT):
                            for xs_, ws_ in ((0, 0), (0, 1), (1, 0)):
                                mm(y, w["oT"][:, xs_, c, t * P:(t + 1) * P], w["wo"][:, ws_, c, :],
                                   start=k == 0, stop=False)
                                k += 1
                        mm(y, w["ones"][0:1, :], w["bo"][0:1, 0, :], start=False, stop=False)
                        last = mm(y, w["ones"][0:1, :], w["bo"][0:1, 1, :], start=False, stop=True)
                    last.then_inc(y_done, 1)

                sequences(pe, ahead, body)

            @block.scalar
            def _(act):
                A = nc.scalar.activation

                def halves(m):
                    for n_, dst in enumerate(("xT", "cT")):
                        act.wait_ge(tr_done, (m + 2) * 2 + n_ + 1)
                        if n_ == 0:
                            act.wait_ge(proj_done, (m + 2) * 5)
                        A(w[dst][:, 0, :, :], psum[:, 4 + n_, :].rearrange("p (c s) -> p c s", c=KT),
                          ACT.Copy).then_inc(tr_hi, 1)

                def take(m, n_):
                    act.wait_ge(proj_done, (m + 2) * 5 + n_ + 1)
                    if n_ == 0:
                        act.wait_ge(kl_ready, m + 2)
                    if n_ == 2:
                        act.wait_ge(q1_ready, m + 2)
                    dst, bias = (w["kf"], w["bk"]) if n_ < 2 else (w["qf"], w["bq"])
                    for g in (n_ % 2 * 2, n_ % 2 * 2 + 1):
                        last = A(dst[:, g, :], psum[:, 4 + n_ % 2, (g % 2) * S:(g % 2 + 1) * S], ACT.Identity,
                                 bias=bias[:, g:g + 1])
                    last.then_inc(proj_out, 1)

                def upper_k(m):
                    if causal_band:
                        act.wait_ge(f_ready, (m + 2) * 2 + 1)
                    else:
                        act.wait_ge(proj_out, (m + 2) * 5 + 2)
                    act.wait_ge(k1_ready, (m + 2) * (16 * GH))
                    act.wait_ge(kl_ready, m + 2)
                    A(w["kh"][:, :, :], w["kf"][:, :, :], ACT.Copy).then_inc(qk_hi, 1)

                def upper_q(m, u):
                    if causal_band:
                        act.wait_ge(f_ready, (m + 3) * 2)
                    else:
                        act.wait_ge(proj_out, (m + 2) * 5 + 4)
                    act.wait_ge(q2_ready, (m + 1) * 2)
                    A(w["qh"][:, u, :, :], w["qf"][:, :, :], ACT.Copy).then_inc(qk_hi, 1)

                def take_v(m, u):
                    act.wait_ge(proj_done, (m + 3) * 5)
                    act.wait_ge(av_done, (m + 1) * 4)
                    A(w["v"][:, u, :, :, 0:DH], psum[:, 4, :].rearrange("p (t h d) -> p t h d", t=TT, h=H),
                      ACT.Copy).then_inc(proj_out, 1)

                def ahead(m, u):
                    halves(m)
                    take(m, 0)
                    take(m, 1)
                    upper_k(m)
                    take(m, 2)
                    take(m, 3)
                    upper_q(m, u)
                    take_v(m, u)

                def exps(m, g):
                    for kt in range(TT):
                        s_ = g * TT + kt
                        act.wait_ge(sc_done, (m + 2) * 8 + s_ + 1)
                        if g >= 2:
                            act.wait_ge(av_done, (m + 2) * 4 + g - 1)
                        else:
                            act.wait_ge(av_done, (m + 2) * 4)
                        a0 = kt * P if causal_band else 0
                        A(w["pr"][:, g % 2, kt, :, a0:S], SC[s_ % 2].rearrange("p (j s) -> p j s", j=GH)[:, :, a0:S],
                          ACT.Exp, scale=1.0 / math.sqrt(DH)).then_inc(ex_done, 1)

                def take_o(m, g):
                    act.wait_ge(av_done, (m + 2) * 4 + g + 1)
                    act.wait_ge(oT_done, (m + 2) * 2)
                    A(w["o"][:, g, :], psum[:, 6 + g % 2, 0:S], ACT.Copy).then_inc(o_out, 1)

                def body(m, u, more):
                    if more:
                        halves(m + 1)
                        take(m + 1, 0)
                        take(m + 1, 1)
                        if not causal_band:
                            upper_k(m + 1)
                        take(m + 1, 2)
                    exps(m, 0)
                    if more:
                        take(m + 1, 3)
                        if not causal_band:
                            upper_q(m + 1, 1 - u)
                    exps(m, 1)
                    take_o(m, 0)
                    if more and causal_band:
                        upper_k(m + 1)
                    exps(m, 2)
                    take_o(m, 1)
                    exps(m, 3)
                    take_o(m, 2)
                    take_o(m, 3)
                    if more and causal_band:
                        upper_q(m + 1, 1 - u)
                    if more:
                        take_v(m + 1, 1 - u)
                    act.wait_ge(on_T, m + 3)
                    for c in range(KT):
                        last = A(w["oT"][:, 0, c, :], psum[:, 2, c * S:(c + 1) * S], ACT.Identity,
                                 bias=w["bv"][:, c:c + 1])
                    last.then_inc(oh_ready, 1)

                sequences(act, ahead, body)

            @block.gpsimd
            def _(pool):
                with pool.Fori(0, B) as m:
                    pool.wait_ge(qk_hi, (m + 2) * 2 + 1)
                    pool.wait_ge(k2_ready, (m + 2) * (16 * GH))
                    pool.tensor_tensor(w["kl"][:, :, :], w["kf"][:, :, :], w["kh"][:, :, :],
                                       ALU.subtract).then_inc(kl_ready, 1)

            @block.vector
            def _(dve):
                V = nc.vector

                def norm(m):
                    dve.wait_ge(tr_done, (m + 2) * 2)
                    for t in range(TT):
                        last = V.tensor_scalar(w["xn"][:, t, :],
                                               x[:, bass.ds(m * TT + t, 1), :].rearrange("p a d -> p (a d)"),
                                               mv[:, bass.ds(m * TT + t, 1), 0], rstd[:, bass.ds(m * TT + t, 1)],
                                               ALU.subtract, ALU.mult)
                    last.then_inc(xn_ready, 1)

                def halves(m):
                    for n_, dst in enumerate(("xT", "cT")):
                        dve.wait_ge(tr_hi, (m + 2) * 2 + n_ + 1)
                        V.tensor_tensor(w[dst][:, 1, :, :], psum[:, 4 + n_, :].rearrange("p (c s) -> p c s", c=KT),
                                        w[dst][:, 0, :, :], ALU.subtract).then_inc(tr_lo, 1)

                def rotate(m, n_):
                    f_ = w[("kf", "qf")[n_]]
                    swap = [(r // DH) * DH + (r % DH + DH // 2) % DH for r in range(SLOT)]
                    hold(dve, proj_out, (m + 2) * 5 + 2 * n_ + 2)
                    hold(dve, f_ready, (m + 2) * 2 + n_)
                    V.stream_shuffle(w["rot"][:, :, :], f_[:, :, :], swap).then_inc(rope, 1)
                    dve.wait_ge(rope, (m + 2) * 6 + n_ * 3 + 1)
                    V.tensor_tensor(w["rot"][:, :, :], w["rot"][:, :, :],
                                    w["sin"][:, :].unsqueeze(1).broadcast_to([P, G, S]), ALU.mult).then_inc(rope, 1)
                    V.tensor_tensor(f_[:, :, :], f_[:, :, :],
                                    w["cos"][:, :].unsqueeze(1).broadcast_to([P, G, S]), ALU.mult).then_inc(rope, 1)
                    dve.wait_ge(rope, (m + 2) * 6 + n_ * 3 + 3)
                    V.tensor_tensor(f_[:, :, :], f_[:, :, :], w["rot"][:, :, :], ALU.add).then_inc(f_ready, 1)

                def mixed_q(m, u):
                    dve.wait_ge(qk_hi, (m + 3) * 2)
                    dve.wait_ge(sc_done, (m + 1) * 8)
                    V.scalar_tensor_tensor(w["q1"][:, u, :, :], w["qh"][:, u, :, :], w["hi_rows"][:, 0:1],
                                           w["qf"][:, :, :], ALU.mult, ALU.add).then_inc(q1_ready, 1)

                def ahead(m, u):
                    norm(m)
                    halves(m)
                    if causal_band:
                        rotate(m, 0)
                        rotate(m, 1)
                    mixed_q(m, u)

                def body(m, u, more):
                    if more:
                        norm(m + 1)
                    for s_ in range(8):
                        t, g = s_ // G, s_ % G
                        if more and s_ == 3:
                            halves(m + 1)
                        dve.wait_ge(mx_scores, (m + 2) * 8 + s_ + 1)
                        cols = pairs(t)
                        src = SC[s_ % 2].rearrange("p (j s) -> p j s", j=GH)[:, :, cols[0] * P:(cols[-1] + 1) * P]
                        V.tensor_reduce(w["m"][:, t, g, DH::SLOT], src, AX.X, ALU.max, negate=True).then_inc(mx_taken, 1)
                    for half in range(2):
                        dve.wait_ge(m_done, (m + 2) * 2 + half + 1)
                        V.scalar_tensor_tensor(w["q2"][:, 2 * half:2 * half + 2, :],
                                               w["qh"][:, u, 2 * half:2 * half + 2, :], w["hi_rows"][:, 1:2],
                                               psum[:, 6 + half, :].rearrange("p (g s) -> p g s", g=2),
                                               ALU.mult, ALU.add).then_inc(q2_ready, 1)
                    if more and causal_band:
                        rotate(m + 1, 0)
                        rotate(m + 1, 1)
                    if more and not causal_band:
                        mixed_q(m + 1, 1 - u)
                    for t in range(TT):
                        dve.wait_ge(oT_done, (m + 2) * 2 + t + 1)
                        heads = psum[:, t, :].rearrange("p (h r) -> p h r", r=SLOT)
                        V.reciprocal(w["rd"][:, t, :], heads[:, :, DH]).then_inc(rd_ready, 1)
                    for t in range(TT):
                        heads = psum[:, t, :].rearrange("p (h r) -> p h r", r=SLOT)
                        dve.wait_ge(rd_ready, (m + 2) * 2 + t + 1)
                        V.tensor_tensor(w["on"][:, t, :].rearrange("p (h d) -> p h d", h=H), heads[:, :, 0:DH],
                                        w["rd"][:, t, :].unsqueeze(2).broadcast_to([P, H, DH]),
                                        ALU.mult).then_inc(on_ready, 1)
                    if more and causal_band:
                        mixed_q(m + 1, 1 - u)
                    dve.wait_ge(oh_ready, m + 3)
                    for c in range(KT):
                        last = V.scalar_tensor_tensor(w["oT"][:, 1, c, :], psum[:, 2, c * S:(c + 1) * S],
                                                      w["bv"][:, c:c + 1], w["oT"][:, 0, c, :],
                                                      ALU.add, ALU.subtract)
                    last.then_inc(ol_ready, 1)
                    dve.wait_ge(y_done, m + 3)
                    for t in range(TT):
                        xt = x[:, bass.ds(m * TT + t, 1), :].rearrange("p a d -> p (a d)")
                        last = V.scalar_tensor_tensor(xt, psum[:, 3, t * D:(t + 1) * D], gate[:, 2 * L:2 * L + 1], xt,
                                                      ALU.mult, ALU.add)
                    last.then_inc(x_new, 1)
                    hold(dve, x_new, m + 3)
                    token_stats(dve, m, st_chain)

                sequences(dve, ahead, body)
        stack.close()

    def moe0():
        E0, F0, CAP = 8, 896, 80
        FT = F0 // P
        ROWS = B * CAP
        CH = 256
        NC = ROWS // CH
        CT = CH // P
        STEPS = E0 * NC
        WP = KT * F0
        disp = nc.dram_tensor("dispatched", (E0 * ROWS, D), F32, kind="Internal").ap()
        eo = nc.dram_tensor("expert_out", (E0 * ROWS, D), F32, kind="Internal").ap()
        stack = ExitStack()

        def sb(name, shape, dt):
            return stack.enter_context(nc.sbuf_tensor("m0_" + name, shape, dt))

        gidx = sb("gather_row", [P, NT, 2], U32)
        gw = sb("gather_weight", [P, NT, 2], F32)

        r = ExitStack()

        def rb(name, shape, dt):
            return r.enter_context(nc.sbuf_tensor("m0_" + name, shape, dt))

        zero = rb("zero", [P, 8, D], F32)
        xn = rb("xn", [P, 2, TT, D], F32)
        xT = rb("xT32", [P, KT, S], F32)
        gate_w = rb("router", [P, KT, E0], F32)
        tri = rb("tri", [P, 2, P], F16)
        iota = rb("iota", [P, E0], F32)
        base = rb("seq_base", [P, 1], F32)
        lg = rb("logits", [P, TT, E0], F32)
        mx = rb("row_max", [P, TT], F32)
        pr = rb("probs", [P, TT, E0], F32)
        rs = rb("row_sum", [P, TT], F32)
        top = rb("top", [P, TT, 8], F32)
        ti = rb("top_index", [P, TT, 8], U32)
        tf = rb("top_index_f", [P, TT, 2], F32)
        oh = rb("one_hot", [P, 2, TT, E0], F32)
        msk = rb("chosen", [P, TT, E0], F16)
        pos = rb("position", [P, TT, E0], F32)
        tmp = rb("picked", [P, 2, 2, TT, E0], F32)
        pk = rb("picked_sum", [P, 2, 2, TT], F32)
        keep = rb("kept", [P, 2, TT], F32)
        row = rb("row", [P, 2, TT], F32)
        far = rb("row_or_far", [P, 2, TT], F32)
        sidx = rb("scatter_row", [P, 2, 2, TT], U32)
        ld = sem("m0_loaded")
        zr = sem("m0_zeroed")
        zset = sem("m0_zero_set")
        with nc.Block() as block:

            @block.sync
            def _(sp):
                sp.dma_start(gate_w[:, :, :], a["L0_router"]).then_inc(ld, 16)
                sp.dma_start(tri[:, :, :], a["tri"]).then_inc(ld, 16)
                sp.dma_start(iota[:, :], a["iota"][:, 0:E0]).then_inc(ld, 16)
                sp.wait_ge(ld, 48)
                sp.wait_ge(zset, 2)
                for c in range(E0 * ROWS // (P * 8)):
                    sp.dma_start(disp[c * P * 8:(c + 1) * P * 8, :].rearrange("(p t) d -> p t d", p=P),
                                 zero[:, :, :]).then_inc(zr, 16)
                sp.wait_ge(zr, 16 * (E0 * ROWS // (P * 8)))

            @block.gpsimd
            def _(pool):
                pool.memset(zero[:, :, :], 0.0).then_inc(zset, 1)
                pool.memset(base[:, :], -1.0).then_inc(zset, 1)

        xn_ready = sem("m0_xn_ready")
        xT_done = sem("m0_xT_done")
        xT_out = sem("m0_xT_out")
        lg_done = sem("m0_logits_done")
        sh_ready = sem("m0_shifted")
        ex_ready = sem("m0_exp")
        m_ready = sem("m0_chosen")
        pos_done = sem("m0_positions")
        idx_ready = sem("m0_rows_ready")
        sent = sem("m0_sent")
        sent_seq = sem("m0_sent_seq")
        ch = sem("m0_chain")
        CHN = 20
        with nc.Block() as block:

            @block.sync
            def _(sp):
                for counter, number in ((xn_ready, 1), (xT_done, 1), (xT_out, 1), (lg_done, 1), (sh_ready, 1),
                                        (ex_ready, 1), (m_ready, 1), (pos_done, 1), (idx_ready, 1), (sent_seq, 2),
                                        (ch, CHN)):
                    sp.sem_inc(counter, number)

        with nc.Block() as block:

            @block.tensor
            def _(pe):
                with pe.Fori(0, B // 2) as i:
                    for u in range(2):
                        n = i * 2 + u
                        pe.wait_ge(xn_ready, n + 2)
                        pe.wait_ge(xT_out, n + 1)
                        for c in range(KT):
                            for t in range(TT):
                                last = nc.tensor.transpose(psum[:, 0, c * S + t * P:c * S + (t + 1) * P],
                                                           xn[:, u, t, c * P:(c + 1) * P], ident32[:, :])
                        last.then_inc(xT_done, 1)
                        pe.wait_ge(xT_out, n + 2)
                        pe.wait_ge(sh_ready, n + 1)
                        for t in range(TT):
                            for c in range(KT):
                                last = nc.tensor.matmul(psum[:, 1, t * E0:(t + 1) * E0], xT[:, c, t * P:(t + 1) * P],
                                                        gate_w[:, c, :], start=c == 0, stop=c == KT - 1)
                        last.then_inc(lg_done, 1)
                        pe.wait_ge(m_ready, n + 2)
                        nc.tensor.matmul(psum[:, 2, 0:E0], tri[:, 0, :], msk[:, 0, :], start=True, stop=True)
                        nc.tensor.matmul(psum[:, 2, E0:2 * E0], tri[:, 0, :], msk[:, 1, :], start=True, stop=False)
                        nc.tensor.matmul(psum[:, 2, E0:2 * E0], tri[:, 1, :], msk[:, 0, :], start=False,
                                         stop=True).then_inc(pos_done, 1)

            @block.scalar
            def _(act):
                with act.Fori(0, B) as n:
                    act.wait_ge(xT_done, n + 2)
                    act.wait_ge(lg_done, n + 1)
                    nc.scalar.activation(xT[:, :, :], psum[:, 0, :].rearrange("p (c s) -> p c s", c=KT),
                                         ACT.Copy).then_inc(xT_out, 1)
                    act.wait_ge(sh_ready, n + 2)
                    nc.scalar.activation(pr[:, :, :], lg[:, :, :], ACT.Exp).then_inc(ex_ready, 1)

            @block.gpsimd
            def _(pool):
                with pool.Fori(0, B // 2) as i:
                    for u in range(2):
                        hold(pool, idx_ready, i * 2 + u + 2)
                        for t in range(TT):
                            for k in range(2):
                                pool.indirect_dma_start(
                                    disp, bass.IndirectOffsetOnAxis(ap=sidx[:, u, k, t:t + 1], axis=0),
                                    xn[:, u, t, :], None, bounds_check=E0 * ROWS - 1, oob_is_err=False)\
                                    .then_inc(sent, 16)
                        hold(pool, sent, (i * 2 + u + 1) * 64)
                        pool.sem_inc(sent_seq, 1)

            @block.vector
            def _(dve):
                V = nc.vector

                with dve.Fori(0, B // 2) as i:
                    for u in range(2):
                        n = i * 2 + u
                        step = [0]

                        def link(ins, step=step, n=n):
                            step[0] += 1
                            ins.then_inc(ch, 1)
                            hold(dve, ch, (n + 1) * CHN + step[0])

                        hold(dve, sent_seq, n + 1)
                        for t in range(TT):
                            nt = n * TT + t
                            last = V.tensor_scalar(xn[:, u, t, :],
                                                   x[:, bass.ds(nt, 1), :].rearrange("p a d -> p (a d)"),
                                                   mv[:, bass.ds(nt, 1), 0], rstd[:, bass.ds(nt, 1)],
                                                   ALU.subtract, ALU.mult)
                        last.then_inc(xn_ready, 1)
                        dve.wait_ge(lg_done, n + 2)
                        link(V.tensor_reduce(mx[:, :], psum[:, 1, 0:TT * E0].rearrange("p (t e) -> p t e", e=E0),
                                             AX.X, ALU.max))
                        V.tensor_tensor(lg[:, :, :], psum[:, 1, 0:TT * E0].rearrange("p (t e) -> p t e", e=E0),
                                        mx[:, :].unsqueeze(2).broadcast_to([P, TT, E0]),
                                        ALU.subtract).then_inc(sh_ready, 1)
                        dve.wait_ge(ex_ready, n + 2)
                        link(V.tensor_reduce(rs[:, :], pr[:, :, :], AX.X, ALU.add))
                        link(V.reciprocal(rs[:, :], rs[:, :]))
                        link(V.tensor_tensor(pr[:, :, :], pr[:, :, :], rs[:, :].unsqueeze(2).broadcast_to([P, TT, E0]),
                                             ALU.mult))
                        V.max(top[:, 0, :], pr[:, 0, :])
                        link(V.max(top[:, 1, :], pr[:, 1, :]))
                        V.max_index(ti[:, 0, :], top[:, 0, :], pr[:, 0, :])
                        link(V.max_index(ti[:, 1, :], top[:, 1, :], pr[:, 1, :]))
                        link(V.tensor_copy(tf[:, :, :], ti[:, :, 0:2]))
                        for k in range(2):
                            last = V.tensor_tensor(oh[:, k, :, :], iota[:, :].unsqueeze(1).broadcast_to([P, TT, E0]),
                                                   tf[:, :, k:k + 1].broadcast_to([P, TT, E0]), ALU.is_equal)
                        link(last)
                        V.tensor_tensor(msk[:, :, :], oh[:, 0, :, :], oh[:, 1, :, :], ALU.add).then_inc(m_ready, 1)
                        for k in range(2):
                            V.tensor_tensor(tmp[:, 1, k, :, :], oh[:, k, :, :], pr[:, :, :], ALU.mult)
                        dve.wait_ge(pos_done, n + 2)
                        for k in range(2):
                            last = V.tensor_tensor(tmp[:, 0, k, :, :], oh[:, k, :, :],
                                                   psum[:, 2, 0:TT * E0].rearrange("p (t e) -> p t e", e=E0), ALU.mult)
                        link(last)
                        link(V.tensor_reduce(pk[:, :, :, :].rearrange("p a k t -> p (a k t)"),
                                             tmp[:, :, :, :, :].rearrange("p a k t e -> p (a k t) e"), AX.X, ALU.add))
                        V.tensor_scalar(keep[:, :, :], pk[:, 0, :, :], float(CAP), None, ALU.is_le)
                        link(V.scalar_tensor_tensor(row[:, :, :], tf[:, :, :].rearrange("p t k -> p k t"), float(ROWS),
                                                    pk[:, 0, :, :], ALU.mult, ALU.add))
                        link(V.tensor_scalar(row[:, :, :], row[:, :, :], base[:, :], None, ALU.add))
                        link(V.tensor_scalar(far[:, :, :], keep[:, :, :], -float(1 << 20), float(1 << 20),
                                             ALU.mult, ALU.add))
                        V.tensor_tensor(sidx[:, u, :, :], row[:, :, :], far[:, :, :], ALU.add).then_inc(idx_ready, 1)
                        V.tensor_tensor(gidx[:, bass.ds(n * TT, TT), :].rearrange("p t k -> p k t"), row[:, :, :],
                                        keep[:, :, :], ALU.mult)
                        link(V.tensor_tensor(pk[:, 1, :, :], pk[:, 1, :, :], keep[:, :, :], ALU.mult))
                        V.tensor_scalar(gw[:, bass.ds(n * TT, TT), :].rearrange("p t k -> p k t"), pk[:, 1, :, :],
                                        gate[:, 1:2], None, ALU.mult)
                        link(V.tensor_scalar(base[:, :], base[:, :], float(CAP), None, ALU.add))
                        while step[0] < CHN:
                            dve.sem_inc(ch, 1)
                            step[0] += 1
        r.close()

        f = ExitStack()

        def fb(name, shape, dt):
            return f.enter_context(nc.sbuf_tensor("m0_" + name, shape, dt))

        wl = fb("w_load", [P, 3, WP], F32)
        wh = fb("w_halves", [P, 2, 2, 3, WP], F16)
        rows = fb("rows", [P, CT, D], F32)
        xT = fb("xT", [P, 2, 2, KT, ROWS], F16)
        hsb = fb("silu", [P, 2, CH], F32)
        hp = fb("hidden", [P, 2, CH], F32)
        hT = fb("hiddenT", [P, 2, FT, CH], F16)
        y = fb("y", [P, CT, D], F32)
        w_dram = [a["L0_w1"], a["L0_w3"], a["L0_w2"]]
        w_loaded = sem("m0f_w_loaded")
        w_hi = sem("m0f_w_hi")
        w_lo = sem("m0f_w_lo")
        rows_in = sem("m0f_rows_in")
        rT_done = sem("m0f_rows_transposed")
        xT_hi = sem("m0f_xT_hi")
        xT_lo = sem("m0f_xT_lo")
        h_done = sem("m0f_h_done")
        s_done = sem("m0f_silu")
        g_done = sem("m0f_gated")
        hh = sem("m0f_hidden_hi")
        hl = sem("m0f_hidden_lo")
        y_done = sem("m0f_y_done")
        y_out = sem("m0f_y_out")
        y_sent = sem("m0f_y_sent")
        y_free = sem("m0f_y_free")
        with nc.Block() as block:

            @block.sync
            def _(sp):
                for counter, number in ((w_loaded, 48), (w_hi, 3), (w_lo, 3), (rows_in, 16), (rT_done, 1),
                                        (xT_hi, 1), (xT_lo, 1), (h_done, FT), (s_done, FT), (g_done, FT), (hh, FT),
                                        (hl, FT), (y_done, 1), (y_out, 1), (y_free, 1)):
                    sp.sem_inc(counter, number)

        def both_(eng, prepare, compute, e, u, c, n):
            compute(u, c, n, lambda: prepare(e + 1, 1 - u, c, n + NC))

        with nc.Block() as block:

            @block.sync
            def _(sp):
                with sp.Fori(0, E0) as e:
                    hold(sp, w_lo, (e + 1) * 3)
                    for m in range(3):
                        sp.dma_start(wl[:, m, :], w_dram[m][e, :, :]).then_inc(w_loaded, 16)
                    with sp.Fori(0, NC) as c:
                        q = e * NC + c
                        hold(sp, rT_done, q + 1)
                        sp.dma_start(rows[:, :, :],
                                     disp[bass.ds(q * CH, CH), :].rearrange("(t p) d -> p t d", p=P))\
                            .then_inc(rows_in, 16)

            @block.gpsimd
            def _(pool):
                with pool.Fori(0, STEPS) as n:
                    hold(pool, y_out, n + 2)
                    pool.dma_start(eo[bass.ds(n * CH, CH), :].rearrange("(t p) d -> p t d", p=P), y[:, :, :])\
                        .then_inc(y_sent, 16)
                    hold(pool, y_sent, (n + 1) * 16)
                    pool.sem_inc(y_free, 1)

            @block.tensor
            def _(pe):
                mm = nc.tensor.matmul

                def prepare(e, u, c, q):
                    pe.wait_ge(rows_in, (q + 2) * 16)
                    pe.wait_ge(xT_lo, q + 1)
                    for d_ in range(KT):
                        for t in range(CT):
                            last = nc.tensor.transpose(psum[:, 3, d_ * CH + t * P:d_ * CH + (t + 1) * P],
                                                       rows[:, t, d_ * P:(d_ + 1) * P], ident32[:, :])
                    last.then_inc(rT_done, 1)

                def compute(u, c, n, fill):
                    pe.wait_ge(xT_lo, n + 2)

                    def hidden(f_):
                        if f_ >= 3:
                            pe.wait_ge(g_done, (n + 1) * FT + f_ - 2)
                        else:
                            pe.wait_ge(g_done, (n + 1) * FT)
                        for m in range(2):
                            k = 0
                            for d_ in range(KT):
                                for ws_, xs_ in ((0, 0), (0, 1), (1, 0)):
                                    last = mm(psum[:, f_ % 3, m * CH:(m + 1) * CH],
                                              wh[:, u, ws_, m, d_ * F0 + f_ * P:d_ * F0 + (f_ + 1) * P],
                                              xT[:, u, xs_, d_, bass.ds(c * CH, CH)],
                                              start=k == 0, stop=k == 5)
                                    k += 1
                        last.then_inc(h_done, 1)

                    def down(f_):
                        pe.wait_ge(hl, (n + 1) * FT + f_ + 1)
                        if f_ == 0:
                            pe.wait_ge(y_out, n + 1)
                        for t in range(CT):
                            k = 0
                            for hs_, ws_ in ((0, 0), (0, 1), (1, 0)):
                                last = mm(psum[:, 4 + t, 0:D], hT[:, hs_, f_, t * P:(t + 1) * P],
                                          wh[:, u, ws_, 2, f_ * D:(f_ + 1) * D],
                                          start=f_ == 0 and k == 0, stop=f_ == FT - 1 and k == 2)
                                k += 1
                        if f_ == FT - 1:
                            last.then_inc(y_done, 1)

                    for f_ in range(FT):
                        hidden(f_)
                        if f_ >= 2:
                            down(f_ - 2)
                    fill()
                    down(FT - 2)
                    down(FT - 1)

                with pe.Fori(0, NC) as c:
                    prepare(0, 0, c, c)
                pe.wait_ge(w_lo, 6)
                with pe.Fori(0, E0 // 2 - 1) as i:
                    for u in range(2):
                        hold(pe, w_lo, (i * 2 + u + 2) * 3)
                        with pe.Fori(0, NC) as c:
                            both_(pe, prepare, compute, i * 2 + u, u, c, (i * 2 + u) * NC + c)
                pe.wait_ge(w_lo, E0 * 3)
                with pe.Fori(0, NC) as c:
                    both_(pe, prepare, compute, E0 - 2, 0, c, (E0 - 2) * NC + c)
                pe.wait_ge(w_lo, (E0 + 1) * 3)
                with pe.Fori(0, NC) as c:
                    compute(1, c, (E0 - 1) * NC + c, lambda: None)

            @block.scalar
            def _(act):
                A = nc.scalar.activation

                def prepare(e, u, c, q):
                    act.wait_ge(rT_done, q + 2)
                    A(xT[:, u, 0, :, bass.ds(c * CH, CH)], psum[:, 3, :].rearrange("p (c s) -> p c s", c=KT),
                      ACT.Copy).then_inc(xT_hi, 1)

                def weights(e, u):
                    for m in range(3):
                        act.wait_ge(w_loaded, (e + 2) * 48)
                        A(wh[:, u, 0, m, :], wl[:, m, :], ACT.Copy).then_inc(w_hi, 1)

                def compute(u, c, n, fill):
                    for f_ in range(FT):
                        act.wait_ge(h_done, (n + 1) * FT + f_ + 1)
                        act.wait_ge(g_done, (n + 1) * FT + f_ - 1)
                        A(hsb[:, f_ % 2, :], psum[:, f_ % 3, 0:CH], ACT.Silu).then_inc(s_done, 1)
                        upper(n, f_)
                    fill()

                def upper(n, f_):
                    act.wait_ge(g_done, (n + 1) * FT + f_ + 1)
                    if f_ == 0:
                        act.wait_ge(y_done, n + 1)
                    A(hT[:, 0, f_, :], hp[:, f_ % 2, :], ACT.Copy).then_inc(hh, 1)

                weights(0, 0)
                with act.Fori(0, NC) as c:
                    prepare(0, 0, c, c)
                with act.Fori(0, E0 // 2 - 1) as i:
                    for u in range(2):
                        act.wait_ge(y_done, (i * 2 + u) * NC + 1)
                        weights(i * 2 + u + 1, 1 - u)
                        with act.Fori(0, NC) as c:
                            both_(act, prepare, compute, i * 2 + u, u, c, (i * 2 + u) * NC + c)
                act.wait_ge(y_done, (E0 - 2) * NC + 1)
                weights(E0 - 1, 1)
                with act.Fori(0, NC) as c:
                    both_(act, prepare, compute, E0 - 2, 0, c, (E0 - 2) * NC + c)
                with act.Fori(0, NC) as c:
                    compute(1, c, (E0 - 1) * NC + c, lambda: None)

            @block.vector
            def _(dve):
                V = nc.vector

                def prepare(e, u, c, q):
                    dve.wait_ge(xT_hi, q + 2)
                    V.tensor_tensor(xT[:, u, 1, :, bass.ds(c * CH, CH)],
                                    psum[:, 3, :].rearrange("p (c s) -> p c s", c=KT),
                                    xT[:, u, 0, :, bass.ds(c * CH, CH)], ALU.subtract).then_inc(xT_lo, 1)

                def weights(e, u):
                    for m in range(3):
                        dve.wait_ge(w_hi, (e + 1) * 3 + m + 1)
                        V.tensor_tensor(wh[:, u, 1, m, :], wl[:, m, :], wh[:, u, 0, m, :],
                                        ALU.subtract).then_inc(w_lo, 1)

                def lower(n, f_):
                    dve.wait_ge(hh, (n + 1) * FT + f_ + 1)
                    V.tensor_tensor(hT[:, 1, f_, :], hp[:, f_ % 2, :], hT[:, 0, f_, :], ALU.subtract).then_inc(hl, 1)

                def compute(u, c, n, fill):
                    for f_ in range(FT):
                        dve.wait_ge(s_done, (n + 1) * FT + f_ + 1)
                        dve.wait_ge(hl, (n + 1) * FT + f_ - 1)
                        V.tensor_tensor(hp[:, f_ % 2, :], psum[:, f_ % 3, CH:2 * CH], hsb[:, f_ % 2, :],
                                        ALU.mult).then_inc(g_done, 1)
                        lower(n, f_)
                    fill()
                    dve.wait_ge(y_done, n + 2)
                    dve.wait_ge(y_free, n + 1)
                    V.tensor_copy(y[:, :, :], psum[:, 4:4 + CT, 0:D]).then_inc(y_out, 1)

                weights(0, 0)
                with dve.Fori(0, NC) as c:
                    prepare(0, 0, c, c)
                with dve.Fori(0, E0 // 2 - 1) as i:
                    for u in range(2):
                        weights(i * 2 + u + 1, 1 - u)
                        with dve.Fori(0, NC) as c:
                            both_(dve, prepare, compute, i * 2 + u, u, c, (i * 2 + u) * NC + c)
                weights(E0 - 1, 1)
                with dve.Fori(0, NC) as c:
                    both_(dve, prepare, compute, E0 - 2, 0, c, (E0 - 2) * NC + c)
                with dve.Fori(0, NC) as c:
                    compute(1, c, (E0 - 1) * NC + c, lambda: None)
        f.close()

        g_ = ExitStack()
        NB = 4
        yb = g_.enter_context(nc.sbuf_tensor("m0_gathered", [P, NB, TT, 2, D], F32))
        gi = g_.enter_context(nc.sbuf_tensor("m0_rows_of_seq", [P, NB, TT, 2], U32))
        gi_ready = sem("m0g_rows")
        got = [sem(f"m0g_gathered{u}") for u in range(NB)]
        used = sem("m0g_used")
        st_chain = sem("m0g_stats")
        with nc.Block() as block:

            @block.sync
            def _(sp):
                for counter, number in ((gi_ready, 1), (used, NB * 2 * TT), (st_chain, 5)):
                    sp.sem_inc(counter, number)

        with nc.Block() as block:

            @block.gpsimd
            def _(pool):
                with pool.Fori(0, B // NB) as i:
                    for u in range(NB):
                        n = i * NB + u
                        hold(pool, used, (n + 1) * 2 * TT)
                        pool.tensor_copy(gi[:, u, :, :], gidx[:, bass.ds(n * TT, TT), :]).then_inc(gi_ready, 1)
                        hold(pool, gi_ready, n + 2)
                        for t in range(TT):
                            for k in range(2):
                                pool.indirect_dma_start(
                                    yb[:, u, t, k, :], None, eo,
                                    bass.IndirectOffsetOnAxis(ap=gi[:, u, t, k:k + 1], axis=0)).then_inc(got[u], 16)

            @block.vector
            def _(dve):
                with dve.Fori(0, B // NB) as i:
                    for u in range(NB):
                        n = i * NB + u
                        dve.wait_ge(got[u], (i + 1) * 64)
                        for k in range(2):
                            for t in range(TT):
                                xt = x[:, bass.ds(n * TT + t, 1), :].rearrange("p a d -> p (a d)")
                                nc.vector.scalar_tensor_tensor(xt, yb[:, u, t, k, :],
                                                               gw[:, bass.ds(n * TT + t, 1), k], xt,
                                                               ALU.mult, ALU.add).then_inc(used, 1)
                            hold(dve, used, (n + NB) * 2 * TT + (k + 1) * TT)
                        token_stats(dve, n, st_chain)
        g_.close()
        stack.close()

    def moe1():
        E1, K1, NG = 16, 4, 4
        EG = E1 // NG
        NE = E1 + 2
        CH = 512
        CT = CH // P
        NC = B * S // CH
        WE = (2 * KT + 2) * P
        SCALE = 2.5
        stack = ExitStack()

        def sb(name, shape, dt):
            return stack.enter_context(nc.sbuf_tensor("m1_" + name, shape, dt))

        ew = sb("expert_weight", [P, NT, NE], F32)
        xTa = sb("xT_all", [P, 2, KT, B * S], F16)
        wh = sb("w_halves", [P, 2, NE, WE], F16)
        NL = 3
        r = ExitStack()

        def rb(name, shape, dt):
            return r.enter_context(nc.sbuf_tensor("m1_" + name, shape, dt))

        wl = rb("w_load", [P, NE // NL, WE], F32)
        xn = rb("xn", [P, 2, TT, D], F32)
        xT = rb("xT32", [P, KT, S], F32)
        router = rb("router", [P, KT, E1], F32)
        e_bias = rb("e_bias", [P, E1], F32)
        iota = rb("iota", [P, E1], F32)
        less = rb("less", [P, NG, NG], F32)
        sg = rb("scores", [P, TT, E1], F32)
        sc = rb("biased", [P, TT, E1], F32)
        hi2 = rb("pair_max", [P, TT * NG, 2], F32)
        lo2 = rb("pair_min", [P, TT * NG, 2], F32)
        g1 = rb("group_first", [P, TT * NG], F32)
        g2 = rb("group_second", [P, TT * NG], F32)
        g3 = rb("group_third", [P, TT * NG], F32)
        gt = rb("above", [P, TT, NG, NG], F32)
        eq = rb("equal", [P, TT, NG, NG], F32)
        rank = rb("rank", [P, TT, NG], F32)
        top = rb("top", [P, TT, 8], F32)
        ti = rb("top_index", [P, TT, 8], U32)
        tf = rb("top_index_f", [P, TT, K1], F32)
        oh = rb("one_hot", [P, TT, K1, E1], F32)
        sel = rb("chosen", [P, TT, E1], F32)
        den = rb("denominator", [P, TT], F32)
        ld = sem("m1_loaded")
        w_loaded = sem("m1_w_loaded")
        w_hi = sem("m1_w_hi")
        w_lo = sem("m1_w_lo")
        xn_ready = sem("m1_xn_ready")
        xT_done = sem("m1_xT_done")
        xT_out = sem("m1_xT_out")
        xT_hi = sem("m1_xT_hi")
        xT_lo = sem("m1_xT_lo")
        lg_done = sem("m1_logits_done")
        sg_ready = sem("m1_scores")
        ch = sem("m1_chain")
        ew_chain = sem("m1_weights_chain")
        CHN = 21
        with nc.Block() as block:

            @block.sync
            def _(sp):
                for counter, number in ((xn_ready, 1), (xT_done, 1), (xT_out, 1), (xT_hi, 1), (xT_lo, 1),
                                        (lg_done, 1), (sg_ready, 1), (ch, CHN)):
                    sp.sem_inc(counter, number)
                for dst, k in ((router[:, :, :], "L1_router"), (e_bias[:, :], "L1_e_bias"), (iota[:, :], "iota"),
                               (less[:, :, :], "less")):
                    sp.dma_start(dst, a[k]).then_inc(ld, 16)
                sp.wait_ge(ld, 64)

            @block.vector
            def _(dve):
                nc.vector.tensor_scalar(ew[:, :, E1:NE], mv[:, :, 0:NE - E1], 0.0, gate[:, 3:4], ALU.mult, ALU.add)

        with nc.Block() as block:

            @block.sync
            def _(sp):
                n = NE // NL
                for c in range(NL):
                    if c:
                        sp.wait_ge(w_lo, c)
                    sp.dma_start(wl[:, :, :], a["L1_experts"][:, c * n:(c + 1) * n, :]).then_inc(w_loaded, 16)

            @block.tensor
            def _(pe):
                with pe.Fori(0, B // 2) as i:
                    for u in range(2):
                        n = i * 2 + u
                        pe.wait_ge(xn_ready, n + 2)
                        pe.wait_ge(xT_lo, n + 1)
                        for c in range(KT):
                            for t in range(TT):
                                last = nc.tensor.transpose(psum[:, 0, c * S + t * P:c * S + (t + 1) * P],
                                                           xn[:, u, t, c * P:(c + 1) * P], ident32[:, :])
                        last.then_inc(xT_done, 1)
                        pe.wait_ge(xT_out, n + 2)
                        pe.wait_ge(sg_ready, n + 1)
                        for t in range(TT):
                            for c in range(KT):
                                last = nc.tensor.matmul(psum[:, 1, t * E1:(t + 1) * E1], xT[:, c, t * P:(t + 1) * P],
                                                        router[:, c, :], start=c == 0, stop=c == KT - 1)
                        last.then_inc(lg_done, 1)

            @block.scalar
            def _(act):
                A = nc.scalar.activation
                n_ = NE // NL
                for c in range(NL):
                    act.wait_ge(w_loaded, 16 * (c + 1))
                    A(wh[:, 0, c * n_:(c + 1) * n_, :], wl[:, :, :], ACT.Copy).then_inc(w_hi, 1)
                with act.Fori(0, B) as n:
                    act.wait_ge(xT_done, n + 2)
                    act.wait_ge(lg_done, n + 1)
                    A(xT[:, :, :], psum[:, 0, :].rearrange("p (c s) -> p c s", c=KT), ACT.Copy).then_inc(xT_out, 1)
                    A(xTa[:, 0, :, bass.ds(n * S, S)], psum[:, 0, :].rearrange("p (c s) -> p c s", c=KT),
                      ACT.Copy).then_inc(xT_hi, 1)
                    act.wait_ge(lg_done, n + 2)
                    A(sg[:, :, :], psum[:, 1, 0:TT * E1].rearrange("p (t e) -> p t e", e=E1),
                      ACT.Sigmoid).then_inc(sg_ready, 1)

            @block.vector
            def _(dve):
                V = nc.vector
                n_ = NE // NL
                for c in range(NL):
                    dve.wait_ge(w_hi, c + 1)
                    V.tensor_tensor(wh[:, 1, c * n_:(c + 1) * n_, :], wl[:, :, :], wh[:, 0, c * n_:(c + 1) * n_, :],
                                    ALU.subtract).then_inc(w_lo, 1)
                with dve.Fori(0, B // 2) as i:
                    for u in range(2):
                        n = i * 2 + u
                        step = [0]

                        def link(ins, step=step, n=n):
                            step[0] += 1
                            ins.then_inc(ch, 1)
                            hold(dve, ch, (n + 1) * CHN + step[0])

                        for t in range(TT):
                            nt = n * TT + t
                            last = V.tensor_scalar(xn[:, u, t, :],
                                                   x[:, bass.ds(nt, 1), :].rearrange("p a d -> p (a d)"),
                                                   mv[:, bass.ds(nt, 1), 0], rstd[:, bass.ds(nt, 1)],
                                                   ALU.subtract, ALU.mult)
                        last.then_inc(xn_ready, 1)
                        dve.wait_ge(xT_hi, n + 2)
                        V.tensor_tensor(xTa[:, 1, :, bass.ds(n * S, S)],
                                        psum[:, 0, :].rearrange("p (c s) -> p c s", c=KT),
                                        xTa[:, 0, :, bass.ds(n * S, S)], ALU.subtract).then_inc(xT_lo, 1)
                        dve.wait_ge(sg_ready, n + 2)
                        link(V.tensor_tensor(sc[:, :, :], sg[:, :, :], e_bias[:, :].unsqueeze(1)
                                             .broadcast_to([P, TT, E1]), ALU.add))
                        four = sc[:, :, :].rearrange("p t (g h r) -> p (t g) h r", h=2, r=2)
                        V.tensor_tensor(hi2[:, :, :], four[:, :, :, 0], four[:, :, :, 1], ALU.max)
                        link(V.tensor_tensor(lo2[:, :, :], four[:, :, :, 0], four[:, :, :, 1], ALU.min))
                        V.tensor_tensor(g1[:, :], hi2[:, :, 0], hi2[:, :, 1], ALU.max)
                        V.tensor_tensor(g2[:, :], hi2[:, :, 0], hi2[:, :, 1], ALU.min)
                        link(V.tensor_tensor(g3[:, :], lo2[:, :, 0], lo2[:, :, 1], ALU.max))
                        link(V.tensor_tensor(g2[:, :], g2[:, :], g3[:, :], ALU.max))
                        link(V.tensor_tensor(g1[:, :], g1[:, :], g2[:, :], ALU.add))
                        gs = g1[:, :].rearrange("p (t g) -> p t g", g=NG)
                        other = gs.unsqueeze(2).broadcast_to([P, TT, NG, NG])
                        own = gs.unsqueeze(3).broadcast_to([P, TT, NG, NG])
                        V.tensor_tensor(gt[:, :, :, :], other, own, ALU.is_gt)
                        link(V.tensor_tensor(eq[:, :, :, :], other, own, ALU.is_equal))
                        link(V.tensor_tensor(eq[:, :, :, :], eq[:, :, :, :],
                                             less[:, :, :].unsqueeze(1).broadcast_to([P, TT, NG, NG]), ALU.mult))
                        link(V.tensor_tensor(gt[:, :, :, :], gt[:, :, :, :], eq[:, :, :, :], ALU.add))
                        link(V.tensor_reduce(rank[:, :, :], gt[:, :, :, :], AX.X, ALU.add))
                        link(V.tensor_scalar(rank[:, :, :], rank[:, :, :], 1.5, None, ALU.is_lt))
                        link(V.tensor_tensor(sc[:, :, :].rearrange("p t (g h) -> p t g h", g=NG),
                                             sc[:, :, :].rearrange("p t (g h) -> p t g h", g=NG),
                                             rank[:, :, :].unsqueeze(3).broadcast_to([P, TT, NG, EG]), ALU.mult))
                        link(V.tensor_scalar(sc[:, :, :], sc[:, :, :], 0.0, None, ALU.add))
                        V.max(top[:, 0, :], sc[:, 0, :])
                        link(V.max(top[:, 1, :], sc[:, 1, :]))
                        V.max_index(ti[:, 0, :], top[:, 0, :], sc[:, 0, :])
                        link(V.max_index(ti[:, 1, :], top[:, 1, :], sc[:, 1, :]))
                        link(V.tensor_copy(tf[:, :, :], ti[:, :, 0:K1]))
                        link(V.tensor_tensor(oh[:, :, :, :],
                                             iota[:, :].unsqueeze(1).unsqueeze(1).broadcast_to([P, TT, K1, E1]),
                                             tf[:, :, :].unsqueeze(3).broadcast_to([P, TT, K1, E1]), ALU.is_equal))
                        link(V.tensor_reduce(sel[:, :, :], oh[:, :, :, :].rearrange("p t k e -> p t e k"), AX.X, ALU.add))
                        link(V.tensor_tensor(sel[:, :, :], sel[:, :, :], sg[:, :, :], ALU.mult))
                        link(V.tensor_reduce(den[:, :], sel[:, :, :], AX.X, ALU.add))
                        link(V.tensor_scalar(den[:, :], den[:, :], 1e-20, None, ALU.add))
                        link(V.reciprocal(den[:, :], den[:, :]))
                        assert step[0] == CHN, step
                        V.tensor_tensor(sel[:, :, :], sel[:, :, :], den[:, :].unsqueeze(2).broadcast_to([P, TT, E1]),
                                        ALU.mult).then_inc(ew_chain, 1)
                        hold(dve, ew_chain, n + 1)
                        V.tensor_scalar(ew[:, bass.ds(n * TT, TT), 0:E1], sel[:, :, :], SCALE, gate[:, 3:4],
                                        ALU.mult, ALU.mult)
        r.close()

        f = ExitStack()

        def fb(name, shape, dt):
            return f.enter_context(nc.sbuf_tensor("m1_" + name, shape, dt))

        hsb = fb("silu", [P, 3, CH], F32)
        hp = fb("hidden", [P, 3, CH], F32)
        hT = fb("hiddenT", [P, 3, 2, CH], F16)
        h_done = sem("m1f_h_done")
        s_done = sem("m1f_silu")
        g_done = sem("m1f_gated")
        hh = sem("m1f_hidden_hi")
        hl = sem("m1f_hidden_lo")
        y_done = sem("m1f_y_done")
        y_add = sem("m1f_y_added")
        with nc.Block() as block:

            @block.sync
            def _(sp):
                for counter, number in ((h_done, 3), (s_done, 3), (g_done, 3), (hh, 3), (hl, 3), (y_done, 3),
                                        (y_add, 3 * CT)):
                    sp.sem_inc(counter, number)

        def steps(eng, head, tail):
            with eng.Fori(0, NC) as c:
                for e in range(2):
                    head(c, e, e, c * NE + e)
                with eng.Fori(0, NE // 3 - 1) as j:
                    for u in range(3):
                        head(c, j * 3 + u + 2, (u + 2) % 3, c * NE + j * 3 + u + 2)
                        tail(c, j * 3 + u, u, c * NE + j * 3 + u)
                head(c, NE - 1, 2, c * NE + NE - 1)
                for u in range(3):
                    tail(c, NE - 3 + u, u, c * NE + NE - 3 + u)

        with nc.Block() as block:

            @block.tensor
            def _(pe):
                mm = nc.tensor.matmul

                def wt(half, e, m):
                    return wh[:, half, bass.ds(e, 1), m * P:(m + 1) * P].rearrange("p a n -> p (a n)")

                def hidden(c, e, u, n):
                    pe.wait_ge(g_done, n + 1)
                    for m in range(2):
                        k = 0
                        for d_ in range(KT):
                            for ws_, xs_ in ((0, 0), (0, 1), (1, 0)):
                                last = mm(psum[:, 2 * u + m, :], wt(ws_, e, m * KT + d_),
                                          xTa[:, xs_, d_, bass.ds(c * CH, CH)], start=k == 0, stop=k == 5)
                                k += 1
                    last.then_inc(h_done, 1)

                def down(c, e, u, n):
                    pe.wait_ge(hl, n + 4)
                    pe.wait_ge(y_add, (n + 3) * CT)
                    for t in range(CT):
                        k = 0
                        for hs_, ws_ in ((0, 0), (0, 1), (1, 0)):
                            w2 = wh[:, ws_, bass.ds(e, 1), 2 * KT * P:WE].rearrange("p a n -> p (a n)")
                            last = mm(psum[:, 6 + t // 2, (t % 2) * D:(t % 2 + 1) * D],
                                      hT[:, u, hs_, t * P:(t + 1) * P], w2, start=k == 0, stop=k == 2)
                            k += 1
                    last.then_inc(y_done, 1)

                steps(pe, hidden, down)

            @block.scalar
            def _(act):
                A = nc.scalar.activation

                def head(c, e, u, n):
                    act.wait_ge(h_done, n + 4)
                    act.wait_ge(g_done, n + 1)
                    A(hsb[:, u, :], psum[:, 2 * u, :], ACT.Silu).then_inc(s_done, 1)
                    act.wait_ge(g_done, n + 4)
                    act.wait_ge(y_done, n + 1)
                    A(hT[:, u, 0, :], hp[:, u, :], ACT.Copy).then_inc(hh, 1)

                steps(act, head, lambda c, e, u, n: None)

            @block.vector
            def _(dve):
                V = nc.vector

                def head(c, e, u, n):
                    dve.wait_ge(s_done, n + 4)
                    dve.wait_ge(hl, n + 1)
                    V.tensor_tensor(hp[:, u, :], psum[:, 2 * u + 1, :], hsb[:, u, :], ALU.mult).then_inc(g_done, 1)
                    dve.wait_ge(hh, n + 4)
                    V.tensor_tensor(hT[:, u, 1, :], hp[:, u, :], hT[:, u, 0, :], ALU.subtract).then_inc(hl, 1)

                def add(c, e, u, n):
                    dve.wait_ge(y_done, n + 4)
                    for t in range(CT):
                        dve.wait_ge(y_add, (n + 2) * CT + t + 1)
                        xt = x[:, bass.ds(c * CT + t, 1), :].rearrange("p a d -> p (a d)")
                        V.scalar_tensor_tensor(xt, psum[:, 6 + t // 2, (t % 2) * D:(t % 2 + 1) * D],
                                               ew[:, bass.ds(c * CT + t, 1), bass.ds(e, 1)].rearrange("p a b -> p (a b)"),
                                               xt, ALU.mult, ALU.add).then_inc(y_add, 1)

                steps(dve, head, add)
        f.close()
        stack.close()

    layernorm_scale("n0")
    attention(0)
    layernorm_scale("n1")
    moe0()
    layernorm_scale("n2")
    attention(1)
    layernorm_scale("n3")
    moe1()
    stored = sem("stored")
    with nc.Block() as block:

        @block.sync
        def _(sp):
            for c in range(4):
                sp.dma_start(out_dram[:, c * 8:(c + 1) * 8, :], x[:, c * 8:(c + 1) * 8, :]).then_inc(stored, 16)
            sp.wait_ge(stored, 64)


def _slots(w):
    w = w.reshape(KT, P, G, GH, 1, DH)
    w = np.broadcast_to(w, (KT, P, G, GH, SLOT // DH, DH))
    return np.ascontiguousarray(w.reshape(KT, P, G * P).transpose(1, 0, 2))


def _rows(w):
    return np.ascontiguousarray(w.reshape(-1, P, *w.shape[1:]).swapaxes(0, 1))


def _constants():
    c = {"ident": np.eye(P, dtype=np.float32)}
    r = np.arange(P) % SLOT
    c["hi_rows"] = np.stack([-(r >= DH).astype(np.float32), (r < DH).astype(np.float32)], 1)
    exact = -math.sqrt(DH) * math.log(2.0)
    soft = np.float16(exact)
    rest = np.float16(float(soft) - exact)
    a_, b_ = np.arange(P)[:, None], np.arange(P)[None, :]
    masks = np.zeros((2, P, 4, P), np.float16)
    masks[0, :, 0] = np.where(a_ > b_, soft, rest)
    off = np.float16(-60000.0)
    masks[1, :, 0] = np.where(a_ > b_, off, 0)
    masks[1, :, 1] = np.where(a_ < b_, off, 0)
    masks[1, :, 2] = masks[1, :, 0].T
    masks[1, :, 3] = masks[1, :, 1].T
    k2 = np.zeros((2, GH, SLOT, GH, G, S), np.float16)
    mrows = np.zeros((2, P, TT, G, GH, SLOT), np.float32)
    for j in range(GH):
        k2[:, j, DH, j] = 0.5
        k2[0, j, DH + 1, j, :, P:] = soft
        k2[0, j, DH + 2, j, :, :P] = rest
    mrows[0, :, 0, :, :, DH + 1] = 1.0
    mrows[0, :, 1, :, :, DH + 2] = 1.0
    for L in range(2):
        c[f"L{L}_masks"] = masks[L]
        c[f"L{L}_k2rows"] = k2[L].reshape(P, GH, G, S)
        c[f"L{L}_mrows"] = mrows[L].reshape(P, TT, G, P)
    half = DH // 2
    inv = np.float32(1.0) / np.float32(10000.0) ** (np.arange(half, dtype=np.float32) / np.float32(half))
    ang = np.arange(S, dtype=np.float32)[:, None] * inv[None, :]
    c["iota"] = np.broadcast_to(np.arange(16, dtype=np.float32), (P, 16))
    c["tri"] = np.stack([np.triu(np.ones((P, P))), np.ones((P, P))], 1).astype(np.float16)
    c["less"] = np.broadcast_to((np.arange(4)[None, :] < np.arange(4)[:, None]).astype(np.float32), (P, 4, 4))
    row = np.arange(P) % DH
    c["cos"] = np.cos(ang).astype(np.float32).T[row % half]
    c["sin"] = (np.where(row < half, -1, 1)[:, None] * np.sin(ang).T[row % half]).astype(np.float32)
    return {k: np.ascontiguousarray(v) for k, v in c.items()}


def _layout(inputs):
    i = {k: np.asarray(v) for k, v in inputs.items()}
    n = {"x": i["x"], "ctx": i["ctx_1024"]}
    gates = np.stack([i["g_xattn"][0], i["g_ffn"][0], i["g_xattn"][1], i["g_ffn"][1]])
    n["gates"] = np.ascontiguousarray(np.broadcast_to(gates[None, :], (P, 4)))
    for L in range(2):
        w = {k: i[f"L{L}_xattn_{k}"] for k in ("Wq", "Wk", "Wv", "Wo", "bq", "bk", "bv", "bo")}
        if L:
            w |= {k: w[k].T for k in ("Wq", "Wk", "Wv", "Wo")}
        n[f"L{L}_wq"], n[f"L{L}_wk"] = _slots(w["Wq"]), _slots(w["Wk"])
        n[f"L{L}_wv"], n[f"L{L}_wo"] = _rows(w["Wv"]), _rows(w["Wo"])
        for k in ("bq", "bk"):
            dup = np.broadcast_to(w[k].reshape(G, GH, 1, DH), (G, GH, SLOT // DH, DH))
            n[f"L{L}_{k}"] = np.ascontiguousarray(dup.reshape(G, P).T)
        n[f"L{L}_bv"] = np.ascontiguousarray(w["bv"].reshape(KT, P).T)
        n[f"L{L}_bo"] = np.ascontiguousarray(w["bo"].reshape(1, D))
    n["L0_router"] = _rows(i["L0_ffn_gate_w"].T)
    for k in ("w1", "w3", "w2"):
        w = i[f"L0_ffn_{k}"]
        n[f"L0_{k}"] = np.ascontiguousarray(w.reshape(w.shape[0], -1, P, w.shape[2]).transpose(0, 2, 1, 3)
                                            .reshape(w.shape[0], P, -1))
    n["L1_router"] = _rows(i["L1_ffn_router_weight"].T)
    n["L1_e_bias"] = np.ascontiguousarray(np.broadcast_to(i["L1_ffn_e_bias"][None, :], (P, 16)))
    up = [np.concatenate([i[f"L1_ffn_{k}_w"], i[f"L1_ffn_sh_{k}_w"].reshape(2, P, D)]) for k in ("gate", "up")]
    down = np.concatenate([i["L1_ffn_down_w"], i["L1_ffn_sh_down_w"].reshape(D, 2, P).transpose(1, 0, 2)])
    up = [w.reshape(-1, P, KT, P).transpose(3, 0, 2, 1).reshape(P, -1, KT * P) for w in up]
    n["L1_experts"] = np.ascontiguousarray(np.concatenate(up + [down.transpose(2, 0, 1)], axis=2))
    return n | _constants()


def kernel(**inputs):
    import concourse.bacc as _bacc
    from concourse.bass_utils import run_bass_kernel_spmd as _run

    arrays = _layout(inputs)
    nc = _bacc.Bacc("TRN2", target_bir_lowering=False, num_devices=1)
    args = {k: nc.dram_tensor(f"in_{k}", v.shape, mybir.dt.from_np(v.dtype), kind="ExternalInput").ap()
            for k, v in arrays.items()}
    out = nc.dram_tensor("out_x", (B, S, D), F32, kind="ExternalOutput").ap()
    flamingo_kernel(nc, args, out)
    r = _run(nc, [{f"in_{k}": v for k, v in arrays.items()}], core_ids=[0])
    return r.results[0]["out_x"]
```

```python
import math
from contextlib import ExitStack

import numpy as np

import concourse.bass as bass
from concourse import mybir

F32 = mybir.dt.float32
F16 = mybir.dt.float16
U32 = mybir.dt.uint32
ACT = mybir.ActivationFunctionType
ALU = mybir.AluOpType
AX = mybir.AxisListType

P = 128
D = 256
KT = D // P
B, S = 16, 256
TT = S // P
NT = B * TT
CAP = 80
RT = 8
RG = NT // RT
H, DH = 16, 16
SLOT = 32
GH = P // SLOT
G = H // GH
EPS = 1e-5


def flamingo_kernel(nc, a, out):

    def sb(name, shape, dt):
        return nc.alloc_sbuf_tensor(name, shape, dt)

    sem = nc.alloc_semaphore
    waited = sem("waited")

    def hold(eng, counter, value):
        eng.wait_ge(counter, value)
        eng.sem_inc(waited, 1)

    x = sb("x_res", [P, NT, D], F32)
    mv = sb("mean_var", [P, NT, 2], F32)
    rstd = sb("rstd", [P, NT], F32)
    nwt = sb("newton", [P, NT], F32)
    ident32 = sb("ident32", [P, P], F32)
    ident16 = sb("ident16", [P, P], F16)
    gate = sb("gate", [P, 4], F32)
    graw = sb("gate_raw", [P, 4], F32)
    stats = sb("bn_stats", [P, TT, 6], F32)
    agg = sb("bn_aggregate", [P, TT, 2], F32)
    psum = nc.alloc_psum_tensor("ps", [P, 8, 512], F32)

    x_dram = a["x"].rearrange("b (t p) d -> p (b t) d", p=P)
    ctx_dram = a["ctx"].rearrange("b (t p) d -> b p t d", p=P)
    out_dram = out.rearrange("b (t p) d -> p (b t) d", p=P)

    def token_stats(dve, i, chain):
        for t in range(TT):
            nc.vector.bn_stats(stats[:, t, :], x[:, bass.ds(i * TT + t, 1), :].rearrange("p a d -> p (a d)"))\
              .then_inc(chain, 1)
        hold(dve, chain, (i + 1) * 5 + 2)
        for t in range(TT):
            nc.vector.bn_aggr(agg[:, t, :], stats[:, t, :]).then_inc(chain, 1)
        hold(dve, chain, (i + 1) * 5 + 4)
        nc.vector.tensor_copy(mv[:, bass.ds(i * TT, TT), :], agg[:, :, :]).then_inc(chain, 1)

    x_loaded = sem("x_loaded")
    consts_loaded = sem("consts_loaded")
    setup_chain = sem("setup_chain")
    with nc.Block() as block:

        @block.sync
        def _(sp):
            sp.dma_start(graw[:, :], a["gates"]).then_inc(consts_loaded, 16)
            sp.dma_start(ident32[:, :], a["ident"]).then_inc(consts_loaded, 16)
            for c in range(4):
                sp.dma_start(x[:, c * 8:(c + 1) * 8, :], x_dram[:, c * 8:(c + 1) * 8, :]).then_inc(x_loaded, 16)

        @block.scalar
        def _(act):
            act.wait_ge(consts_loaded, 32)
            nc.scalar.activation(gate[:, :], graw[:, :], ACT.Tanh)
            nc.scalar.activation(ident16[:, :], ident32[:, :], ACT.Copy)

        @block.vector
        def _(dve):
            dve.wait_ge(x_loaded, 64)
            dve.sem_inc(setup_chain, 5)
            with dve.Fori(0, B) as i:
                token_stats(dve, i, setup_chain)

    def layernorm_scale(tag):
        ve = sem(f"{tag}_var_eps")
        sq = sem(f"{tag}_sqrt")
        ch = sem(f"{tag}_rstd_chain")
        with nc.Block() as block:

            @block.vector
            def _(dve):
                nc.vector.tensor_scalar(mv[:, :, 1], mv[:, :, 1], EPS, None, ALU.add).then_inc(ve, 1)
                dve.wait_ge(sq, 1)
                n = 0
                for step in (
                    lambda: nc.vector.reciprocal(rstd[:, :], rstd[:, :]),
                    lambda: nc.vector.tensor_tensor(nwt[:, :], rstd[:, :], rstd[:, :], ALU.mult),
                    lambda: nc.vector.tensor_tensor(nwt[:, :], nwt[:, :], mv[:, :, 1], ALU.mult),
                    lambda: nc.vector.tensor_scalar(nwt[:, :], nwt[:, :], -0.5, 1.5, ALU.mult, ALU.add),
                    lambda: nc.vector.tensor_tensor(rstd[:, :], rstd[:, :], nwt[:, :], ALU.mult),
                ):
                    step().then_inc(ch, 1)
                    n += 1
                    dve.wait_ge(ch, n)

            @block.scalar
            def _(act):
                act.wait_ge(ve, 1)
                nc.scalar.activation(rstd[:, :], mv[:, :, 1], ACT.Sqrt).then_inc(sq, 1)

    def attention_buffers(sb):
        return dict(
            xin=sb("ctx_in", [P, TT, D], F32),
            xn=sb("xn", [P, TT, D], F32),
            xT=sb("xT", [P, 2, KT, S], F16),
            cT=sb("cT", [P, 2, KT, S], F16),
            wq=sb("wq", [P, 2, KT, G, P], F16),
            wk=sb("wk", [P, 2, KT, G, P], F16),
            wv=sb("wv", [P, 2, KT, D], F16),
            wo=sb("wo", [P, 2, KT, D], F16),
            wld=sb("w_load", [P, KT, G * P], F32),
            bq=sb("bq", [P, G], F32),
            bk=sb("bk", [P, G], F32),
            bv=sb("bv", [P, KT], F32),
            bo32=sb("bo32", [1, D], F32),
            bo=sb("bo", [1, 2, D], F16),
            ones=sb("ones_row", [1, P], F16),
            qf=sb("qf", [P, G, S], F32),
            kf=sb("kf", [P, G, S], F32),
            rot=sb("rotated", [P, G, S], F32),
            qh=sb("qh", [P, 2, G, S], F16),
            q1=sb("q1", [P, 2, G, S], F16),
            q2=sb("q2", [P, G, S], F16),
            kh=sb("kh", [P, G, S], F16),
            kl=sb("kl", [P, G, S], F16),
            k1=sb("k1", [P, 2, GH, G, S], F16),
            k2=sb("k2", [P, 2, GH, G, S], F16),
            v=sb("v_ext", [P, 2, TT, H, SLOT], F32),
            m=sb("neg_max", [P, TT, G, P], F32),
            pr=sb("probs", [P, 2, TT, GH, S], F32),
            o=sb("o_slots", [P, G, S], F32),
            on=sb("o_norm", [P, TT, D], F32),
            rd=sb("recip_den", [P, TT, H], F32),
            oT=sb("oT", [P, 2, KT, S], F16),
            hi_rows=sb("hi_rows", [P, 2], F32),
            cos=sb("rope_cos", [P, S], F32),
            sin=sb("rope_sin", [P, S], F32),
            masks=sb("masks16", [P, 4, P], F16),
        )

    def attention(L):
        stack = ExitStack()
        w = attention_buffers(lambda name, shape, dt: stack.enter_context(
            nc.sbuf_tensor(f"a{L}_{name}", shape, dt)))
        causal_band = L == 1
        n = f"A{L}_"
        def pairs(qt):
            return [qt - 1, qt] if causal_band and qt else [qt] if causal_band else list(range(TT))

        wl = sem(n + "weights_loaded")
        ws = sem(n + "weights_split")
        hi_done = sem(n + "weight_hi")
        jobs = [("wq", G * P), ("wk", G * P), ("wv", D), ("wo", D)]
        flat = {k: w[k][:, :, :, :, :].rearrange("p s k g m -> p s k (g m)") for k in ("wq", "wk")}
        flat |= {k: w[k][:, :, :, :] for k in ("wv", "wo")}
        small = [("bq", w["bq"][:, :]), ("bk", w["bk"][:, :]), ("bv", w["bv"][:, :]), ("bo", w["bo32"][0:1, :])]
        with nc.Block() as block:

            @block.sync
            def _(sp):
                for i, (k, dst) in enumerate(small):
                    sp.dma_start(dst, a[f"L{L}_{k}"]).then_inc(wl, 16)
                sp.dma_start(w["masks"][:, :, :], a[f"L{L}_masks"]).then_inc(wl, 16)
                sp.dma_start(w["m"][:, :, :, :], a[f"L{L}_mrows"]).then_inc(wl, 16)
                sp.dma_start(w["hi_rows"][:, :], a["hi_rows"]).then_inc(wl, 16)
                for u in range(2):
                    sp.dma_start(w["k2"][:, u, :, :, :], a[f"L{L}_k2rows"]).then_inc(wl, 16)
                if causal_band:
                    sp.dma_start(w["cos"][:, :], a["cos"]).then_inc(wl, 16)
                    sp.dma_start(w["sin"][:, :], a["sin"]).then_inc(wl, 16)
                base = 16 * (len(small) + 5 + 2 * causal_band)
                for i, (k, width) in enumerate(jobs):
                    sp.wait_ge(wl, base + 16 * i)
                    if i:
                        sp.wait_ge(ws, i)
                    sp.dma_start(w["wld"][:, :, 0:width], a[f"L{L}_{k}"]).then_inc(wl, 16)

            @block.scalar
            def _(act):
                base = 16 * (len(small) + 5 + 2 * causal_band)
                for i, (k, width) in enumerate(jobs):
                    act.wait_ge(wl, base + 16 * (i + 1))
                    nc.scalar.activation(flat[k][:, 0, :, :], w["wld"][:, :, 0:width], ACT.Copy).then_inc(hi_done, 1)
                nc.scalar.activation(w["bo"][0:1, 0, :], w["bo32"][0:1, :], ACT.Copy).then_inc(hi_done, 1)

            @block.gpsimd
            def _(pool):
                pool.memset(w["k1"][:, :, :, :, :], 0.0)
                pool.memset(w["v"][:, :, :, :, DH:SLOT], 1.0)
                pool.memset(w["ones"][0:1, :], 1.0)

            @block.vector
            def _(dve):
                for i, (k, width) in enumerate(jobs):
                    dve.wait_ge(hi_done, i + 1)
                    nc.vector.tensor_tensor(flat[k][:, 1, :, :], w["wld"][:, :, 0:width], flat[k][:, 0, :, :],
                                            ALU.subtract).then_inc(ws, 1)
                dve.wait_ge(hi_done, len(jobs) + 1)
                nc.vector.tensor_tensor(w["bo"][0:1, 1, :], w["bo32"][0:1, :], w["bo"][0:1, 0, :], ALU.subtract)

        counts = {}

        def counter(name, number):
            s_ = sem(n + name)
            counts[name] = (s_, number)
            return s_

        ctx_loaded = counter("ctx_loaded", 16)
        xn_ready = counter("xn_ready", 1)
        tr_done = counter("transposed", 2)
        tr_hi = counter("transposed_hi", 2)
        tr_lo = counter("transposed_lo", 2)
        proj_done = counter("projected", 5)
        proj_out = counter("projection_taken", 5)
        f_ready = counter("qk_rotated", 2)
        rope = counter("rope_steps", 6)
        qk_hi = counter("qk_hi", 2)
        q1_ready = counter("q1_ready", 1)
        kl_ready = counter("k_lo_ready", 1)
        k1_ready = counter("k1_placed", 16 * GH)
        k2_ready = counter("k2_placed", 16 * GH)
        mx_scores = counter("max_scores", 8)
        mx_taken = counter("maxima_taken", 8)
        m_done = counter("maxima_transposed", 2)
        q2_ready = counter("q2_ready", 2)
        sc_done = counter("scores_done", 8)
        ex_done = counter("exp_done", 8)
        av_done = counter("av_done", 4)
        o_out = counter("o_taken", 4)
        oT_done = counter("o_natural", 2)
        rd_ready = counter("recip_ready", 2)
        on_ready = counter("o_normalised", 2)
        on_T = counter("o_norm_transposed", 1)
        oh_ready = counter("oT_hi", 1)
        ol_ready = counter("oT_lo", 1)
        y_done = counter("y_done", 1)
        x_new = counter("x_updated", 1)
        st_chain = counter("stats_chain", 5)
        with nc.Block() as block:

            @block.sync
            def _(sp):
                for s_, number in counts.values():
                    sp.sem_inc(s_, number if s_ is st_chain else 2 * number)

        SC = [psum[:, 0:2, :].rearrange("p b n -> p (b n)"), psum[:, 2:4, :].rearrange("p b n -> p (b n)")]

        def sequences(eng, ahead, body):
            ahead(0, 0)
            with eng.Fori(0, B // 2 - 1) as i:
                for u in range(2):
                    body(i * 2 + u, u, True)
            body(B - 2, 0, True)
            body(B - 1, 1, False)

        with nc.Block() as block:

            @block.sync
            def _(sp):
                def stage(m, u):
                    hold(sp, tr_done, (m + 2) * 2)
                    sp.dma_start(w["xin"][:, :, :], ctx_dram[m, :, :, :]).then_inc(ctx_loaded, 16)
                    hold(sp, qk_hi, (m + 2) * 2 + 1)
                    hold(sp, sc_done, (m + 1) * 8)
                    for j in range(GH):
                        sp.dma_start(w["k1"][j * SLOT:(j + 1) * SLOT, u, j, :, :],
                                     w["kh"][j * SLOT:(j + 1) * SLOT, :, :]).then_inc(k1_ready, 16)
                    hold(sp, kl_ready, m + 3)
                    for j in range(GH):
                        sp.dma_start(w["k2"][j * SLOT:j * SLOT + DH, u, j, :, :],
                                     w["kl"][j * SLOT:j * SLOT + DH, :, :]).then_inc(k2_ready, 16)

                with sp.Fori(0, B // 2) as i:
                    for u in range(2):
                        stage(i * 2 + u, u)

            @block.tensor
            def _(pe):
                mm = nc.tensor.matmul

                def transposes(m):
                    for n_, (src, ready) in enumerate((("xn", None), ("xin", None))):
                        if n_ == 0:
                            pe.wait_ge(xn_ready, m + 3)
                            pe.wait_ge(proj_out, (m + 2) * 5)
                        else:
                            pe.wait_ge(ctx_loaded, (m + 3) * 16)
                        for c in range(KT):
                            for t in range(TT):
                                last = nc.tensor.transpose(psum[:, 4 + n_, c * S + t * P:c * S + (t + 1) * P],
                                                           w[src][:, t, c * P:(c + 1) * P], ident32[:, :])
                        last.then_inc(tr_done, 1)

                def project(m, n_):
                    wt, src = ("wk", "cT") if n_ < 2 else ("wq", "xT")
                    if n_ < 2:
                        pe.wait_ge(tr_lo, (m + 2) * 2 + 2)
                    else:
                        pe.wait_ge(proj_out, (m + 2) * 5 + n_ - 1)
                    for g in (n_ % 2 * 2, n_ % 2 * 2 + 1):
                        o_ = psum[:, 4 + n_ % 2, (g % 2) * S:(g % 2 + 1) * S]
                        k = 0
                        for c in range(KT):
                            for ws_, xs_ in ((0, 0), (0, 1), (1, 0)):
                                last = mm(o_, w[wt][:, ws_, c, g, :], w[src][:, xs_, c, :], start=k == 0, stop=k == 5)
                                k += 1
                    last.then_inc(proj_done, 1)

                def project_v(m):
                    pe.wait_ge(proj_out, (m + 2) * 5 + 3)
                    for t in range(TT):
                        k = 0
                        for c in range(KT):
                            for xs_, ws_ in ((0, 0), (0, 1), (1, 0)):
                                last = mm(psum[:, 4, t * D:(t + 1) * D], w["cT"][:, xs_, c, t * P:(t + 1) * P],
                                          w["wv"][:, ws_, c, :], start=k == 0, stop=k == 5)
                                k += 1
                    last.then_inc(proj_done, 1)

                def ahead(m, u):
                    transposes(m)
                    for n_ in range(4):
                        project(m, n_)
                    project_v(m)

                def max_scores(m, u, s_):
                    t, g = s_ // G, s_ % G
                    if s_ == 0:
                        pe.wait_ge(k1_ready, (m + 3) * (16 * GH))
                        pe.wait_ge(qk_hi, (m + 3) * 2)
                    if s_ == 1:
                        pe.wait_ge(x_new, m + 2)
                    if s_ >= 2:
                        pe.wait_ge(mx_taken, (m + 2) * 8 + s_ - 1)
                    cols = pairs(t)
                    c0, c1 = cols[0] * P, (cols[-1] + 1) * P
                    for j in range(GH):
                        last = mm(SC[s_ % 2][:, j * S + c0:j * S + c1], w["qh"][:, u, g, t * P:(t + 1) * P],
                                  w["k1"][:, u, j, g, c0:c1], start=True, stop=not causal_band)
                        if causal_band:
                            for e, kt in enumerate(cols):
                                last = mm(SC[s_ % 2][:, j * S + kt * P:j * S + (kt + 1) * P], ident16[:, :],
                                          w["masks"][:, 2 if kt == t else 3, :], start=False, stop=e == len(cols) - 1)
                    last.then_inc(mx_scores, 1)

                def max_transposes(m):
                    pe.wait_ge(mx_taken, (m + 3) * 8)
                    pe.wait_ge(o_out, (m + 2) * 4)
                    for half in range(2):
                        for g in (2 * half, 2 * half + 1):
                            for t in range(TT):
                                last = nc.tensor.transpose(
                                    psum[:, 6 + half, (g % 2) * S + t * P:(g % 2) * S + (t + 1) * P],
                                    w["m"][:, t, g, :], ident32[:, :])
                        last.then_inc(m_done, 1)

                def scores(m, u, g):
                    pe.wait_ge(q2_ready, (m + 2) * 2 + g // 2 + 1)
                    for kt in range(TT):
                        s_ = g * TT + kt
                        if s_ >= 2:
                            pe.wait_ge(ex_done, (m + 2) * 8 + s_ - 1)
                        qs = [t for t in range(TT) if kt in pairs(t)]
                        a0, a1 = qs[0] * P, (qs[-1] + 1) * P
                        for j in range(GH):
                            at = SC[s_ % 2][:, j * S + a0:j * S + a1]
                            ks = slice(kt * P, (kt + 1) * P)
                            mm(at, w["k1"][:, u, j, g, ks], w["q1"][:, u, g, a0:a1], start=True, stop=False)
                            for t in qs:
                                if t == kt or causal_band:
                                    mm(SC[s_ % 2][:, j * S + t * P:j * S + (t + 1) * P], ident16[:, :],
                                       w["masks"][:, 0 if t == kt else 1, :], start=False, stop=False)
                            last = mm(at, w["k2"][:, u, j, g, ks], w["q2"][:, g, a0:a1], start=False, stop=True)
                        last.then_inc(sc_done, 1)

                def values(m, u, g):
                    pe.wait_ge(ex_done, (m + 2) * 8 + g * 2 + 2)
                    if g == 0:
                        pe.wait_ge(q2_ready, (m + 3) * 2)
                        pe.wait_ge(proj_out, (m + 3) * 5)
                    if g >= 2:
                        pe.wait_ge(o_out, (m + 2) * 4 + g - 1)
                    for kt in range(TT):
                        q0 = kt * P if causal_band else 0
                        for j in range(GH):
                            last = mm(psum[j * SLOT:(j + 1) * SLOT, 6 + g % 2, q0:S],
                                      w["v"][:, u, kt, g * GH + j, :], w["pr"][:, g % 2, kt, j, q0:S],
                                      start=kt == 0, stop=kt == TT - 1, tile_position=(0, j * SLOT))
                    last.then_inc(av_done, 1)

                def body(m, u, more):
                    for s_ in range(8):
                        max_scores(m, u, s_)
                        if more and s_ == 1:
                            transposes(m + 1)
                        if more and s_ in (4, 6):
                            project(m + 1, s_ // 2 - 2)
                    if more:
                        project(m + 1, 2)
                    max_transposes(m)
                    if more:
                        project(m + 1, 3)
                    pe.wait_ge(q1_ready, m + 3)
                    pe.wait_ge(k2_ready, (m + 3) * (16 * GH))
                    for g in range(G):
                        scores(m, u, g)
                        if g:
                            values(m, u, g - 1)
                    values(m, u, G - 1)
                    pe.wait_ge(o_out, (m + 3) * 4)
                    for t in range(TT):
                        for g in range(G):
                            last = nc.tensor.transpose(psum[:, t, g * P:(g + 1) * P],
                                                       w["o"][:, g, t * P:(t + 1) * P], ident32[:, :])
                        last.then_inc(oT_done, 1)
                    if more:
                        project_v(m + 1)
                    pe.wait_ge(on_ready, (m + 3) * 2)
                    for c in range(KT):
                        for t in range(TT):
                            last = nc.tensor.transpose(psum[:, 2, c * S + t * P:c * S + (t + 1) * P],
                                                       w["on"][:, t, c * P:(c + 1) * P], ident32[:, :])
                    last.then_inc(on_T, 1)
                    pe.wait_ge(ol_ready, m + 3)
                    for t in range(TT):
                        y = psum[:, 3, t * D:(t + 1) * D]
                        k = 0
                        for c in range(KT):
                            for xs_, ws_ in ((0, 0), (0, 1), (1, 0)):
                                mm(y, w["oT"][:, xs_, c, t * P:(t + 1) * P], w["wo"][:, ws_, c, :],
                                   start=k == 0, stop=False)
                                k += 1
                        mm(y, w["ones"][0:1, :], w["bo"][0:1, 0, :], start=False, stop=False)
                        last = mm(y, w["ones"][0:1, :], w["bo"][0:1, 1, :], start=False, stop=True)
                    last.then_inc(y_done, 1)

                sequences(pe, ahead, body)

            @block.scalar
            def _(act):
                A = nc.scalar.activation

                def halves(m):
                    for n_, dst in enumerate(("xT", "cT")):
                        act.wait_ge(tr_done, (m + 2) * 2 + n_ + 1)
                        if n_ == 0:
                            act.wait_ge(proj_done, (m + 2) * 5)
                        A(w[dst][:, 0, :, :], psum[:, 4 + n_, :].rearrange("p (c s) -> p c s", c=KT),
                          ACT.Copy).then_inc(tr_hi, 1)

                def take(m, n_):
                    act.wait_ge(proj_done, (m + 2) * 5 + n_ + 1)
                    if n_ == 0:
                        act.wait_ge(kl_ready, m + 2)
                    if n_ == 2:
                        act.wait_ge(q1_ready, m + 2)
                    dst, bias = (w["kf"], w["bk"]) if n_ < 2 else (w["qf"], w["bq"])
                    for g in (n_ % 2 * 2, n_ % 2 * 2 + 1):
                        last = A(dst[:, g, :], psum[:, 4 + n_ % 2, (g % 2) * S:(g % 2 + 1) * S], ACT.Identity,
                                 bias=bias[:, g:g + 1])
                    last.then_inc(proj_out, 1)

                def upper_k(m):
                    if causal_band:
                        act.wait_ge(f_ready, (m + 2) * 2 + 1)
                    else:
                        act.wait_ge(proj_out, (m + 2) * 5 + 2)
                    act.wait_ge(k1_ready, (m + 2) * (16 * GH))
                    act.wait_ge(kl_ready, m + 2)
                    A(w["kh"][:, :, :], w["kf"][:, :, :], ACT.Copy).then_inc(qk_hi, 1)

                def upper_q(m, u):
                    if causal_band:
                        act.wait_ge(f_ready, (m + 3) * 2)
                    else:
                        act.wait_ge(proj_out, (m + 2) * 5 + 4)
                    act.wait_ge(q2_ready, (m + 1) * 2)
                    A(w["qh"][:, u, :, :], w["qf"][:, :, :], ACT.Copy).then_inc(qk_hi, 1)

                def take_v(m, u):
                    act.wait_ge(proj_done, (m + 3) * 5)
                    act.wait_ge(av_done, (m + 1) * 4)
                    A(w["v"][:, u, :, :, 0:DH], psum[:, 4, :].rearrange("p (t h d) -> p t h d", t=TT, h=H),
                      ACT.Copy).then_inc(proj_out, 1)

                def ahead(m, u):
                    halves(m)
                    take(m, 0)
                    take(m, 1)
                    upper_k(m)
                    take(m, 2)
                    take(m, 3)
                    upper_q(m, u)
                    take_v(m, u)

                def exps(m, g):
                    for kt in range(TT):
                        s_ = g * TT + kt
                        act.wait_ge(sc_done, (m + 2) * 8 + s_ + 1)
                        if g >= 2:
                            act.wait_ge(av_done, (m + 2) * 4 + g - 1)
                        else:
                            act.wait_ge(av_done, (m + 2) * 4)
                        a0 = kt * P if causal_band else 0
                        A(w["pr"][:, g % 2, kt, :, a0:S], SC[s_ % 2].rearrange("p (j s) -> p j s", j=GH)[:, :, a0:S],
                          ACT.Exp, scale=1.0 / math.sqrt(DH)).then_inc(ex_done, 1)

                def take_o(m, g):
                    act.wait_ge(av_done, (m + 2) * 4 + g + 1)
                    act.wait_ge(oT_done, (m + 2) * 2)
                    A(w["o"][:, g, :], psum[:, 6 + g % 2, 0:S], ACT.Copy).then_inc(o_out, 1)

                def body(m, u, more):
                    if more:
                        halves(m + 1)
                        take(m + 1, 0)
                        take(m + 1, 1)
                        if not causal_band:
                            upper_k(m + 1)
                        take(m + 1, 2)
                    exps(m, 0)
                    if more:
                        take(m + 1, 3)
                        if not causal_band:
                            upper_q(m + 1, 1 - u)
                    exps(m, 1)
                    take_o(m, 0)
                    if more and causal_band:
                        upper_k(m + 1)
                    exps(m, 2)
                    take_o(m, 1)
                    exps(m, 3)
                    take_o(m, 2)
                    take_o(m, 3)
                    if more and causal_band:
                        upper_q(m + 1, 1 - u)
                    if more:
                        take_v(m + 1, 1 - u)
                    act.wait_ge(on_T, m + 3)
                    for c in range(KT):
                        last = A(w["oT"][:, 0, c, :], psum[:, 2, c * S:(c + 1) * S], ACT.Identity,
                                 bias=w["bv"][:, c:c + 1])
                    last.then_inc(oh_ready, 1)

                sequences(act, ahead, body)

            @block.gpsimd
            def _(pool):
                with pool.Fori(0, B) as m:
                    pool.wait_ge(qk_hi, (m + 2) * 2 + 1)
                    pool.wait_ge(k2_ready, (m + 2) * (16 * GH))
                    pool.tensor_tensor(w["kl"][:, :, :], w["kf"][:, :, :], w["kh"][:, :, :],
                                       ALU.subtract).then_inc(kl_ready, 1)

            @block.vector
            def _(dve):
                V = nc.vector

                def norm(m):
                    dve.wait_ge(tr_done, (m + 2) * 2)
                    for t in range(TT):
                        last = V.tensor_scalar(w["xn"][:, t, :],
                                               x[:, bass.ds(m * TT + t, 1), :].rearrange("p a d -> p (a d)"),
                                               mv[:, bass.ds(m * TT + t, 1), 0], rstd[:, bass.ds(m * TT + t, 1)],
                                               ALU.subtract, ALU.mult)
                    last.then_inc(xn_ready, 1)

                def halves(m):
                    for n_, dst in enumerate(("xT", "cT")):
                        dve.wait_ge(tr_hi, (m + 2) * 2 + n_ + 1)
                        V.tensor_tensor(w[dst][:, 1, :, :], psum[:, 4 + n_, :].rearrange("p (c s) -> p c s", c=KT),
                                        w[dst][:, 0, :, :], ALU.subtract).then_inc(tr_lo, 1)

                def rotate(m, n_):
                    f_ = w[("kf", "qf")[n_]]
                    swap = [(r // DH) * DH + (r % DH + DH // 2) % DH for r in range(SLOT)]
                    hold(dve, proj_out, (m + 2) * 5 + 2 * n_ + 2)
                    hold(dve, f_ready, (m + 2) * 2 + n_)
                    V.stream_shuffle(w["rot"][:, :, :], f_[:, :, :], swap).then_inc(rope, 1)
                    dve.wait_ge(rope, (m + 2) * 6 + n_ * 3 + 1)
                    V.tensor_tensor(w["rot"][:, :, :], w["rot"][:, :, :],
                                    w["sin"][:, :].unsqueeze(1).broadcast_to([P, G, S]), ALU.mult).then_inc(rope, 1)
                    V.tensor_tensor(f_[:, :, :], f_[:, :, :],
                                    w["cos"][:, :].unsqueeze(1).broadcast_to([P, G, S]), ALU.mult).then_inc(rope, 1)
                    dve.wait_ge(rope, (m + 2) * 6 + n_ * 3 + 3)
                    V.tensor_tensor(f_[:, :, :], f_[:, :, :], w["rot"][:, :, :], ALU.add).then_inc(f_ready, 1)

                def mixed_q(m, u):
                    dve.wait_ge(qk_hi, (m + 3) * 2)
                    dve.wait_ge(sc_done, (m + 1) * 8)
                    V.scalar_tensor_tensor(w["q1"][:, u, :, :], w["qh"][:, u, :, :], w["hi_rows"][:, 0:1],
                                           w["qf"][:, :, :], ALU.mult, ALU.add).then_inc(q1_ready, 1)

                def ahead(m, u):
                    norm(m)
                    halves(m)
                    if causal_band:
                        rotate(m, 0)
                        rotate(m, 1)
                    mixed_q(m, u)

                def body(m, u, more):
                    if more:
                        norm(m + 1)
                    for s_ in range(8):
                        t, g = s_ // G, s_ % G
                        if more and s_ == 3:
                            halves(m + 1)
                        dve.wait_ge(mx_scores, (m + 2) * 8 + s_ + 1)
                        cols = pairs(t)
                        src = SC[s_ % 2].rearrange("p (j s) -> p j s", j=GH)[:, :, cols[0] * P:(cols[-1] + 1) * P]
                        V.tensor_reduce(w["m"][:, t, g, DH::SLOT], src, AX.X, ALU.max, negate=True).then_inc(mx_taken, 1)
                    for half in range(2):
                        dve.wait_ge(m_done, (m + 2) * 2 + half + 1)
                        V.scalar_tensor_tensor(w["q2"][:, 2 * half:2 * half + 2, :],
                                               w["qh"][:, u, 2 * half:2 * half + 2, :], w["hi_rows"][:, 1:2],
                                               psum[:, 6 + half, :].rearrange("p (g s) -> p g s", g=2),
                                               ALU.mult, ALU.add).then_inc(q2_ready, 1)
                    if more and causal_band:
                        rotate(m + 1, 0)
                        rotate(m + 1, 1)
                    if more and not causal_band:
                        mixed_q(m + 1, 1 - u)
                    for t in range(TT):
                        dve.wait_ge(oT_done, (m + 2) * 2 + t + 1)
                        heads = psum[:, t, :].rearrange("p (h r) -> p h r", r=SLOT)
                        V.reciprocal(w["rd"][:, t, :], heads[:, :, DH]).then_inc(rd_ready, 1)
                    for t in range(TT):
                        heads = psum[:, t, :].rearrange("p (h r) -> p h r", r=SLOT)
                        dve.wait_ge(rd_ready, (m + 2) * 2 + t + 1)
                        V.tensor_tensor(w["on"][:, t, :].rearrange("p (h d) -> p h d", h=H), heads[:, :, 0:DH],
                                        w["rd"][:, t, :].unsqueeze(2).broadcast_to([P, H, DH]),
                                        ALU.mult).then_inc(on_ready, 1)
                    if more and causal_band:
                        mixed_q(m + 1, 1 - u)
                    dve.wait_ge(oh_ready, m + 3)
                    for c in range(KT):
                        last = V.scalar_tensor_tensor(w["oT"][:, 1, c, :], psum[:, 2, c * S:(c + 1) * S],
                                                      w["bv"][:, c:c + 1], w["oT"][:, 0, c, :],
                                                      ALU.add, ALU.subtract)
                    last.then_inc(ol_ready, 1)
                    dve.wait_ge(y_done, m + 3)
                    for t in range(TT):
                        xt = x[:, bass.ds(m * TT + t, 1), :].rearrange("p a d -> p (a d)")
                        last = V.scalar_tensor_tensor(xt, psum[:, 3, t * D:(t + 1) * D], gate[:, 2 * L:2 * L + 1], xt,
                                                      ALU.mult, ALU.add)
                    last.then_inc(x_new, 1)
                    hold(dve, x_new, m + 3)
                    token_stats(dve, m, st_chain)

                sequences(dve, ahead, body)
        stack.close()

    def moe0():
        E0, F0 = 8, 896
        FT = F0 // P
        ROWS = B * CAP
        CH = 256
        NC = ROWS // CH
        CT = CH // P
        STEPS = E0 * NC
        WP = KT * F0
        disp = nc.dram_tensor("dispatched", (E0 * ROWS, D), F32, kind="Internal").ap()
        eo = nc.dram_tensor("expert_out", (E0 * ROWS, D), F32, kind="Internal").ap()
        stack = ExitStack()

        def sb(name, shape, dt):
            return stack.enter_context(nc.sbuf_tensor("m0_" + name, shape, dt))

        gidx = sb("gather_row", [P, NT, 2], U32)
        gw = sb("gather_weight", [P, NT, 2], F32)

        r = ExitStack()

        def rb(name, shape, dt):
            return r.enter_context(nc.sbuf_tensor("m0_" + name, shape, dt))

        zero = rb("zero", [P, 8, D], F32)
        xn = rb("xn", [P, NT, D], F32)
        xT = rb("xT32", [P, KT, RT * P], F32)
        gate_w = rb("router", [P, KT, E0], F32)
        tri = rb("tri", [P, 2, P], F16)
        iota = rb("iota", [P, E0], F32)
        base = rb("seq_base", [P, NT], F32)
        lg = rb("logits", [P, RT, E0], F32)
        mx = rb("row_max", [P, RT], F32)
        pr = rb("probs", [P, RT, E0], F32)
        rs = rb("row_sum", [P, RT], F32)
        top = rb("top", [P, RT, 8], F32)
        ti = rb("top_index", [P, RT, 8], U32)
        tf = rb("top_index_f", [P, RT, 2], F32)
        oh = rb("one_hot", [P, 2, RT, E0], F32)
        msk = rb("chosen", [P, RT, E0], F16)
        tmp = rb("picked", [P, 2, 2, RT, E0], F32)
        pk = rb("picked_sum", [P, 2, 2, RT], F32)
        keep = rb("kept", [P, 2, RT], F32)
        row = rb("row", [P, 2, RT], F32)
        far = rb("row_or_far", [P, 2, RT], F32)
        sidx = rb("scatter_row", [P, 2, NT], U32)
        ld = sem("m0_loaded")
        zr = sem("m0_zeroed")
        zset = sem("m0_zero_set")
        xn_ready = sem("m0_xn_ready")
        xT_done = sem("m0_xT_done")
        xT_out = sem("m0_xT_out")
        lg_done = sem("m0_logits_done")
        sh_ready = sem("m0_shifted")
        ex_ready = sem("m0_exp")
        m_ready = sem("m0_chosen")
        pos_done = sem("m0_positions")
        idx_ready = sem("m0_rows_ready")
        sent = sem("m0_sent")
        ch = sem("m0_chain")
        with nc.Block() as block:

            @block.sync
            def _(sp):
                sp.dma_start(gate_w[:, :, :], a["L0_router"]).then_inc(ld, 16)
                sp.dma_start(tri[:, :, :], a["tri"]).then_inc(ld, 16)
                sp.dma_start(iota[:, :], a["iota"][:, 0:E0]).then_inc(ld, 16)
                sp.dma_start(base[:, :], a["seq_base"]).then_inc(ld, 16)
                sp.wait_ge(ld, 64)

            @block.gpsimd
            def _(pool):
                pool.memset(zero[:, :, :], 0.0).then_inc(zset, 1)

        with nc.Block() as block:

            @block.sync
            def _(sp):
                for c in range(E0 * ROWS // (P * 8)):
                    sp.dma_start(disp[c * P * 8:(c + 1) * P * 8, :].rearrange("(p t) d -> p t d", p=P),
                                 zero[:, :, :]).then_inc(zr, 16)

            @block.tensor
            def _(pe):
                def transposes(n):
                    pe.wait_ge(xn_ready, n + 1)
                    if n:
                        pe.wait_ge(xT_out, n)
                    for c in range(KT):
                        for t in range(RT):
                            col = c * RT + t
                            last = nc.tensor.transpose(
                                psum[:, col // 4, (col % 4) * P:(col % 4 + 1) * P],
                                xn[:, n * RT + t, c * P:(c + 1) * P], ident32[:, :])
                    last.then_inc(xT_done, 1)

                transposes(0)
                for n in range(RG):
                    pe.wait_ge(xT_out, n + 1)
                    if n:
                        pe.wait_ge(sh_ready, n)
                    for t in range(RT):
                        for c in range(KT):
                            last = nc.tensor.matmul(psum[:, 4, t * E0:(t + 1) * E0], xT[:, c, t * P:(t + 1) * P],
                                                    gate_w[:, c, :], start=c == 0, stop=c == KT - 1)
                    last.then_inc(lg_done, 1)
                    if n + 1 < RG:
                        transposes(n + 1)
                    by = msk[:, :, :].rearrange("p (b t) e -> p t b e", t=TT)
                    half = RT // TT * E0
                    pe.wait_ge(m_ready, n + 1)
                    nc.tensor.matmul(psum[:, 5, 0:half], tri[:, 0, :], by[:, 0, :, :], start=True, stop=True)
                    nc.tensor.matmul(psum[:, 5, half:2 * half], tri[:, 0, :], by[:, 1, :, :], start=True, stop=False)
                    nc.tensor.matmul(psum[:, 5, half:2 * half], tri[:, 1, :], by[:, 0, :, :], start=False,
                                     stop=True).then_inc(pos_done, 1)

            @block.scalar
            def _(act):
                def take(n):
                    act.wait_ge(xT_done, n + 1)
                    if n:
                        act.wait_ge(lg_done, n)
                    nc.scalar.activation(xT[:, :, :], psum[:, 0:4, :].rearrange("p b s -> p (b s)")
                                         .rearrange("p (c s) -> p c s", c=KT), ACT.Copy).then_inc(xT_out, 1)

                take(0)
                for n in range(RG):
                    if n + 1 < RG:
                        take(n + 1)
                    act.wait_ge(sh_ready, n + 1)
                    nc.scalar.activation(pr[:, :, :], lg[:, :, :], ACT.Exp).then_inc(ex_ready, 1)

            @block.gpsimd
            def _(pool):
                pool.wait_ge(zr, 16 * (E0 * ROWS // (P * 8)))
                for t in range(NT):
                    pool.wait_ge(idx_ready, t // RT + 1)
                    for k in range(2):
                        pool.indirect_dma_start(disp, bass.IndirectOffsetOnAxis(ap=sidx[:, k, t:t + 1], axis=0),
                                                xn[:, t, :], None, bounds_check=E0 * ROWS - 1, oob_is_err=False)\
                            .then_inc(sent, 16)
                pool.wait_ge(sent, 2 * NT * 16)

            @block.vector
            def _(dve):
                V = nc.vector

                def normalise(n):
                    for t in range(RT):
                        nt = n * RT + t
                        last = V.tensor_scalar(xn[:, nt, :], x[:, nt, :], mv[:, nt, 0:1], rstd[:, nt:nt + 1],
                                               ALU.subtract, ALU.mult)
                    last.then_inc(xn_ready, 1)

                steps = 0

                def link(ins):
                    nonlocal steps
                    steps += 1
                    ins.then_inc(ch, 1)
                    dve.wait_ge(ch, steps)

                normalise(0)
                for n in range(RG):
                    here = slice(n * RT, (n + 1) * RT)
                    if n + 1 < RG:
                        normalise(n + 1)
                    logits = psum[:, 4, 0:RT * E0].rearrange("p (t e) -> p t e", e=E0)
                    dve.wait_ge(lg_done, n + 1)
                    link(V.tensor_reduce(mx[:, :], logits, AX.X, ALU.max))
                    V.tensor_tensor(lg[:, :, :], logits, mx[:, :].unsqueeze(2).broadcast_to([P, RT, E0]),
                                    ALU.subtract).then_inc(sh_ready, 1)
                    dve.wait_ge(ex_ready, n + 1)
                    link(V.tensor_reduce(rs[:, :], pr[:, :, :], AX.X, ALU.add))
                    link(V.reciprocal(rs[:, :], rs[:, :]))
                    link(V.tensor_tensor(pr[:, :, :], pr[:, :, :], rs[:, :].unsqueeze(2).broadcast_to([P, RT, E0]),
                                         ALU.mult))
                    for t in range(RT):
                        last = V.max(top[:, t, :], pr[:, t, :])
                    link(last)
                    for t in range(RT):
                        last = V.max_index(ti[:, t, :], top[:, t, :], pr[:, t, :])
                    link(last)
                    link(V.tensor_copy(tf[:, :, :], ti[:, :, 0:2]))
                    for k in range(2):
                        last = V.tensor_tensor(oh[:, k, :, :], iota[:, :].unsqueeze(1).broadcast_to([P, RT, E0]),
                                               tf[:, :, k:k + 1].broadcast_to([P, RT, E0]), ALU.is_equal)
                    link(last)
                    V.tensor_tensor(msk[:, :, :], oh[:, 0, :, :], oh[:, 1, :, :], ALU.add).then_inc(m_ready, 1)
                    for k in range(2):
                        V.tensor_tensor(tmp[:, 1, k, :, :], oh[:, k, :, :], pr[:, :, :], ALU.mult)
                    dve.wait_ge(pos_done, n + 1)
                    for k in range(2):
                        last = V.tensor_tensor(tmp[:, 0, k, :, :].rearrange("p (b t) e -> p t b e", t=TT),
                                               oh[:, k, :, :].rearrange("p (b t) e -> p t b e", t=TT),
                                               psum[:, 5, 0:RT * E0].rearrange("p (t b e) -> p t b e", t=TT, e=E0),
                                               ALU.mult)
                    link(last)
                    link(V.tensor_reduce(pk[:, :, :, :].rearrange("p a k t -> p (a k t)"),
                                         tmp[:, :, :, :, :].rearrange("p a k t e -> p (a k t) e"), AX.X, ALU.add))
                    V.tensor_scalar(keep[:, :, :], pk[:, 0, :, :], float(CAP), None, ALU.is_le)
                    link(V.scalar_tensor_tensor(row[:, :, :], tf[:, :, :].rearrange("p t k -> p k t"), float(ROWS),
                                                pk[:, 0, :, :], ALU.mult, ALU.add))
                    link(V.tensor_tensor(row[:, :, :], row[:, :, :],
                                         base[:, here].unsqueeze(1).broadcast_to([P, 2, RT]), ALU.add))
                    link(V.tensor_scalar(far[:, :, :], keep[:, :, :], -float(1 << 20), float(1 << 20),
                                         ALU.mult, ALU.add))
                    V.tensor_tensor(sidx[:, :, here], row[:, :, :], far[:, :, :],
                                    ALU.add).then_inc(idx_ready, 1)
                    V.tensor_tensor(gidx[:, here, :].rearrange("p t k -> p k t"), row[:, :, :],
                                    keep[:, :, :], ALU.mult)
                    link(V.tensor_tensor(pk[:, 1, :, :], pk[:, 1, :, :], keep[:, :, :], ALU.mult))
                    link(V.tensor_scalar(gw[:, here, :].rearrange("p t k -> p k t"), pk[:, 1, :, :],
                                         gate[:, 1:2], None, ALU.mult))
        r.close()

        f = ExitStack()

        def fb(name, shape, dt):
            return f.enter_context(nc.sbuf_tensor("m0_" + name, shape, dt))

        wl = fb("w_load", [P, 3, WP], F32)
        wh = fb("w_halves", [P, 2, 2, 3, WP], F16)
        rows = fb("rows", [P, CT, D], F32)
        xT = fb("xT", [P, 2, 2, KT, ROWS], F16)
        hsb = fb("silu", [P, 2, CH], F32)
        hp = fb("hidden", [P, 2, CH], F32)
        hT = fb("hiddenT", [P, 2, FT, CH], F16)
        y = fb("y", [P, CT, D], F32)
        w_dram = [a["L0_w1"], a["L0_w3"], a["L0_w2"]]
        w_loaded = sem("m0f_w_loaded")
        w_hi = sem("m0f_w_hi")
        w_lo = sem("m0f_w_lo")
        rows_in = sem("m0f_rows_in")
        rT_done = sem("m0f_rows_transposed")
        xT_hi = sem("m0f_xT_hi")
        xT_lo = sem("m0f_xT_lo")
        h_done = sem("m0f_h_done")
        s_done = sem("m0f_silu")
        g_done = sem("m0f_gated")
        hh = sem("m0f_hidden_hi")
        hl = sem("m0f_hidden_lo")
        y_done = sem("m0f_y_done")
        y_out = sem("m0f_y_out")
        y_sent = sem("m0f_y_sent")
        y_free = sem("m0f_y_free")
        with nc.Block() as block:

            @block.sync
            def _(sp):
                for counter, number in ((w_loaded, 48), (w_hi, 3), (w_lo, 3), (rows_in, 16), (rT_done, 1),
                                        (xT_hi, 1), (xT_lo, 1), (h_done, FT), (s_done, FT), (g_done, FT), (hh, FT),
                                        (hl, FT), (y_done, 1), (y_out, 1), (y_free, 1)):
                    sp.sem_inc(counter, number)

        def both_(eng, prepare, compute, e, u, c, n):
            compute(u, c, n, lambda: prepare(e + 1, 1 - u, c, n + NC))

        with nc.Block() as block:

            @block.sync
            def _(sp):
                with sp.Fori(0, E0) as e:
                    hold(sp, w_lo, (e + 1) * 3)
                    for m in range(3):
                        sp.dma_start(wl[:, m, :], w_dram[m][e, :, :]).then_inc(w_loaded, 16)
                    with sp.Fori(0, NC) as c:
                        q = e * NC + c
                        hold(sp, rT_done, q + 1)
                        sp.dma_start(rows[:, :, :],
                                     disp[bass.ds(q * CH, CH), :].rearrange("(t p) d -> p t d", p=P))\
                            .then_inc(rows_in, 16)

            @block.gpsimd
            def _(pool):
                with pool.Fori(0, STEPS) as n:
                    hold(pool, y_out, n + 2)
                    pool.dma_start(eo[bass.ds(n * CH, CH), :].rearrange("(t p) d -> p t d", p=P), y[:, :, :])\
                        .then_inc(y_sent, 16)
                    hold(pool, y_sent, (n + 1) * 16)
                    pool.sem_inc(y_free, 1)

            @block.tensor
            def _(pe):
                mm = nc.tensor.matmul

                def prepare(e, u, c, q):
                    pe.wait_ge(rows_in, (q + 2) * 16)
                    pe.wait_ge(xT_lo, q + 1)
                    for d_ in range(KT):
                        for t in range(CT):
                            last = nc.tensor.transpose(psum[:, 3, d_ * CH + t * P:d_ * CH + (t + 1) * P],
                                                       rows[:, t, d_ * P:(d_ + 1) * P], ident32[:, :])
                    last.then_inc(rT_done, 1)

                def compute(u, c, n, fill):
                    pe.wait_ge(xT_lo, n + 2)

                    def hidden(f_):
                        if f_ >= 3:
                            pe.wait_ge(g_done, (n + 1) * FT + f_ - 2)
                        else:
                            pe.wait_ge(g_done, (n + 1) * FT)
                        for m in range(2):
                            k = 0
                            for d_ in range(KT):
                                for ws_, xs_ in ((0, 0), (0, 1), (1, 0)):
                                    last = mm(psum[:, f_ % 3, m * CH:(m + 1) * CH],
                                              wh[:, u, ws_, m, d_ * F0 + f_ * P:d_ * F0 + (f_ + 1) * P],
                                              xT[:, u, xs_, d_, bass.ds(c * CH, CH)],
                                              start=k == 0, stop=k == 5)
                                    k += 1
                        last.then_inc(h_done, 1)

                    def down(f_):
                        pe.wait_ge(hl, (n + 1) * FT + f_ + 1)
                        if f_ == 0:
                            pe.wait_ge(y_out, n + 1)
                        for t in range(CT):
                            k = 0
                            for hs_, ws_ in ((0, 0), (0, 1), (1, 0)):
                                last = mm(psum[:, 4 + t, 0:D], hT[:, hs_, f_, t * P:(t + 1) * P],
                                          wh[:, u, ws_, 2, f_ * D:(f_ + 1) * D],
                                          start=f_ == 0 and k == 0, stop=f_ == FT - 1 and k == 2)
                                k += 1
                        if f_ == FT - 1:
                            last.then_inc(y_done, 1)

                    for f_ in range(FT):
                        hidden(f_)
                        if f_ >= 2:
                            down(f_ - 2)
                    fill()
                    down(FT - 2)
                    down(FT - 1)

                with pe.Fori(0, NC) as c:
                    prepare(0, 0, c, c)
                pe.wait_ge(w_lo, 6)
                with pe.Fori(0, E0 // 2 - 1) as i:
                    for u in range(2):
                        hold(pe, w_lo, (i * 2 + u + 2) * 3)
                        with pe.Fori(0, NC) as c:
                            both_(pe, prepare, compute, i * 2 + u, u, c, (i * 2 + u) * NC + c)
                pe.wait_ge(w_lo, E0 * 3)
                with pe.Fori(0, NC) as c:
                    both_(pe, prepare, compute, E0 - 2, 0, c, (E0 - 2) * NC + c)
                pe.wait_ge(w_lo, (E0 + 1) * 3)
                with pe.Fori(0, NC) as c:
                    compute(1, c, (E0 - 1) * NC + c, lambda: None)

            @block.scalar
            def _(act):
                A = nc.scalar.activation

                def prepare(e, u, c, q):
                    act.wait_ge(rT_done, q + 2)
                    A(xT[:, u, 0, :, bass.ds(c * CH, CH)], psum[:, 3, :].rearrange("p (c s) -> p c s", c=KT),
                      ACT.Copy).then_inc(xT_hi, 1)

                def weights(e, u):
                    for m in range(3):
                        act.wait_ge(w_loaded, (e + 2) * 48)
                        A(wh[:, u, 0, m, :], wl[:, m, :], ACT.Copy).then_inc(w_hi, 1)

                def compute(u, c, n, fill):
                    for f_ in range(FT):
                        act.wait_ge(h_done, (n + 1) * FT + f_ + 1)
                        act.wait_ge(g_done, (n + 1) * FT + f_ - 1)
                        A(hsb[:, f_ % 2, :], psum[:, f_ % 3, 0:CH], ACT.Silu).then_inc(s_done, 1)
                        upper(n, f_)
                    fill()

                def upper(n, f_):
                    act.wait_ge(g_done, (n + 1) * FT + f_ + 1)
                    if f_ == 0:
                        act.wait_ge(y_done, n + 1)
                    A(hT[:, 0, f_, :], hp[:, f_ % 2, :], ACT.Copy).then_inc(hh, 1)

                weights(0, 0)
                with act.Fori(0, NC) as c:
                    prepare(0, 0, c, c)
                with act.Fori(0, E0 // 2 - 1) as i:
                    for u in range(2):
                        act.wait_ge(y_done, (i * 2 + u) * NC + 1)
                        weights(i * 2 + u + 1, 1 - u)
                        with act.Fori(0, NC) as c:
                            both_(act, prepare, compute, i * 2 + u, u, c, (i * 2 + u) * NC + c)
                act.wait_ge(y_done, (E0 - 2) * NC + 1)
                weights(E0 - 1, 1)
                with act.Fori(0, NC) as c:
                    both_(act, prepare, compute, E0 - 2, 0, c, (E0 - 2) * NC + c)
                with act.Fori(0, NC) as c:
                    compute(1, c, (E0 - 1) * NC + c, lambda: None)

            @block.vector
            def _(dve):
                V = nc.vector

                def prepare(e, u, c, q):
                    dve.wait_ge(xT_hi, q + 2)
                    V.tensor_tensor(xT[:, u, 1, :, bass.ds(c * CH, CH)],
                                    psum[:, 3, :].rearrange("p (c s) -> p c s", c=KT),
                                    xT[:, u, 0, :, bass.ds(c * CH, CH)], ALU.subtract).then_inc(xT_lo, 1)

                def weights(e, u):
                    for m in range(3):
                        dve.wait_ge(w_hi, (e + 1) * 3 + m + 1)
                        V.tensor_tensor(wh[:, u, 1, m, :], wl[:, m, :], wh[:, u, 0, m, :],
                                        ALU.subtract).then_inc(w_lo, 1)

                def lower(n, f_):
                    dve.wait_ge(hh, (n + 1) * FT + f_ + 1)
                    V.tensor_tensor(hT[:, 1, f_, :], hp[:, f_ % 2, :], hT[:, 0, f_, :], ALU.subtract).then_inc(hl, 1)

                def compute(u, c, n, fill):
                    for f_ in range(FT):
                        dve.wait_ge(s_done, (n + 1) * FT + f_ + 1)
                        dve.wait_ge(hl, (n + 1) * FT + f_ - 1)
                        V.tensor_tensor(hp[:, f_ % 2, :], psum[:, f_ % 3, CH:2 * CH], hsb[:, f_ % 2, :],
                                        ALU.mult).then_inc(g_done, 1)
                        lower(n, f_)
                    fill()
                    dve.wait_ge(y_done, n + 2)
                    dve.wait_ge(y_free, n + 1)
                    V.tensor_copy(y[:, :, :], psum[:, 4:4 + CT, 0:D]).then_inc(y_out, 1)

                weights(0, 0)
                with dve.Fori(0, NC) as c:
                    prepare(0, 0, c, c)
                with dve.Fori(0, E0 // 2 - 1) as i:
                    for u in range(2):
                        weights(i * 2 + u + 1, 1 - u)
                        with dve.Fori(0, NC) as c:
                            both_(dve, prepare, compute, i * 2 + u, u, c, (i * 2 + u) * NC + c)
                weights(E0 - 1, 1)
                with dve.Fori(0, NC) as c:
                    both_(dve, prepare, compute, E0 - 2, 0, c, (E0 - 2) * NC + c)
                with dve.Fori(0, NC) as c:
                    compute(1, c, (E0 - 1) * NC + c, lambda: None)
        f.close()

        g_ = ExitStack()
        NB = 4
        yb = g_.enter_context(nc.sbuf_tensor("m0_gathered", [P, NB, TT, 2, D], F32))
        gi = g_.enter_context(nc.sbuf_tensor("m0_rows_of_seq", [P, NB, TT, 2], U32))
        gi_ready = sem("m0g_rows")
        got = [sem(f"m0g_gathered{u}") for u in range(NB)]
        used = sem("m0g_used")
        st_chain = sem("m0g_stats")
        with nc.Block() as block:

            @block.sync
            def _(sp):
                for counter, number in ((gi_ready, 1), (used, NB * 2 * TT), (st_chain, 5)):
                    sp.sem_inc(counter, number)

        with nc.Block() as block:

            @block.gpsimd
            def _(pool):
                with pool.Fori(0, B // NB) as i:
                    for u in range(NB):
                        n = i * NB + u
                        hold(pool, used, (n + 1) * 2 * TT)
                        pool.tensor_copy(gi[:, u, :, :], gidx[:, bass.ds(n * TT, TT), :]).then_inc(gi_ready, 1)
                        hold(pool, gi_ready, n + 2)
                        for t in range(TT):
                            for k in range(2):
                                pool.indirect_dma_start(
                                    yb[:, u, t, k, :], None, eo,
                                    bass.IndirectOffsetOnAxis(ap=gi[:, u, t, k:k + 1], axis=0)).then_inc(got[u], 16)

            @block.vector
            def _(dve):
                with dve.Fori(0, B // NB) as i:
                    for u in range(NB):
                        n = i * NB + u
                        dve.wait_ge(got[u], (i + 1) * 64)
                        for k in range(2):
                            for t in range(TT):
                                xt = x[:, bass.ds(n * TT + t, 1), :].rearrange("p a d -> p (a d)")
                                nc.vector.scalar_tensor_tensor(xt, yb[:, u, t, k, :],
                                                               gw[:, bass.ds(n * TT + t, 1), k], xt,
                                                               ALU.mult, ALU.add).then_inc(used, 1)
                            hold(dve, used, (n + NB) * 2 * TT + (k + 1) * TT)
                        token_stats(dve, n, st_chain)
        g_.close()
        stack.close()

    def moe1():
        E1, K1, NG = 16, 4, 4
        EG = E1 // NG
        NE = E1 + 2
        CH = 512
        CT = CH // P
        NC = B * S // CH
        WE = (2 * KT + 2) * P
        SCALE = 2.5
        stack = ExitStack()

        def sb(name, shape, dt):
            return stack.enter_context(nc.sbuf_tensor("m1_" + name, shape, dt))

        ew = sb("expert_weight", [P, NT, NE], F32)
        xTa = sb("xT_all", [P, 2, KT, B * S], F16)
        wh = sb("w_halves", [P, 2, NE, WE], F16)
        NL = 3
        r = ExitStack()

        def rb(name, shape, dt):
            return r.enter_context(nc.sbuf_tensor("m1_" + name, shape, dt))

        wl = rb("w_load", [P, NE // NL, WE], F32)
        xn = rb("xn", [P, 2, RT, D], F32)
        xT = rb("xT32", [P, KT, RT * P], F32)
        router = rb("router", [P, KT, E1], F32)
        e_bias = rb("e_bias", [P, E1], F32)
        iota = rb("iota", [P, E1], F32)
        less = rb("less", [P, NG, NG], F32)
        sg = rb("scores", [P, RT, E1], F32)
        sc = rb("biased", [P, RT, E1], F32)
        hi2 = rb("pair_max", [P, RT * NG, 2], F32)
        lo2 = rb("pair_min", [P, RT * NG, 2], F32)
        g1 = rb("group_first", [P, RT * NG], F32)
        g2 = rb("group_second", [P, RT * NG], F32)
        g3 = rb("group_third", [P, RT * NG], F32)
        gt = rb("above", [P, RT, NG, NG], F32)
        eq = rb("equal", [P, RT, NG, NG], F32)
        rank = rb("rank", [P, RT, NG], F32)
        top = rb("top", [P, RT, 8], F32)
        ti = rb("top_index", [P, RT, 8], U32)
        tf = rb("top_index_f", [P, RT, K1], F32)
        oh = rb("one_hot", [P, RT, K1, E1], F32)
        sel = rb("chosen", [P, RT, E1], F32)
        den = rb("denominator", [P, RT], F32)
        transposed = psum[:, 0:4, :].rearrange("p b s -> p (b s)").rearrange("p (c s) -> p c s", c=KT)
        ld = sem("m1_loaded")
        w_loaded = sem("m1_w_loaded")
        w_hi = sem("m1_w_hi")
        w_lo = sem("m1_w_lo")
        xn_ready = sem("m1_xn_ready")
        xT_done = sem("m1_xT_done")
        xT_out = sem("m1_xT_out")
        xT_hi = sem("m1_xT_hi")
        xT_lo = sem("m1_xT_lo")
        lg_done = sem("m1_logits_done")
        sg_ready = sem("m1_scores")
        ch = sem("m1_chain")
        ew_chain = sem("m1_weights_chain")
        with nc.Block() as block:

            @block.sync
            def _(sp):
                for dst, k in ((router[:, :, :], "L1_router"), (e_bias[:, :], "L1_e_bias"), (iota[:, :], "iota"),
                               (less[:, :, :], "less")):
                    sp.dma_start(dst, a[k]).then_inc(ld, 16)
                sp.wait_ge(ld, 64)

            @block.vector
            def _(dve):
                nc.vector.tensor_scalar(ew[:, :, E1:NE], mv[:, :, 0:NE - E1], 0.0, gate[:, 3:4], ALU.mult, ALU.add)

        with nc.Block() as block:

            @block.sync
            def _(sp):
                n = NE // NL
                for c in range(NL):
                    if c:
                        sp.wait_ge(w_lo, c)
                    sp.dma_start(wl[:, :, :], a["L1_experts"][:, c * n:(c + 1) * n, :]).then_inc(w_loaded, 16)

            @block.tensor
            def _(pe):
                def transposes(n):
                    pe.wait_ge(xn_ready, n + 1)
                    if n:
                        pe.wait_ge(xT_lo, n)
                    for c in range(KT):
                        for t in range(RT):
                            col = c * RT + t
                            last = nc.tensor.transpose(psum[:, col // 4, (col % 4) * P:(col % 4 + 1) * P],
                                                       xn[:, n % 2, t, c * P:(c + 1) * P], ident32[:, :])
                    last.then_inc(xT_done, 1)

                transposes(0)
                for n in range(RG):
                    pe.wait_ge(xT_out, n + 1)
                    if n:
                        pe.wait_ge(sg_ready, n)
                    for t in range(RT):
                        for c in range(KT):
                            last = nc.tensor.matmul(psum[:, 4, t * E1:(t + 1) * E1], xT[:, c, t * P:(t + 1) * P],
                                                    router[:, c, :], start=c == 0, stop=c == KT - 1)
                    last.then_inc(lg_done, 1)
                    if n + 1 < RG:
                        transposes(n + 1)

            @block.scalar
            def _(act):
                A = nc.scalar.activation
                n_ = NE // NL
                for c in range(NL):
                    act.wait_ge(w_loaded, 16 * (c + 1))
                    A(wh[:, 0, c * n_:(c + 1) * n_, :], wl[:, :, :], ACT.Copy).then_inc(w_hi, 1)
                for n in range(RG):
                    act.wait_ge(xT_done, n + 1)
                    if n:
                        act.wait_ge(lg_done, n)
                    A(xT[:, :, :], transposed, ACT.Copy).then_inc(xT_out, 1)
                    A(xTa[:, 0, :, n * RT * P:(n + 1) * RT * P], transposed, ACT.Copy).then_inc(xT_hi, 1)
                    act.wait_ge(lg_done, n + 1)
                    if n:
                        act.wait_ge(ew_chain, n)
                    A(sg[:, :, :], psum[:, 4, 0:RT * E1].rearrange("p (t e) -> p t e", e=E1),
                      ACT.Sigmoid).then_inc(sg_ready, 1)

            @block.vector
            def _(dve):
                V = nc.vector
                n_ = NE // NL
                for c in range(NL):
                    dve.wait_ge(w_hi, c + 1)
                    V.tensor_tensor(wh[:, 1, c * n_:(c + 1) * n_, :], wl[:, :, :], wh[:, 0, c * n_:(c + 1) * n_, :],
                                    ALU.subtract).then_inc(w_lo, 1)
                steps = 0

                def link(ins):
                    nonlocal steps
                    steps += 1
                    ins.then_inc(ch, 1)
                    dve.wait_ge(ch, steps)

                def normalise(n):
                    if n > 1:
                        dve.wait_ge(xT_done, n - 1)
                    for t in range(RT):
                        nt = n * RT + t
                        last = V.tensor_scalar(xn[:, n % 2, t, :], x[:, nt, :], mv[:, nt, 0:1], rstd[:, nt:nt + 1],
                                               ALU.subtract, ALU.mult)
                    last.then_inc(xn_ready, 1)

                normalise(0)
                for n in range(RG):
                    here = slice(n * RT * P, (n + 1) * RT * P)
                    dve.wait_ge(xT_hi, n + 1)
                    V.tensor_tensor(xTa[:, 1, :, here], transposed, xTa[:, 0, :, here], ALU.subtract)\
                     .then_inc(xT_lo, 1)
                    if n + 1 < RG:
                        normalise(n + 1)
                    dve.wait_ge(sg_ready, n + 1)
                    link(V.tensor_tensor(sc[:, :, :], sg[:, :, :], e_bias[:, :].unsqueeze(1)
                                         .broadcast_to([P, RT, E1]), ALU.add))
                    four = sc[:, :, :].rearrange("p t (g h r) -> p (t g) h r", h=2, r=2)
                    V.tensor_tensor(hi2[:, :, :], four[:, :, :, 0], four[:, :, :, 1], ALU.max)
                    link(V.tensor_tensor(lo2[:, :, :], four[:, :, :, 0], four[:, :, :, 1], ALU.min))
                    V.tensor_tensor(g1[:, :], hi2[:, :, 0], hi2[:, :, 1], ALU.max)
                    V.tensor_tensor(g2[:, :], hi2[:, :, 0], hi2[:, :, 1], ALU.min)
                    link(V.tensor_tensor(g3[:, :], lo2[:, :, 0], lo2[:, :, 1], ALU.max))
                    link(V.tensor_tensor(g2[:, :], g2[:, :], g3[:, :], ALU.max))
                    link(V.tensor_tensor(g1[:, :], g1[:, :], g2[:, :], ALU.add))
                    gs = g1[:, :].rearrange("p (t g) -> p t g", g=NG)
                    other = gs.unsqueeze(2).broadcast_to([P, RT, NG, NG])
                    own = gs.unsqueeze(3).broadcast_to([P, RT, NG, NG])
                    V.tensor_tensor(gt[:, :, :, :], other, own, ALU.is_gt)
                    link(V.tensor_tensor(eq[:, :, :, :], other, own, ALU.is_equal))
                    link(V.tensor_tensor(eq[:, :, :, :], eq[:, :, :, :],
                                         less[:, :, :].unsqueeze(1).broadcast_to([P, RT, NG, NG]), ALU.mult))
                    link(V.tensor_tensor(gt[:, :, :, :], gt[:, :, :, :], eq[:, :, :, :], ALU.add))
                    link(V.tensor_reduce(rank[:, :, :], gt[:, :, :, :], AX.X, ALU.add))
                    link(V.tensor_scalar(rank[:, :, :], rank[:, :, :], 1.5, None, ALU.is_lt))
                    link(V.tensor_tensor(sc[:, :, :].rearrange("p t (g h) -> p t g h", g=NG),
                                         sc[:, :, :].rearrange("p t (g h) -> p t g h", g=NG),
                                         rank[:, :, :].unsqueeze(3).broadcast_to([P, RT, NG, EG]), ALU.mult))
                    link(V.tensor_scalar(sc[:, :, :], sc[:, :, :], 0.0, None, ALU.add))
                    for t in range(RT):
                        last = V.max(top[:, t, :], sc[:, t, :])
                    link(last)
                    for t in range(RT):
                        last = V.max_index(ti[:, t, :], top[:, t, :], sc[:, t, :])
                    link(last)
                    link(V.tensor_copy(tf[:, :, :], ti[:, :, 0:K1]))
                    link(V.tensor_tensor(oh[:, :, :, :],
                                         iota[:, :].unsqueeze(1).unsqueeze(1).broadcast_to([P, RT, K1, E1]),
                                         tf[:, :, :].unsqueeze(3).broadcast_to([P, RT, K1, E1]), ALU.is_equal))
                    link(V.tensor_reduce(sel[:, :, :], oh[:, :, :, :].rearrange("p t k e -> p t e k"), AX.X, ALU.add))
                    link(V.tensor_tensor(sel[:, :, :], sel[:, :, :], sg[:, :, :], ALU.mult))
                    link(V.tensor_reduce(den[:, :], sel[:, :, :], AX.X, ALU.add))
                    link(V.tensor_scalar(den[:, :], den[:, :], 1e-20, None, ALU.add))
                    link(V.reciprocal(den[:, :], den[:, :]))
                    V.tensor_tensor(sel[:, :, :], sel[:, :, :], den[:, :].unsqueeze(2).broadcast_to([P, RT, E1]),
                                    ALU.mult).then_inc(ew_chain, 1)
                    dve.wait_ge(ew_chain, n + 1)
                    V.tensor_scalar(ew[:, n * RT:(n + 1) * RT, 0:E1], sel[:, :, :], SCALE, gate[:, 3:4],
                                    ALU.mult, ALU.mult)
        r.close()

        f = ExitStack()

        def fb(name, shape, dt):
            return f.enter_context(nc.sbuf_tensor("m1_" + name, shape, dt))

        hsb = fb("silu", [P, 3, CH], F32)
        hp = fb("hidden", [P, 3, CH], F32)
        hT = fb("hiddenT", [P, 3, 2, CH], F16)
        h_done = sem("m1f_h_done")
        s_done = sem("m1f_silu")
        g_done = sem("m1f_gated")
        hh = sem("m1f_hidden_hi")
        hl = sem("m1f_hidden_lo")
        y_done = sem("m1f_y_done")
        y_add = sem("m1f_y_added")
        with nc.Block() as block:

            @block.sync
            def _(sp):
                for counter, number in ((h_done, 3), (s_done, 3), (g_done, 3), (hh, 3), (hl, 3), (y_done, 3),
                                        (y_add, 3 * CT)):
                    sp.sem_inc(counter, number)

        def steps(eng, head, tail):
            with eng.Fori(0, NC) as c:
                for e in range(2):
                    head(c, e, e, c * NE + e)
                with eng.Fori(0, NE // 3 - 1) as j:
                    for u in range(3):
                        head(c, j * 3 + u + 2, (u + 2) % 3, c * NE + j * 3 + u + 2)
                        tail(c, j * 3 + u, u, c * NE + j * 3 + u)
                head(c, NE - 1, 2, c * NE + NE - 1)
                for u in range(3):
                    tail(c, NE - 3 + u, u, c * NE + NE - 3 + u)

        with nc.Block() as block:

            @block.tensor
            def _(pe):
                mm = nc.tensor.matmul

                def wt(half, e, m):
                    return wh[:, half, bass.ds(e, 1), m * P:(m + 1) * P].rearrange("p a n -> p (a n)")

                def hidden(c, e, u, n):
                    pe.wait_ge(g_done, n + 1)
                    for m in range(2):
                        k = 0
                        for d_ in range(KT):
                            for ws_, xs_ in ((0, 0), (0, 1), (1, 0)):
                                last = mm(psum[:, 2 * u + m, :], wt(ws_, e, m * KT + d_),
                                          xTa[:, xs_, d_, bass.ds(c * CH, CH)], start=k == 0, stop=k == 5)
                                k += 1
                    last.then_inc(h_done, 1)

                def down(c, e, u, n):
                    pe.wait_ge(hl, n + 4)
                    pe.wait_ge(y_add, (n + 3) * CT)
                    for t in range(CT):
                        k = 0
                        for hs_, ws_ in ((0, 0), (0, 1), (1, 0)):
                            w2 = wh[:, ws_, bass.ds(e, 1), 2 * KT * P:WE].rearrange("p a n -> p (a n)")
                            last = mm(psum[:, 6 + t // 2, (t % 2) * D:(t % 2 + 1) * D],
                                      hT[:, u, hs_, t * P:(t + 1) * P], w2, start=k == 0, stop=k == 2)
                            k += 1
                    last.then_inc(y_done, 1)

                steps(pe, hidden, down)

            @block.scalar
            def _(act):
                A = nc.scalar.activation

                def head(c, e, u, n):
                    act.wait_ge(h_done, n + 4)
                    act.wait_ge(g_done, n + 1)
                    A(hsb[:, u, :], psum[:, 2 * u, :], ACT.Silu).then_inc(s_done, 1)
                    act.wait_ge(g_done, n + 4)
                    act.wait_ge(y_done, n + 1)
                    A(hT[:, u, 0, :], hp[:, u, :], ACT.Copy).then_inc(hh, 1)

                steps(act, head, lambda c, e, u, n: None)

            @block.vector
            def _(dve):
                V = nc.vector

                def head(c, e, u, n):
                    dve.wait_ge(s_done, n + 4)
                    dve.wait_ge(hl, n + 1)
                    V.tensor_tensor(hp[:, u, :], psum[:, 2 * u + 1, :], hsb[:, u, :], ALU.mult).then_inc(g_done, 1)
                    dve.wait_ge(hh, n + 4)
                    V.tensor_tensor(hT[:, u, 1, :], hp[:, u, :], hT[:, u, 0, :], ALU.subtract).then_inc(hl, 1)

                def add(c, e, u, n):
                    dve.wait_ge(y_done, n + 4)
                    for t in range(CT):
                        dve.wait_ge(y_add, (n + 2) * CT + t + 1)
                        xt = x[:, bass.ds(c * CT + t, 1), :].rearrange("p a d -> p (a d)")
                        V.scalar_tensor_tensor(xt, psum[:, 6 + t // 2, (t % 2) * D:(t % 2 + 1) * D],
                                               ew[:, bass.ds(c * CT + t, 1), bass.ds(e, 1)].rearrange("p a b -> p (a b)"),
                                               xt, ALU.mult, ALU.add).then_inc(y_add, 1)

                steps(dve, head, add)
        f.close()
        stack.close()

    layernorm_scale("n0")
    attention(0)
    layernorm_scale("n1")
    moe0()
    layernorm_scale("n2")
    attention(1)
    layernorm_scale("n3")
    moe1()
    stored = sem("stored")
    with nc.Block() as block:

        @block.sync
        def _(sp):
            for c in range(4):
                sp.dma_start(out_dram[:, c * 8:(c + 1) * 8, :], x[:, c * 8:(c + 1) * 8, :]).then_inc(stored, 16)
            sp.wait_ge(stored, 64)


def _slots(w):
    w = w.reshape(KT, P, G, GH, 1, DH)
    w = np.broadcast_to(w, (KT, P, G, GH, SLOT // DH, DH))
    return np.ascontiguousarray(w.reshape(KT, P, G * P).transpose(1, 0, 2))


def _rows(w):
    return np.ascontiguousarray(w.reshape(-1, P, *w.shape[1:]).swapaxes(0, 1))


def _constants():
    c = {"ident": np.eye(P, dtype=np.float32)}
    r = np.arange(P) % SLOT
    c["hi_rows"] = np.stack([-(r >= DH).astype(np.float32), (r < DH).astype(np.float32)], 1)
    exact = -math.sqrt(DH) * math.log(2.0)
    soft = np.float16(exact)
    rest = np.float16(float(soft) - exact)
    a_, b_ = np.arange(P)[:, None], np.arange(P)[None, :]
    masks = np.zeros((2, P, 4, P), np.float16)
    masks[0, :, 0] = np.where(a_ > b_, soft, rest)
    off = np.float16(-60000.0)
    masks[1, :, 0] = np.where(a_ > b_, off, 0)
    masks[1, :, 1] = np.where(a_ < b_, off, 0)
    masks[1, :, 2] = masks[1, :, 0].T
    masks[1, :, 3] = masks[1, :, 1].T
    k2 = np.zeros((2, GH, SLOT, GH, G, S), np.float16)
    mrows = np.zeros((2, P, TT, G, GH, SLOT), np.float32)
    for j in range(GH):
        k2[:, j, DH, j] = 0.5
        k2[0, j, DH + 1, j, :, P:] = soft
        k2[0, j, DH + 2, j, :, :P] = rest
    mrows[0, :, 0, :, :, DH + 1] = 1.0
    mrows[0, :, 1, :, :, DH + 2] = 1.0
    for L in range(2):
        c[f"L{L}_masks"] = masks[L]
        c[f"L{L}_k2rows"] = k2[L].reshape(P, GH, G, S)
        c[f"L{L}_mrows"] = mrows[L].reshape(P, TT, G, P)
    half = DH // 2
    inv = np.float32(1.0) / np.float32(10000.0) ** (np.arange(half, dtype=np.float32) / np.float32(half))
    ang = np.arange(S, dtype=np.float32)[:, None] * inv[None, :]
    c["iota"] = np.broadcast_to(np.arange(16, dtype=np.float32), (P, 16))
    c["seq_base"] = np.broadcast_to((np.arange(NT) // TT * CAP - 1).astype(np.float32), (P, NT))
    c["tri"] = np.stack([np.triu(np.ones((P, P))), np.ones((P, P))], 1).astype(np.float16)
    c["less"] = np.broadcast_to((np.arange(4)[None, :] < np.arange(4)[:, None]).astype(np.float32), (P, 4, 4))
    row = np.arange(P) % DH
    c["cos"] = np.cos(ang).astype(np.float32).T[row % half]
    c["sin"] = (np.where(row < half, -1, 1)[:, None] * np.sin(ang).T[row % half]).astype(np.float32)
    return {k: np.ascontiguousarray(v) for k, v in c.items()}


def _layout(inputs):
    i = {k: np.asarray(v) for k, v in inputs.items()}
    n = {"x": i["x"], "ctx": i["ctx_1024"]}
    gates = np.stack([i["g_xattn"][0], i["g_ffn"][0], i["g_xattn"][1], i["g_ffn"][1]])
    n["gates"] = np.ascontiguousarray(np.broadcast_to(gates[None, :], (P, 4)))
    for L in range(2):
        w = {k: i[f"L{L}_xattn_{k}"] for k in ("Wq", "Wk", "Wv", "Wo", "bq", "bk", "bv", "bo")}
        if L:
            w |= {k: w[k].T for k in ("Wq", "Wk", "Wv", "Wo")}
        n[f"L{L}_wq"], n[f"L{L}_wk"] = _slots(w["Wq"]), _slots(w["Wk"])
        n[f"L{L}_wv"], n[f"L{L}_wo"] = _rows(w["Wv"]), _rows(w["Wo"])
        for k in ("bq", "bk"):
            dup = np.broadcast_to(w[k].reshape(G, GH, 1, DH), (G, GH, SLOT // DH, DH))
            n[f"L{L}_{k}"] = np.ascontiguousarray(dup.reshape(G, P).T)
        n[f"L{L}_bv"] = np.ascontiguousarray(w["bv"].reshape(KT, P).T)
        n[f"L{L}_bo"] = np.ascontiguousarray(w["bo"].reshape(1, D))
    n["L0_router"] = _rows(i["L0_ffn_gate_w"].T)
    for k in ("w1", "w3", "w2"):
        w = i[f"L0_ffn_{k}"]
        n[f"L0_{k}"] = np.ascontiguousarray(w.reshape(w.shape[0], -1, P, w.shape[2]).transpose(0, 2, 1, 3)
                                            .reshape(w.shape[0], P, -1))
    n["L1_router"] = _rows(i["L1_ffn_router_weight"].T)
    n["L1_e_bias"] = np.ascontiguousarray(np.broadcast_to(i["L1_ffn_e_bias"][None, :], (P, 16)))
    up = [np.concatenate([i[f"L1_ffn_{k}_w"], i[f"L1_ffn_sh_{k}_w"].reshape(2, P, D)]) for k in ("gate", "up")]
    down = np.concatenate([i["L1_ffn_down_w"], i["L1_ffn_sh_down_w"].reshape(D, 2, P).transpose(1, 0, 2)])
    up = [w.reshape(-1, P, KT, P).transpose(3, 0, 2, 1).reshape(P, -1, KT * P) for w in up]
    n["L1_experts"] = np.ascontiguousarray(np.concatenate(up + [down.transpose(2, 0, 1)], axis=2))
    return n | _constants()


def kernel(**inputs):
    import concourse.bacc as _bacc
    from concourse.bass_utils import run_bass_kernel_spmd as _run

    arrays = _layout(inputs)
    nc = _bacc.Bacc("TRN2", target_bir_lowering=False, num_devices=1)
    args = {k: nc.dram_tensor(f"in_{k}", v.shape, mybir.dt.from_np(v.dtype), kind="ExternalInput").ap()
            for k, v in arrays.items()}
    out = nc.dram_tensor("out_x", (B, S, D), F32, kind="ExternalOutput").ap()
    flamingo_kernel(nc, args, out)
    r = _run(nc, [{f"in_{k}": v for k, v in arrays.items()}], core_ids=[0])
    return r.results[0]["out_x"]
```
